# Optimizing a Trainium2 kernel written in Bass

```python
import numpy as np
import jax
import jax.numpy as jnp

def _softmax(x, axis=-1):
    return jax.nn.softmax(x, axis=axis)

def _gelu(x):
    return jax.nn.gelu(x, approximate=True)

def _silu(x):
    return jax.nn.silu(x)

def _sigmoid(x):
    return jax.nn.sigmoid(x)

def _layernorm(x, axis=-1, eps=1e-05):
    m = jnp.mean(x, axis=axis, keepdims=True)
    v = jnp.var(x, axis=axis, keepdims=True)
    return (x - m) / jnp.sqrt(v + eps)

def _scatter_add(tgt, idx, src, axis=0):
    return tgt.at[idx].add(src)

def _segment_sum(src, seg, n):
    return jax.ops.segment_sum(src, seg, n)
kernel_name = 'mk_gnn_preln_d4_gnn_r32_425d8b'

def setup_inputs(seed: int=0):
    np.random.seed(seed)
    _w = jnp.asarray

    def _rec_inputs():
        import jax
        import jax.numpy as jnp
        _gk = jax.random.key(seed)
        x = -0.000202 + 1 * jax.random.normal(jax.random.fold_in(_gk, 1), (50000, 64), jnp.float32)
        src = jax.random.randint(jax.random.fold_in(_gk, 2), (50000,), 0, 50000, jnp.int32)
        dst = jax.random.randint(jax.random.fold_in(_gk, 3), (50000,), 0, 50000, jnp.int32)
        _o = jnp.argsort(dst, stable=True)
        src = src[_o]
        dst = dst[_o]
        edge_attr_8 = -0.000153872 + 1.00011 * jax.random.normal(jax.random.fold_in(_gk, 12), (50000, 8), jnp.float32)
        return (x, src, dst, edge_attr_8)
    x, src, dst, edge_attr_8 = _rec_inputs()

    def _L0_gnn_setup():
        import jax, jax.numpy as jnp
        import numpy as np
        N_NODES = 3125
        key = jax.random.key(seed)
        k1, k2 = jax.random.split(key)
        x = jax.random.normal(k1, (N_NODES, 64), dtype=jnp.float32)
        adj_t = jax.random.randint(k2, (2, 100000), 0, N_NODES, dtype=jnp.int32)
        return {'x': x, 'adj_t': adj_t, 'num_layers': 3}
    _L0_gnn_all = _L0_gnn_setup()
    _L0_gnn_in = {k: v for k, v in _L0_gnn_all.items() if k in ()}
    del _L0_gnn_all

    def _L1_gnn_setup():
        import jax, jax.numpy as jnp
        import numpy as np
        N_NODES = 625
        N_EDGES = 31250
        C = 64
        H = 64
        N_BASIS = 8
        key = jax.random.key(seed)
        ks = jax.random.split(key, 10)

        def glorot(k, shape):
            fan_in, fan_out = (shape[0], shape[1])
            lim = np.sqrt(6.0 / (fan_in + fan_out)).astype(np.float32)
            return jax.random.uniform(k, shape, jnp.float32, -lim, lim)
        return {'p': jax.random.normal(ks[0], (N_NODES, C), jnp.float32), 'idx_i': jax.random.randint(ks[1], (N_EDGES,), 0, N_NODES), 'idx_j': jax.random.randint(ks[2], (N_EDGES,), 0, N_NODES), 'basis': jax.random.normal(ks[3], (N_EDGES, N_BASIS), jnp.float32), 'pp_W': glorot(ks[4], (C, C)), 'pp_b': jnp.zeros((C,), jnp.float32), 'pi_W1': glorot(ks[5], (2 * C, H)), 'pi_b1': jnp.zeros((H,), jnp.float32), 'pi_W2': glorot(ks[6], (H, H * N_BASIS)), 'ii_W': glorot(ks[7], (H, C)), 'ii_b': jnp.zeros((C,), jnp.float32)}
    _L1_gnn_all = _L1_gnn_setup()
    _L1_gnn_in = {k: v for k, v in _L1_gnn_all.items() if k in ('pp_W', 'pp_b', 'pi_W1', 'pi_b1', 'pi_W2', 'ii_W', 'ii_b')}
    del _L1_gnn_all

    def _L2_gnn_setup():
        import jax, jax.numpy as jnp
        import numpy as np
        N = 3125
        E = 50000
        D = 64
        key = jax.random.key(seed)
        ks = jax.random.split(key, 6)
        x = jax.random.normal(ks[0], (N, D), dtype=jnp.float32)
        edge_index = jax.random.randint(ks[1], (2, E), 0, N, dtype=jnp.int64)
        s = 1.0 / np.sqrt(D)
        W0 = jax.random.uniform(ks[2], (D, D), jnp.float32, -s, s)
        W1 = jax.random.uniform(ks[3], (D, D), jnp.float32, -s, s)
        Wm = jax.random.uniform(ks[4], (D, D), jnp.float32, -s, s)
        eps0 = jnp.zeros((), jnp.float32)
        eps1 = jnp.zeros((), jnp.float32)
        return {'x': x, 'edge_index': edge_index, 'W0': W0, 'eps0': eps0, 'W1': W1, 'eps1': eps1, 'Wm': Wm}
    _L2_gnn_all = _L2_gnn_setup()
    _L2_gnn_in = {k: v for k, v in _L2_gnn_all.items() if k in ('W0', 'eps0', 'W1', 'eps1', 'Wm')}
    del _L2_gnn_all

    def _L3_gnn_setup():
        import jax, jax.numpy as jnp
        import numpy as np
        N_NODES = 3125
        N_EDGES = 37500
        D_IN = 64
        D_HID = 64
        D_OUT = 64

        def _sage_conv(x, row, col, W, b):
            n = x.shape[0]
            neighbor_sum = jax.ops.segment_sum(x[col], row, num_segments=n)
            deg = jax.ops.segment_sum(jnp.ones(row.shape[0], x.dtype), row, num_segments=n)
            deg = jnp.maximum(deg, 1.0)
            neighbor_agg = neighbor_sum / deg[:, None]
            out = jnp.concatenate([x, neighbor_agg], axis=-1)
            return out @ W + b
        key = jax.random.key(seed)
        k1, k2, k3, k4, k5, k6 = jax.random.split(key, 6)
        x = jax.random.normal(k1, (N_NODES, D_IN), dtype=jnp.float32)
        edge_index = jax.random.randint(k2, (2, N_EDGES), 0, N_NODES, dtype=jnp.int32)
        s1 = 1.0 / np.sqrt(2 * D_IN)
        s2 = 1.0 / np.sqrt(2 * D_HID)
        W1 = jax.random.uniform(k3, (2 * D_IN, D_HID), jnp.float32, -s1, s1)
        b1 = jax.random.uniform(k4, (D_HID,), jnp.float32, -s1, s1)
        W2 = jax.random.uniform(k5, (2 * D_HID, D_OUT), jnp.float32, -s2, s2)
        b2 = jax.random.uniform(k6, (D_OUT,), jnp.float32, -s2, s2)
        return {'x': x, 'edge_index': edge_index, 'W1': W1, 'b1': b1, 'W2': W2, 'b2': b2}
    _L3_gnn_all = _L3_gnn_setup()
    _L3_gnn_in = {k: v for k, v in _L3_gnn_all.items() if k in ('W1', 'b1', 'W2', 'b2')}
    del _L3_gnn_all
    return {'x': x, 'src': src, 'dst': dst, 'edge_attr_8': edge_attr_8, 'L1_gnn_pp_W': _L1_gnn_in['pp_W'], 'L1_gnn_pp_b': _L1_gnn_in['pp_b'], 'L1_gnn_pi_W1': _L1_gnn_in['pi_W1'], 'L1_gnn_pi_b1': _L1_gnn_in['pi_b1'], 'L1_gnn_pi_W2': _L1_gnn_in['pi_W2'], 'L1_gnn_ii_W': _L1_gnn_in['ii_W'], 'L1_gnn_ii_b': _L1_gnn_in['ii_b'], 'L2_gnn_W0': _L2_gnn_in['W0'], 'L2_gnn_eps0': _L2_gnn_in['eps0'], 'L2_gnn_W1': _L2_gnn_in['W1'], 'L2_gnn_eps1': _L2_gnn_in['eps1'], 'L2_gnn_Wm': _L2_gnn_in['Wm'], 'L3_gnn_W1': _L3_gnn_in['W1'], 'L3_gnn_b1': _L3_gnn_in['b1'], 'L3_gnn_W2': _L3_gnn_in['W2'], 'L3_gnn_b2': _L3_gnn_in['b2']}

def reference(x, src, dst, edge_attr_8, L1_gnn_pp_W, L1_gnn_pp_b, L1_gnn_pi_W1, L1_gnn_pi_b1, L1_gnn_pi_W2, L1_gnn_ii_W, L1_gnn_ii_b, L2_gnn_W0, L2_gnn_eps0, L2_gnn_W1, L2_gnn_eps1, L2_gnn_Wm, L3_gnn_W1, L3_gnn_b1, L3_gnn_W2, L3_gnn_b2):
    import jax
    import jax.numpy as jnp

    def _L0_gnn_ref(x, adj_t, num_layers):
        import jax, jax.numpy as jnp
        import numpy as np
        N_NODES = 3125
        n = x.shape[0]
        ei = jnp.concatenate([adj_t, adj_t[::-1, :]], axis=1)
        row, col = (ei[0], ei[1])
        deg = jax.ops.segment_sum(jnp.ones_like(col, dtype=x.dtype), col, num_segments=n)
        deg_inv_sqrt = jnp.where(deg > 0, jax.lax.rsqrt(deg), 0.0)
        w = deg_inv_sqrt[row] * deg_inv_sqrt[col]
        out_ls = []
        cur = x
        for _ in range(num_layers):
            out_ls.append(cur)
            msg = w[:, None] * cur[row]
            cur = jax.ops.segment_sum(msg, col, num_segments=n)
        return jnp.mean(jnp.stack(out_ls), axis=0)

    def _L1_gnn_ref(p, idx_i, idx_j, basis, pp_W, pp_b, pi_W1, pi_b1, pi_W2, ii_W, ii_b):
        import jax, jax.numpy as jnp
        import numpy as np
        N_NODES = 625
        N_EDGES = 31250
        C = 64
        H = 64
        N_BASIS = 8
        p1 = jnp.tanh(p @ pp_W + pp_b)
        pair = jnp.concatenate([p1[idx_i], p1[idx_j]], axis=-1)
        h = pair @ pi_W1 + pi_b1
        h = (h @ pi_W2).reshape(-1, H, N_BASIS)
        i1 = jnp.einsum('ecb,eb->ec', h, basis)
        i2 = jnp.tanh(i1 @ ii_W + ii_b)
        return p.at[idx_i].add(i2)

    def _L2_gnn_ref(x, edge_index, W0, eps0, W1, eps1, Wm):
        import jax, jax.numpy as jnp
        import numpy as np
        N = 3125
        E = 50000
        D = 64
        n = x.shape[0]
        src, dst = (edge_index[0], edge_index[1])

        def gin_conv(h, W, eps):
            agg = jax.ops.segment_sum(h[src], dst, num_segments=n)
            return (agg + (1.0 + eps) * h) @ W.T
        h1 = jax.nn.relu(gin_conv(x, W0, eps0))
        h2 = jax.nn.relu(gin_conv(h1, W1, eps1))
        return (h1 @ Wm.T + h2) / 2.0

    def _L3_gnn_ref(x, edge_index, W1, b1, W2, b2):
        import jax, jax.numpy as jnp
        import numpy as np
        N_NODES = 3125
        N_EDGES = 37500
        D_IN = 64
        D_HID = 64
        D_OUT = 64

        def _sage_conv(x, row, col, W, b):
            n = x.shape[0]
            neighbor_sum = jax.ops.segment_sum(x[col], row, num_segments=n)
            deg = jax.ops.segment_sum(jnp.ones(row.shape[0], x.dtype), row, num_segments=n)
            deg = jnp.maximum(deg, 1.0)
            neighbor_agg = neighbor_sum / deg[:, None]
            out = jnp.concatenate([x, neighbor_agg], axis=-1)
            return out @ W + b
        row, col = (edge_index[0], edge_index[1])
        h = jax.nn.relu(_sage_conv(x, row, col, W1, b1))
        return _sage_conv(h, row, col, W2, b2)
    edge_index = jnp.stack([src, dst])
    h = jnp.maximum(_layernorm(x, axis=-1), 0.0)
    x = x + _L0_gnn_ref(h, edge_index, 3)
    h = jnp.maximum(_layernorm(x, axis=-1), 0.0)
    x = x + _L1_gnn_ref(h, src, dst, edge_attr_8, L1_gnn_pp_W, L1_gnn_pp_b, L1_gnn_pi_W1, L1_gnn_pi_b1, L1_gnn_pi_W2, L1_gnn_ii_W, L1_gnn_ii_b)
    h = jnp.maximum(_layernorm(x, axis=-1), 0.0)
    x = x + _L2_gnn_ref(h, edge_index, L2_gnn_W0, L2_gnn_eps0, L2_gnn_W1, L2_gnn_eps1, L2_gnn_Wm)
    h = jnp.maximum(_layernorm(x, axis=-1), 0.0)
    x = x + _L3_gnn_ref(h, edge_index, L3_gnn_W1, L3_gnn_b1, L3_gnn_W2, L3_gnn_b2)
    return x

_drawn_inputs = setup_inputs


def setup_inputs(seed=0):
    import zlib

    import numpy as np

    out = dict(_drawn_inputs(seed))
    spreads = {'L1_gnn_pp_b': (0.0, 0.1), 'L1_gnn_pi_b1': (0.0, 0.1), 'L1_gnn_ii_b': (0.0, 0.1)}
    factors = {'L3_gnn_b1': 5.568}
    for name, (base, spread) in spreads.items():
        noise = np.random.default_rng([zlib.crc32(name.encode()), seed]).standard_normal(out[name].shape)
        drawn = base * np.exp(spread * noise) if base else spread * noise
        out[name] = jnp.asarray(drawn.astype(out[name].dtype))
    for name, factor in factors.items():
        out[name] = (out[name] * factor).astype(out[name].dtype)
    return out
```

```python
import concourse.bass as bass
from concourse import mybir
from contextlib import ExitStack

P = 128
NODES = 50000
EDGES = 50000
D = 64
COLS = 392
NPAD = P * COLS
BCOLS = 4
BLOCKS = COLS // BCOLS
BW = BCOLS * P
ETILES = 392
EPAD = P * ETILES
TILES = ETILES + BLOCKS
SLOTS = P * TILES
BASIS = 8
FS = 3 + BASIS
FD = 2
U = 14
HU = U // 2
CC = 14
CHUNKS = COLS // CC
CE = CC * D
PAIRS = CC // 2
G4 = 4
GROUPS = ETILES // G4
EPS = 1e-5

CONST_COLS = 128 + 2 * 98
W_NAMES = ["pp", "w1a", "w1b", "g0", "gm", "g1", "s1x", "s1a", "s2x", "s2a"]


def build_program(nc, x_in, src_in, dst_in, attr_in, consts32, consts16, weights, w2t, iiw,
                  vectors, out):
    f32, i32 = mybir.dt.float32, mybir.dt.int32
    f16, bf16 = mybir.dt.float16, mybir.dt.bfloat16
    ALU, ACT, AX = mybir.AluOpType, mybir.ActivationFunctionType, mybir.AxisListType
    ds = bass.ds

    def dram(name, shape):
        return nc.dram_tensor(name, shape, f32, kind="Internal").ap()

    tab_s, tab_d = dram("tab_s", [SLOTS, FS]), dram("tab_d", [SLOTS, FD])
    t_g0, t_g1, t_a, t_c, t_h2, t_h1, t_h3, t_h4 = (
        dram(n, [NPAD, D]) for n in ("t_g0", "t_g1", "t_a", "t_c", "t_h2", "t_h1", "t_h3", "t_h4"))
    r_0, r_1, r_2, r_3, r_4, r_5 = (dram(n, [NPAD, D]) for n in ("r_0", "r_1", "r_2", "r_3", "r_4", "r_5"))

    def per_partition(t):
        return t.rearrange("(p c) d -> p (c d)", p=P)

    with ExitStack() as ctx:
        def sb(name, shape, dt=f32):
            return ctx.enter_context(nc.sbuf_tensor(name, shape, dt))

        def sem(name):
            return ctx.enter_context(nc.semaphore(name))

        acc = sb("acc", [P, COLS * D])
        work = sb("work", [P, 14 * CE])
        iota16 = sb("iota16", [P, 512], f16)
        mats16 = sb("mats16", [P, 2 * P], f16)
        c32 = sb("c32", [P, CONST_COLS])
        w_sb = sb("w_sb", [P, len(W_NAMES) * P])
        small64 = sb("small64", [D, D + 512])
        vmix = sb("vmix", [D, BASIS * D])
        vecs = sb("vecs", [P, 4 * D + 4])
        key_s, key_d = sb("key_s", [P, TILES]), sb("key_d", [P, TILES])
        idx_s, idx_d = sb("idx_s", [P, TILES], i32), sb("idx_d", [P, TILES], i32)
        own_s = sb("own_s", [P, TILES], i32)
        basis = sb("basis", [P, TILES, BASIS])
        block_at = sb("block_at", [1, 2, TILES], i32)
        dinv, rdeg = sb("dinv", [P, COLS]), sb("rdeg", [P, COLS])
        zero = sb("zero", [P, 1])
        st = sb("st", [P, 16, CC])

        PS = ctx.enter_context(nc.psum_tensor("PS", [P, 4096], f32))
        ident = c32[:, 0:P]
        pre_inc, pre_exc = c32[0:BLOCKS, P:P + 98], c32[0:BLOCKS, P + 98:P + 196]
        lower16, ones16 = mats16[:, 0:P], mats16[:, P:2 * P]
        W = {n: w_sb[:, i * P:(i + 1) * P] for i, n in enumerate(W_NAMES)}
        b_pi1, b_ii, b_s1, b_s2 = (vecs[:, i * D:(i + 1) * D] for i in range(4))
        b_pp, ep0, ep1 = (vecs[:, 4 * D + i:4 * D + i + 1] for i in range(3))

        phase_end = sem("phase_end")
        const_in, edges_in, filled = sem("const_in"), sem("edges_in"), sem("filled")
        dve_step = sem("dve_step")
        deg_oh, deg_mm = sem("deg_oh"), sem("deg_mm")
        pe_prep, dve_prep, act_prep = sem("pe_prep"), sem("dve_prep"), sem("act_prep")
        rk_oh = [sem(f"rk_oh{s}") for s in range(2)]
        rk_mm = [sem(f"rk_mm{s}") for s in range(2)]
        rk_row = [sem(f"rk_row{s}") for s in range(2)]
        rk_pay = [sem(f"rk_pay{s}") for s in range(2)]
        rk_cum = [sem(f"rk_cum{s}") for s in range(2)]
        rk_dve = sem("rk_dve")
        sent = [[sem(f"sent{s}{u}") for u in range(G4)] for s in range(2)]
        issuing = sem("issuing")
        tab_in = sem("tab_in")
        staged = sem("staged")
        got = [sem(f"got{u}") for u in range(U)]
        got2 = [sem(f"got2_{u}") for u in range(U)]
        onehot_ready, sum_ready, added = sem("onehot_ready"), sem("sum_ready"), sem("added")
        h_ready, ht_mm, ht_ready, z_mm, z_used, pre_ready, msg_ready = (
            sem(n) for n in ("h_ready", "ht_mm", "ht_ready", "z_mm", "z_used", "pre_ready", "msg_ready"))
        l1_dve = sem("l1_dve")
        loaded = [sem(f"loaded{h}") for h in range(2)]
        stored = [sem(f"stored{h}") for h in range(2)]
        n_dve = sem("n_dve")
        in_used, out_ready, acc_used, cleared = (sem(n) for n in ("in_used", "out_ready", "acc_used", "cleared"))
        centered, squared, var_ready, root_ready = (
            sem(n) for n in ("centered", "squared", "var_ready", "root_ready"))
        mm_in = sem("mm_in")
        turned, turned_sb, prod, prod_act = (sem(n) for n in ("turned", "turned_sb", "prod", "prod_act"))
        prod2, prod3, prod_out = sem("prod2"), sem("prod3"), sem("prod_out")

        block = ctx.enter_context(nc.Block())
        phase_no = {}

        def end_phase(e, name):
            phase_no[name] = phase_no.get(name, 0) + 1
            e.drain().then_inc(phase_end, 1)
            e.wait_ge(phase_end, 5 * phase_no[name])

        def wait_past(e, s, v):
            if isinstance(v, int) and v <= 0:
                return
            e.wait_ge(s, v)

        o = 0

        def scratch(n):
            nonlocal o
            o += n
            return acc[:, o - n:o]

        E2 = 2 * ETILES
        ed_i = scratch(E2).bitcast(i32)
        ti = scratch(E2).bitcast(i32)
        nf, q_p, r_m, q_b, rem_b, t1 = (scratch(E2) for _ in range(6))
        attr = scratch(ETILES * BASIS)
        pay_s, pay_d = scratch(ETILES * FS), scratch(ETILES * FD)
        deg = scratch(2 * COLS)
        degb = scratch(2 * BLOCKS)
        fill = acc[:, o:o + SLOTS * FS // P]
        tabs_sb = acc[:, o:o + TILES * FS]
        tabd_sb = acc[:, o + TILES * FS:o + TILES * (FS + FD)]
        wo = 0

        def wscratch(n, dt=f32):
            nonlocal wo
            words = n // 2 if dt in (f16, bf16) else n
            wo += words
            a = work[:, wo - words:wo]
            return a if dt == f32 else a.bitcast(dt)

        oh_p = [[wscratch(P, bf16) for _ in range(2)] for _ in range(2)]
        oh_m = [[wscratch(COLS, bf16) for _ in range(2)] for _ in range(2)]
        oh_b = [wscratch(G4 * BLOCKS, f16) for _ in range(2)]
        cum = [wscratch(BLOCKS, f16) for _ in range(2)]
        base16 = wscratch(2 * BLOCKS, f16)
        row128 = wscratch(P, f16)
        pick = [wscratch(G4 * BLOCKS) for _ in range(2)]
        csum = [wscratch(BLOCKS) for _ in range(2)]
        posf = [wscratch(G4) for _ in range(2)]
        pos_i, pos_lo, pos_hi, row_i = ([wscratch(G4, i32) for _ in range(2)] for _ in range(4))
        pring = [wscratch(G4 * FS), wscratch(G4 * FD)]
        tl = wscratch(2)
        tl_i = wscratch(2, i32)
        tl_w = wscratch(2 * P)
        end_t = wscratch(2)
        cmp16 = wscratch(2 * TILES, f16)
        ones32 = wscratch(1)
        pays, pay_n, tabs = [pay_s, pay_d], [FS, FD], [tab_s, tab_d]

        def prep_sync(e):
            for dst_, src_ in ((iota16[:, :], consts16[:, 0:512]), (mats16[:, :], consts16[:, 512:768]),
                               (c32[:, :], consts32), (w_sb[:, :], weights), (small64[:, 0:D], iiw),
                               (small64[:, D:], w2t), (vecs[:, :], vectors)):
                e.dma_start(dst_, src_).then_inc(const_in, 16)
            e.dma_start(ed_i[:, 0:ETILES], src_in).then_inc(edges_in, 16)
            e.dma_start(ed_i[:, ETILES:], dst_in).then_inc(edges_in, 16)
            e.dma_start(attr, attr_in).then_inc(edges_in, 16)
            e.wait_ge(dve_prep, 1)
            e.dma_start(tab_s.rearrange("(p a) f -> p (a f)", p=P), fill).then_inc(filled, 16)
            e.dma_start(tab_d.rearrange("(p a) f -> p (a f)", p=P), fill[:, 0:SLOTS * FD // P]).then_inc(filled, 16)

        def prep_vector(e):
            steps = [0]

            def step(ins):
                steps[0] += 1
                ins.then_inc(dve_step, 1)
                e.wait_ge(dve_step, steps[0])

            v = nc.vector
            v.memset(zero[:, :], 0.0)
            v.memset(fill, -1.0).then_inc(dve_prep, 1)
            v.memset(ones32, 1.0)
            v.memset(row128[0:1, :], 128.0)
            for s in range(2):
                v.memset(cum[s], 0.0)
            e.wait_ge(const_in, 16 * 7)
            step(v.tensor_scalar(vecs[:, 4 * D + 1:4 * D + 3], vecs[:, 4 * D + 1:4 * D + 3], 1.0, None, ALU.add))
            e.wait_ge(edges_in, 48)
            step(v.tensor_copy(nf, ed_i))

            def divmod_(a, n, q, r):
                step(v.tensor_scalar(t1, a, 1.0 / n, None, ALU.mult))
                step(v.tensor_copy(ti, t1))
                step(v.tensor_copy(q, ti))
                step(v.scalar_tensor_tensor(r, q, -float(n), a, ALU.mult, ALU.add))
                for op, bound, sign in ((ALU.is_lt, 0.0, -1.0), (ALU.is_ge, float(n), 1.0)):
                    step(v.tensor_scalar(t1, r, bound, sign, op, ALU.mult))
                    step(v.tensor_tensor(q, q, t1, ALU.add))
                    step(v.scalar_tensor_tensor(r, t1, -float(n), r, ALU.mult, ALU.add))

            divmod_(nf, COLS, q_p, r_m)
            divmod_(r_m, BCOLS, q_b, rem_b)
            step(v.scalar_tensor_tensor(t1, rem_b, float(P), q_p, ALU.mult, ALU.add))
            ps3 = pay_s.rearrange("p (t f) -> p t f", f=FS)
            pd3 = pay_d.rearrange("p (t f) -> p t f", f=FD)
            v.tensor_copy(ps3[:, :, 0], nf[:, ETILES:])
            v.tensor_copy(ps3[:, :, 1], t1[:, 0:ETILES])
            v.tensor_copy(ps3[:, :, 2], nf[:, 0:ETILES])
            v.tensor_copy(ps3[:, :, 3:], attr.rearrange("p (t f) -> p t f", f=BASIS))
            v.tensor_copy(pd3[:, :, 0], nf[:, 0:ETILES])
            step(v.tensor_copy(pd3[:, :, 1], t1[:, ETILES:]))

            def degree_tile(j, h):
                t = 2 * j + h
                for s in range(2):
                    wait_past(e, deg_mm, 2 * (t - 2) + s + 1)
                    v.tensor_scalar(oh_p[h][s], iota16[:, 0:P], q_p[:, ds(t + s * ETILES, 1)], None, ALU.is_equal)
                    v.tensor_scalar(oh_m[h][s], iota16[:, 0:COLS], r_m[:, ds(t + s * ETILES, 1)], None,
                                    ALU.is_equal).then_inc(deg_oh, 1)

            degree_tile(0, 0)
            degree_tile(0, 1)
            with e.Fori(1, ETILES // 2) as j:
                degree_tile(j, 0)
                degree_tile(j, 1)
            e.wait_ge(deg_mm, 2 * ETILES)
            for s in range(2):
                step(v.tensor_copy(deg[:, s * COLS:(s + 1) * COLS], PS[:, s * 512:s * 512 + COLS]))
            v.tensor_reduce(degb, deg.rearrange("p (b c) -> p b c", c=BCOLS), AX.X, ALU.add).then_inc(dve_prep, 1)
            e.wait_ge(pe_prep, 1)
            step(v.tensor_scalar(tl_i[0:BLOCKS, :], PS[0:BLOCKS, 1024:1026], float(P - 1), None, ALU.add))
            step(v.tensor_scalar(tl_i[0:BLOCKS, :], tl_i[0:BLOCKS, :], 7, None, ALU.logical_shift_right))
            step(v.tensor_copy(tl[0:BLOCKS, :], tl_i[0:BLOCKS, :]))
            v.tensor_copy(tl_w[0:BLOCKS, :].rearrange("b (s p) -> b s p", s=2),
                          tl[0:BLOCKS, :].unsqueeze(2).to_broadcast([BLOCKS, 2, P])).then_inc(dve_prep, 1)
            e.wait_ge(pe_prep, 2)
            step(v.tensor_copy(end_t[0:BLOCKS, :], PS[0:BLOCKS, 1536:1538]))
            v.tensor_copy(base16[0:1, :], PS[0:1, 2048:2048 + 2 * BLOCKS])
            for s in range(2):
                ins = v.tensor_scalar(cmp16[0:BLOCKS, s * TILES:(s + 1) * TILES], iota16[0:BLOCKS, 0:TILES],
                                      end_t[0:BLOCKS, s:s + 1], None, ALU.is_ge)
            ins.then_inc(dve_prep, 1)
            e.wait_ge(pe_prep, 3)
            for s in range(2):
                ins = v.tensor_scalar(block_at[0:1, s, :], PS[0:1, 2560 + 512 * s:2560 + 512 * s + TILES],
                                      float(BLOCKS - 1), float(BCOLS * D), ALU.min, ALU.mult)
            step(ins)
            step(v.tensor_tensor(t1[:, 0:COLS], deg[:, 0:COLS], deg[:, COLS:], ALU.add))
            v.tensor_scalar(t1[:, COLS:], t1[:, 0:COLS], 1.0, None, ALU.max).then_inc(dve_prep, 1)
            e.wait_ge(act_prep, 1)
            step(v.reciprocal(dinv[:, :], nf[:, 0:COLS]))
            step(v.tensor_scalar(t1[:, 0:COLS], t1[:, 0:COLS], 1.0, None, ALU.is_ge))
            step(v.tensor_tensor(dinv[:, :], dinv[:, :], t1[:, 0:COLS], ALU.mult))
            step(v.tensor_scalar(rdeg[:, :], deg[:, 0:COLS], 1.0, None, ALU.max))
            step(v.reciprocal(rdeg[:, :], rdeg[:, :]))
            e.wait_ge(pe_prep, 4)
            step(v.tensor_copy(vmix[:, :], PS[0:D, 3584:4096]))

            n = [0]

            def link(ins, before):
                n[0] += 1
                ins.then_inc(rk_dve, 1)
                e.wait_ge(rk_dve, before + n[0])

            def group(g, before):
                n[0] = 0
                for s in range(2):
                    oh3 = oh_b[s].rearrange("p (u b) -> p u b", u=G4)
                    v.tensor_tensor(oh3, iota16[:, 0:BLOCKS].unsqueeze(1).to_broadcast([P, G4, BLOCKS]),
                                    q_b[:, ds(g * G4 + s * ETILES, G4)].unsqueeze(2).to_broadcast([P, G4, BLOCKS]),
                                    ALU.is_equal).then_inc(rk_oh[s], 1)
                for s in range(2):
                    oh3 = oh_b[s].rearrange("p (u b) -> p u b", u=G4)
                    wait_past(e, rk_oh[s], g + 1)
                    link(v.tensor_reduce(csum[s], oh3.rearrange("p u b -> p b u"), AX.X, ALU.add), before)
                    e.wait_ge(rk_mm[s], g + 1)
                    link(v.tensor_tensor(pick[s], PS[:, 512 * s:512 * s + G4 * BLOCKS], oh_b[s], ALU.mult), before)
                    v.tensor_tensor(cum[s], cum[s], csum[s], ALU.add).then_inc(rk_cum[s], 1)
                    link(v.tensor_reduce(posf[s], pick[s].rearrange("p (u b) -> p u b", u=G4), AX.X, ALU.add), before)
                    link(v.tensor_copy(pos_i[s], posf[s]), before)
                    link(v.tensor_scalar(pos_lo[s], pos_i[s], P - 1, None, ALU.bitwise_and), before)
                    link(v.tensor_scalar(pos_hi[s], pos_i[s], 7, None, ALU.logical_shift_right), before)
                    for u in range(G4):
                        wait_past(e, sent[s][u], 16 * g)
                    v.scalar_tensor_tensor(row_i[s], pos_lo[s], float(TILES), pos_hi[s], ALU.mult,
                                           ALU.add).then_inc(rk_row[s], 1)
                return n[0]

            k = group(0, 0)
            with e.Fori(1, GROUPS) as g:
                group(g, g * k)
            e.wait_ge(tab_in, 32)
            s3 = tabs_sb.rearrange("p (t f) -> p t f", f=FS)
            d3 = tabd_sb.rearrange("p (t f) -> p t f", f=FD)
            v.tensor_scalar(idx_s[:, :], s3[:, :, 0], 0.0, None, ALU.max)
            v.tensor_copy(key_s[:, :], s3[:, :, 1])
            v.tensor_scalar(own_s[:, :], s3[:, :, 2], 0.0, None, ALU.max)
            v.tensor_copy(basis[:, :, :], s3[:, :, 3:])
            v.tensor_scalar(idx_d[:, :], d3[:, :, 0], 0.0, None, ALU.max)
            step(v.tensor_copy(key_d[:, :], d3[:, :, 1]))
            step(v.memset(acc[:, :], 0.0))

        def prep_scalar(e):
            e.wait_ge(dve_prep, 5)
            e.activation(nf[:, 0:COLS], t1[:, COLS:], ACT.Sqrt).then_inc(act_prep, 1)

            def group(g):
                for s in range(2):
                    for u in range(G4):
                        wait_past(e, sent[s][u], 16 * g)
                    n = G4 * pay_n[s]
                    e.copy(pring[s], pays[s][:, ds(g * n, n)]).then_inc(rk_pay[s], 1)

            group(0)
            with e.Fori(1, GROUPS) as g:
                group(g)

        def prep_tensor(e):
            mm = nc.tensor.matmul

            def degree_tile(t, h, start, stop):
                for s in range(2):
                    e.wait_ge(deg_oh, 2 * t + s + 1)
                    mm(PS[:, s * 512:s * 512 + COLS], oh_p[h][s], oh_m[h][s], start=start, stop=stop,
                       skip_group_check=True).then_inc(deg_mm, 1)

            degree_tile(0, 0, True, False)
            degree_tile(1, 1, False, False)
            with e.Fori(1, ETILES // 2 - 1) as j:
                degree_tile(2 * j, 0, False, False)
                degree_tile(2 * j + 1, 1, False, False)
            degree_tile(ETILES - 2, 0, False, False)
            degree_tile(ETILES - 1, 1, False, True)
            e.wait_ge(dve_prep, 2)
            for s in range(2):
                ins = mm(PS[0:BLOCKS, 1024 + s:1025 + s], degb[:, s * BLOCKS:(s + 1) * BLOCKS], ones32,
                         start=True, stop=True)
            ins.then_inc(pe_prep, 1)
            e.wait_ge(dve_prep, 3)
            for s in range(2):
                mm(PS[0:BLOCKS, 1536 + s:1537 + s], pre_inc, tl[0:BLOCKS, s:s + 1], start=True, stop=True)
                ins = mm(PS[:, 2048 + s * BLOCKS:2048 + (s + 1) * BLOCKS], tl_w[0:BLOCKS, s * P:(s + 1) * P],
                         pre_exc, start=True, stop=True)
            ins.then_inc(pe_prep, 1)
            e.wait_ge(dve_prep, 4)
            for s in range(2):
                ins = mm(PS[:, 2560 + 512 * s:2560 + 512 * s + TILES], ones16[0:BLOCKS, :],
                         cmp16[0:BLOCKS, s * TILES:(s + 1) * TILES], start=True, stop=True)
            ins.then_inc(pe_prep, 1)
            for b in range(BASIS):
                ins = mm(PS[0:D, 3584 + b * D:3584 + (b + 1) * D], small64[:, D + b * D:D + (b + 1) * D],
                         small64[:, 0:D], start=True, stop=True)
            ins.then_inc(pe_prep, 1)

            def group(g):
                for s in range(2):
                    ps = PS[:, 512 * s:512 * s + G4 * BLOCKS]
                    ps3 = ps.rearrange("p (u b) -> p u b", u=G4)
                    e.wait_ge(rk_oh[s], g + 1)
                    wait_past(e, rk_cum[s], g)
                    mm(ps, lower16, oh_b[s], start=True, stop=False, skip_group_check=True)
                    mm(ps3, ones16, cum[s].unsqueeze(1).to_broadcast([P, G4, BLOCKS]), start=False, stop=False,
                       skip_group_check=True)
                    for u in range(G4 - 1):
                        mm(ps3[:, u + 1:, :], ones16,
                           oh_b[s][:, u * BLOCKS:(u + 1) * BLOCKS].unsqueeze(1).to_broadcast([P, G4 - 1 - u, BLOCKS]),
                           start=False, stop=False, skip_group_check=True)
                    mm(ps3, row128[0:1, :],
                       base16[0:1, s * BLOCKS:(s + 1) * BLOCKS].unsqueeze(1).to_broadcast([1, G4, BLOCKS]),
                       start=False, stop=True, skip_group_check=True).then_inc(rk_mm[s], 1)

            group(0)
            with e.Fori(1, GROUPS) as g:
                group(g)

        def prep_gpsimd(e):
            e.wait_ge(filled, 32)

            def group(g):
                for s in range(2):
                    e.wait_ge(rk_row[s], g + 1)
                    e.wait_ge(rk_pay[s], g + 1)
                    e.sem_inc(issuing, 1)
                    for u in range(G4):
                        e.indirect_dma_start(
                            out=tabs[s], out_offset=bass.IndirectOffsetOnAxis(ap=row_i[s][:, u:u + 1], axis=0),
                            in_=pring[s][:, u * pay_n[s]:(u + 1) * pay_n[s]], in_offset=None,
                        ).then_inc(sent[s][u], 16)

            group(0)
            with e.Fori(1, GROUPS) as g:
                group(g)

        def prep_sync_end(e):
            for s in range(2):
                for u in range(G4):
                    e.wait_ge(sent[s][u], 16 * GROUPS)
            e.dma_start(tabs_sb, tab_s.rearrange("(p a) f -> p (a f)", p=P)).then_inc(tab_in, 16)
            e.dma_start(tabd_sb, tab_d.rearrange("(p a) f -> p (a f)", p=P)).then_inc(tab_in, 16)

        wp = 0

        def ring(n, dt=f32):
            nonlocal wp
            wp += n
            a = work[:, wp - n:wp]
            return a if dt == f32 else a.bitcast(dt)

        stage = [ring(HU, i32) for _ in range(2)]
        stage2 = [ring(HU, i32) for _ in range(2)]
        rows = ring(U * D)
        rows2 = ring(U * D)
        onehot = [ring(BW) for _ in range(2)]
        iota_w = iota16[:, 0:BW]
        h_r = [ring(D) for _ in range(2)]
        ht_r = [ring(P) for _ in range(2)]
        zb_r = [ring(BASIS * D) for _ in range(2)]
        red_r = [ring(D) for _ in range(2)]
        pre_r = [ring(D) for _ in range(2)]
        msg_r = [ring(D) for _ in range(2)]
        assert wp <= 14 * CE
        LOOPS = TILES // U
        LAG = 5

        class Pass:
            def __init__(self, table, idx, key, side, k, table2=None, m=0):
                self.table, self.idx, self.key, self.side, self.table2 = table, idx, key, side, table2
                self.t0, self.e0, self.m0 = k * TILES, k * LOOPS, m * TILES

        def pass_scalar(e, q):
            def body(i):
                for h in range(2):
                    wait_past(e, sum_ready, q.t0 + (i - 1) * U + (h + 1) * HU)
                    e.copy(stage[h], q.idx[:, ds(i * U + h * HU, HU)]).then_inc(staged, 1)
            body(0)
            with e.Fori(1, LOOPS) as i:
                body(i)

        def pass_gpsimd(e, q):
            def body(i):
                for u in range(U):
                    h = u // HU
                    if u % HU == 0:
                        e.wait_ge(staged, 2 * q.e0 + 2 * i + h + 1)
                    wait_past(e, sum_ready, q.t0 + (i - 1) * U + u + 1)
                    e.sem_inc(issuing, 1)
                    if q.table2 is not None:
                        e.indirect_dma_start(out=rows2[:, u * D:(u + 1) * D], out_offset=None, in_=q.table2,
                                             in_offset=bass.IndirectOffsetOnAxis(
                                                 ap=stage2[h][:, u % HU:u % HU + 1], axis=0)).then_inc(got2[u], 16)
                    e.indirect_dma_start(out=rows[:, u * D:(u + 1) * D], out_offset=None, in_=q.table,
                                         in_offset=bass.IndirectOffsetOnAxis(
                                             ap=stage[h][:, u % HU:u % HU + 1], axis=0)).then_inc(got[u], 16)
            body(0)
            with e.Fori(1, LOOPS) as i:
                body(i)

        def sums(u):
            return PS[:, 512 * (u % 2):512 * (u % 2) + BCOLS * D]

        def tile_sum(e, q, t, u, msg):
            e.wait_ge(onehot_ready, q.t0 + t + 1)
            wait_past(e, added, q.t0 + t - 1)
            for j in range(BCOLS):
                ins = nc.tensor.matmul(sums(u)[:, j * D:(j + 1) * D], onehot[u % 2][:, j * P:(j + 1) * P], msg,
                                       start=True, stop=True)
            ins.then_inc(sum_ready, 1)

        def pass_tensor(e, q):
            def body(i):
                for u in range(U):
                    e.wait_ge(got[u], 16 * (q.e0 + i + 1))
                    tile_sum(e, q, i * U + u, u, rows[:, u * D:(u + 1) * D])
            body(0)
            with e.Fori(1, LOOPS) as i:
                body(i)

        def make_onehot(e, q, t, par):
            wait_past(e, sum_ready, q.t0 + t - 1)
            nc.vector.tensor_scalar(onehot[par], iota_w, q.key[:, ds(t, 1)], None,
                                    ALU.is_equal).then_inc(onehot_ready, 1)

        def add_tile(e, q, t, u, where):
            e.wait_ge(sum_ready, q.t0 + t + 1)
            wait_past(e, added, q.t0 + t)
            a = acc[:, ds(where, BCOLS * D)]
            nc.vector.tensor_tensor(a, a, sums(u), ALU.add).then_inc(added, 1)

        def load_blocks(e, q, i, regs, n=U):
            e.load(regs[0:n], block_at[0:1, q.side, ds(i * U, n)])
            return [e.snap(r, min_val=0, max_val=(BLOCKS - 1) * BCOLS * D) for r in regs[0:n]]

        def pass_vector(e, q, regs):
            def body(i, last):
                at = load_blocks(e, q, i, regs)
                for u in range(U):
                    if not (last and u == U - 1):
                        make_onehot(e, q, i * U + u + 1, (u + 1) % 2)
                    add_tile(e, q, i * U + u, u, at[u])
            make_onehot(e, q, 0, 0)
            body(0, False)
            with e.Fori(1, LOOPS - 1) as i:
                body(i, False)
            body(LOOPS - 1, True)

        def edge_tensor(e, q):
            mm = nc.tensor.matmul

            def turn(t, u):
                e.wait_ge(h_ready, q.m0 + t + 1)
                wait_past(e, ht_ready, q.m0 + t - 1)
                mm(PS[0:D, 1024 + 512 * (u % 2):1024 + 512 * (u % 2) + P], h_r[u % 2], ident,
                   start=True, stop=True).then_inc(ht_mm, 1)

            def mix(t, u):
                e.wait_ge(ht_ready, q.m0 + t + 1)
                wait_past(e, z_used, q.m0 + t - 1)
                mm(PS[:, 2048 + 512 * (u % 2):2560 + 512 * (u % 2)], ht_r[u % 2][0:D, :], vmix[:, :],
                   start=True, stop=True).then_inc(z_mm, 1)

            def scatter(t, u):
                e.wait_ge(msg_ready, q.m0 + t + 1)
                tile_sum(e, q, t, u, msg_r[u % 2])

            def body(i):
                for u in range(U):
                    t = i * U + u
                    turn(t, u)
                    if not (isinstance(t, int) and t < 1):
                        mix(t - 1, u - 1)
                    if not (isinstance(t, int) and t < 3):
                        scatter(t - 3, u - 3)
            body(0)
            with e.Fori(1, LOOPS) as i:
                body(i)
            mix(TILES - 1, U - 1)
            for t in range(TILES - 3, TILES):
                scatter(t, t)

        def edge_scalar(e, q):
            def stage_half(i, h):
                wait_past(e, h_ready, q.m0 + (i - 1) * U + (h + 1) * HU)
                e.copy(stage2[h], own_s[:, ds(i * U + h * HU, HU)]).then_inc(act_prep, 1)
                e.copy(stage[h], q.idx[:, ds(i * U + h * HU, HU)]).then_inc(staged, 1)

            def turn_out(t, u):
                e.wait_ge(ht_mm, q.m0 + t + 1)
                wait_past(e, z_mm, q.m0 + t - 1)
                e.copy(ht_r[u % 2][0:D, :], PS[0:D, 1024 + 512 * (u % 2):1024 + 512 * (u % 2) + P]).then_inc(ht_ready, 1)

            def message(t, u):
                e.wait_ge(pre_ready, q.m0 + t + 1)
                wait_past(e, sum_ready, q.t0 + t - 1)
                e.activation(msg_r[u % 2], pre_r[u % 2], ACT.Tanh).then_inc(msg_ready, 1)

            def body(i, last):
                for u in range(U):
                    t = i * U + u
                    turn_out(t, u)
                    if not (isinstance(t, int) and t < 2):
                        message(t - 2, u - 2)
                    if u == 0 and not (isinstance(i, int) and i == 0):
                        stage_half(i, 1)
                    if u == HU and not last:
                        stage_half(i + 1, 0)
            stage_half(0, 0)
            stage_half(0, 1)
            body(0, False)
            with e.Fori(1, LOOPS - 1) as i:
                body(i, False)
            body(LOOPS - 1, True)
            for t in range(TILES - 2, TILES):
                message(t, t)

        def edge_vector(e, q, regs):
            v = nc.vector

            def ends(t, u, i):
                e.wait_ge(got[u], 16 * (q.e0 + i + 1))
                e.wait_ge(got2[u], 16 * (i + 1))
                wait_past(e, ht_mm, q.m0 + t - 1)
                v.tensor_tensor(h_r[u % 2], rows[:, u * D:(u + 1) * D], rows2[:, u * D:(u + 1) * D],
                                ALU.add).then_inc(h_ready, 1)

            def weigh(t, u):
                s = u % 2
                e.wait_ge(z_mm, q.m0 + t + 1)
                v.tensor_tensor(zb_r[s].rearrange("p (b c) -> p b c", b=BASIS),
                                PS[:, 2048 + 512 * s:2560 + 512 * s].rearrange("p (b c) -> p b c", b=BASIS),
                                basis[:, ds(t, 1), :].rearrange("p o b -> p (o b)").unsqueeze(2).to_broadcast([P, BASIS, D]),
                                ALU.mult).then_inc(z_used, 1)
                e.wait_ge(z_used, q.m0 + t + 1)
                v.tensor_reduce(red_r[s], zb_r[s].rearrange("p (b c) -> p c b", b=BASIS), AX.X,
                                ALU.add).then_inc(l1_dve, 1)
                e.wait_ge(l1_dve, t + 1)
                wait_past(e, msg_ready, q.m0 + t - 1)
                v.tensor_tensor(pre_r[s], red_r[s], b_ii, ALU.add).then_inc(pre_ready, 1)

            def blocks_from(t, n):
                e.load(regs[0:n], block_at[0:1, q.side, ds(t, n)])
                return [e.snap(r, min_val=0, max_val=(BLOCKS - 1) * BCOLS * D) for r in regs[0:n]]

            def body(i):
                first = isinstance(i, int)
                at = [None] * LAG + blocks_from(0, U - LAG) if first else blocks_from(i * U - LAG, U)
                for u in range(U):
                    t = i * U + u
                    ends(t, u, i)
                    if not (first and t < 2):
                        weigh(t - 2, u - 2)
                    if not (first and t < 3):
                        make_onehot(e, q, t - 3, (u - 3) % 2)
                    if not (first and t < 5):
                        add_tile(e, q, t - LAG, u - LAG, at[u])
            body(0)
            with e.Fori(1, LOOPS) as i:
                body(i)
            tail = blocks_from(TILES - LAG, LAG)
            for k in range(LAG):
                t = TILES + k
                if k < 2:
                    weigh(t - 2, t)
                if k < 3:
                    make_onehot(e, q, t - 3, (t - 3) % 2)
                add_tile(e, q, t - LAG, t - LAG, tail[k])


        def chunk_of(a, n):
            return a[:, ds(n * CE, CE)]

        def buf(k):
            return work[:, k * CE:(k + 1) * CE]

        def c3(a):
            return a.rearrange("p (c d) -> p c d", d=D)

        def per_node(a, n):
            return a[:, ds(n * CC, CC)].unsqueeze(2).to_broadcast([P, CC, D])

        def feat(a):
            return a.unsqueeze(1).to_broadcast([P, CC, D])

        IN0, IN1 = [buf(0), buf(1)], [buf(2), buf(3)]
        OUT0, OUT1, OUT2 = [buf(4), buf(5)], [buf(6), buf(7)], [buf(8), buf(9)]
        TMP0, TMP1, TMP2, TMP3 = buf(10), buf(11), buf(12), buf(13)
        HALF = CHUNKS // 2

        class Phase:
            def __init__(self, k, ins, outs, norm, prods, uses_acc=True):
                self.k, self.ins, self.outs, self.norm, self.prods, self.uses_acc = k, ins, outs, norm, prods, uses_acc
                self.c0 = k * CHUNKS

        def over_chunks(e, chunk):
            chunk(0, 0, 0)
            chunk(0, 1, 1)
            with e.Fori(1, HALF) as j:
                chunk(j, 0, 2 * j)
                chunk(j, 1, 2 * j + 1)

        totals = dict(ld=0, st=0, ln=0, acc=0, mi=0)

        def plan(ph):
            ph.ld0, ph.st0, ph.ln0, ph.acc0, ph.mi0 = (totals[x] for x in ("ld", "st", "ln", "acc", "mi"))
            totals["ld"] += 16 * len(ph.ins) * HALF
            totals["st"] += 16 * len(ph.outs) * HALF
            totals["ln"] += CHUNKS if ph.norm else 0
            totals["acc"] += CHUNKS if ph.uses_acc else 0
            totals["mi"] += CHUNKS if ph.prods else 0
            return ph

        def dense_sync(e, ph):
            bufs_in, bufs_out = [IN0, IN1], [OUT0, OUT1, OUT2]

            def load(n, h):
                wait_past(e, in_used, ph.c0 + n - 1 if not (isinstance(n, int) and n < 2) else 0)
                for a, t in zip(bufs_in, ph.ins):
                    e.dma_start(a[h], chunk_of(per_partition(t), n)).then_inc(loaded[h], 16)

            def store(n, h):
                e.wait_ge(out_ready, ph.c0 + n + 1)
                for a, t in zip(bufs_out, ph.outs):
                    e.dma_start(chunk_of(per_partition(t), n), a[h]).then_inc(stored[h], 16)

            load(0, 0)
            load(1, 1)
            store(0, 0)
            with e.Fori(1, HALF) as j:
                load(2 * j, 0)
                store(2 * j - 1, 1)
                load(2 * j + 1, 1)
                store(2 * j, 0)
            store(CHUNKS - 1, 1)
            for h in range(2):
                e.wait_ge(stored[h], ph.st0 + 16 * len(ph.outs) * HALF)

        def dense_gpsimd(e, ph):
            if not ph.uses_acc:
                return

            def chunk(j, h, n):
                e.wait_ge(acc_used, ph.acc0 + n + 1)
                e.tensor_copy(chunk_of(acc, n), zero[:, 0:1].to_broadcast([P, CE])).then_inc(cleared, 1)
            over_chunks(e, chunk)

        def dense_vector(e, ph, first_part, last_part):
            v = nc.vector
            count = [0]

            def chunk(j, h, n, before):
                count[0] = 0

                def link(ins):
                    count[0] += 1
                    ins.then_inc(n_dve, 1)
                    e.wait_ge(n_dve, before + count[0])

                e.wait_ge(loaded[h], ph.ld0 + 16 * len(ph.ins) * (j + 1))
                wait_past(e, stored[h], ph.st0 + 16 * len(ph.outs) * j)
                first_part(e, ph, v, h, n, link)
                last_part(e, ph, v, h, n, link)
                return count[0]

            base = dve_total[0]
            k = chunk(0, 0, 0, base)
            assert chunk(0, 1, 1, base + k) == k
            with e.Fori(1, HALF) as j:
                chunk(j, 0, 2 * j, base + 2 * j * k)
                chunk(j, 1, 2 * j + 1, base + 2 * j * k + k)
            dve_total[0] += k * CHUNKS

        dve_total = [0]
        mean, var, rstd = st[:, 0, :], st[:, 1, :], st[:, 2, :]
        root = st[:, 3, :]

        def bc(a):
            return a.unsqueeze(2).to_broadcast([P, CC, D])

        def normalise(e, ph, v, n, link, src, dst, cen):
            link(v.tensor_reduce(mean, c3(src), AX.X, ALU.add))
            link(v.tensor_scalar(mean, mean, 1.0 / D, None, ALU.mult))
            v.tensor_tensor(c3(cen), c3(src), bc(mean), ALU.subtract).then_inc(centered, 1)
            e.wait_ge(squared, ph.ln0 + n + 1)
            link(v.tensor_reduce(var, c3(TMP1), AX.X, ALU.add))
            v.tensor_scalar(var, var, 1.0 / D, EPS, ALU.mult, ALU.add).then_inc(var_ready, 1)
            e.wait_ge(root_ready, ph.ln0 + n + 1)
            link(v.reciprocal(rstd, root))
            link(v.scalar_tensor_tensor(c3(dst), c3(cen), 0.0, bc(rstd), ALU.max, ALU.mult))

        def norm_scalar(e, ph, n):
            e.wait_ge(centered, ph.ln0 + n + 1)
            e.activation(TMP1, TMP0, ACT.Square).then_inc(squared, 1)
            e.wait_ge(var_ready, ph.ln0 + n + 1)
            e.activation(root, var, ACT.Sqrt).then_inc(root_ready, 1)

        def nothing(*a):
            pass

        def p0_last(e, ph, v, h, n, link):
            x = IN0[h]
            normalise(e, ph, v, n, link, x, TMP2, TMP0)
            link(v.tensor_tensor(c3(OUT0[h]), c3(TMP2), per_node(dinv, n), ALU.mult))
            v.scalar_tensor_tensor(OUT1[h], TMP2, 1.0 / 3.0, x, ALU.mult, ALU.add).then_inc(out_ready, 1)
            e.wait_ge(out_ready, ph.c0 + n + 1)
            e.sem_inc(in_used, 1)

        def p1_last(e, ph, v, h, n, link):
            v.tensor_tensor(c3(TMP2), c3(chunk_of(acc, n)), per_node(dinv, n), ALU.mult).then_inc(acc_used, 1)
            e.wait_ge(acc_used, ph.acc0 + n + 1)
            link(v.tensor_tensor(c3(OUT0[h]), c3(TMP2), per_node(dinv, n), ALU.mult))
            v.scalar_tensor_tensor(OUT1[h], TMP2, 1.0 / 3.0, IN0[h], ALU.mult, ALU.add).then_inc(out_ready, 1)
            e.wait_ge(out_ready, ph.c0 + n + 1)
            e.sem_inc(in_used, 1)

        def p2_first(e, ph, v, h, n, link):
            v.tensor_tensor(c3(TMP2), c3(chunk_of(acc, n)), per_node(dinv, n), ALU.mult).then_inc(acc_used, 1)
            e.wait_ge(acc_used, ph.acc0 + n + 1)
            link(v.scalar_tensor_tensor(TMP2, TMP2, 1.0 / 3.0, IN0[h], ALU.mult, ALU.add))
            normalise(e, ph, v, n, link, TMP2, TMP3, TMP0)
            e.sem_inc(mm_in, 1)
            link(v.tensor_tensor(OUT0[h], TMP2, TMP3, ALU.add))
            e.sem_inc(in_used, 1)

        def p2_last(e, ph, v, h, n, link):
            e.wait_ge(prod3, n + 1)
            ac = PS[:, 2048:2048 + PAIRS * 256].rearrange("p (g s c) -> p g s c", s=2, c=P)
            v.tensor_tensor(OUT1[h].rearrange("p (g n d) -> p g n d", n=2, d=D),
                            ac[:, :, 0, :].rearrange("p g (n d) -> p g n d", d=D),
                            b_pi1.unsqueeze(1).unsqueeze(1).to_broadcast([P, PAIRS, 2, D]), ALU.add)
            link(v.tensor_copy(OUT2[h].rearrange("p (g c) -> p g c", c=P), ac[:, :, 1, :]))
            e.sem_inc(prod_out, 1)
            e.sem_inc(out_ready, 1)

        def turn_chunk(srcs, at):
            for k, s in enumerate(srcs):
                for g in range(PAIRS):
                    ins = nc.tensor.transpose(PS[:, at + 1024 * k + g * P:at + 1024 * k + (g + 1) * P],
                                              s[:, g * P:(g + 1) * P], ident)
            return ins

        def p2_tensor(e, ph):
            mm = nc.tensor.matmul

            def chunk(j, h, n):
                e.wait_ge(mm_in, ph.mi0 + n + 1)
                wait_past(e, turned_sb, n)
                turn_chunk([TMP3], 0).then_inc(turned, 1)
                e.wait_ge(turned_sb, n + 1)
                wait_past(e, prod_act, n)
                mm(PS[:, 1024:1536], W["pp"], OUTT[:, 0:512], start=True, stop=True)
                mm(PS[:, 1536:1024 + CE], W["pp"], OUTT[:, 512:CE], start=True, stop=True).then_inc(prod, 1)
                e.wait_ge(prod_act, n + 1)
                wait_past(e, prod_out, n)
                for g in range(PAIRS):
                    ins = mm(PS[:, 2048 + g * 256:2048 + (g + 1) * 256], P1T[:, g * P:(g + 1) * P],
                             w_sb[:, P:3 * P], start=True, stop=True)
                ins.then_inc(prod3, 1)
            over_chunks(e, chunk)

        OUTT, P1T = IN1[0], IN1[1]

        def p2_scalar(e, ph):
            def chunk(j, h, n):
                norm_scalar(e, ph, n)
                e.wait_ge(turned, n + 1)
                wait_past(e, prod, n)
                e.copy(OUTT, PS[:, 0:CE]).then_inc(turned_sb, 1)
                e.wait_ge(prod, n + 1)
                wait_past(e, prod3, n)
                e.activation(P1T, PS[:, 1024:1024 + CE], ACT.Tanh, bias=b_pp).then_inc(prod_act, 1)
            over_chunks(e, chunk)

        def p3_last(e, ph, v, h, n, link):
            v.tensor_tensor(OUT1[h], chunk_of(acc, n), IN0[h], ALU.add).then_inc(acc_used, 1)
            e.wait_ge(acc_used, ph.acc0 + n + 1)
            e.sem_inc(in_used, 1)
            normalise(e, ph, v, n, link, OUT1[h], OUT0[h], TMP0)
            e.sem_inc(out_ready, 1)

        def gin_first(ep):
            def part(e, ph, v, h, n, link):
                v.scalar_tensor_tensor(TMP3, IN0[h], ep, chunk_of(acc, n), ALU.mult, ALU.add).then_inc(mm_in, 1)
                e.wait_ge(mm_in, ph.mi0 + n + 1)
                e.sem_inc(acc_used, 1)
            return part

        def p4_last(e, ph, v, h, n, link):
            e.wait_ge(prod3, CHUNKS + n + 1)
            v.scalar_tensor_tensor(OUT1[h], PS[:, 3072:3072 + CE], 0.5, IN1[h], ALU.mult, ALU.add).then_inc(prod_out, 1)
            e.wait_ge(prod_out, CHUNKS + n + 1)
            e.sem_inc(in_used, 1)

        def p4_tensor(e, ph):
            mm = nc.tensor.matmul
            c0 = CHUNKS

            def chunk(j, h, n):
                e.wait_ge(mm_in, ph.mi0 + n + 1)
                wait_past(e, turned_sb, c0 + n)
                turn_chunk([TMP3], 0).then_inc(turned, 1)
                e.wait_ge(turned_sb, c0 + n + 1)
                wait_past(e, prod_act, c0 + n)
                mm(PS[:, 1024:1536], W["g0"], TMP0[:, 0:512], start=True, stop=True)
                mm(PS[:, 1536:1024 + CE], W["g0"], TMP0[:, 512:CE], start=True, stop=True)
                for g in range(PAIRS):
                    ins = mm(PS[:, 2048 + g * P:2048 + (g + 1) * P], TMP0[:, g * P:(g + 1) * P], W["g0"],
                             start=True, stop=True)
                ins.then_inc(prod, 1)
                e.wait_ge(prod_act, c0 + n + 1)
                wait_past(e, prod_out, c0 + n)
                for g in range(PAIRS):
                    ins = mm(PS[:, 3072 + g * P:3072 + (g + 1) * P], TMP1[:, g * P:(g + 1) * P], W["gm"],
                             start=True, stop=True)
                ins.then_inc(prod3, 1)
            over_chunks(e, chunk)

        def p4_scalar(e, ph):
            c0 = CHUNKS

            def chunk(j, h, n):
                e.wait_ge(turned, c0 + n + 1)
                wait_past(e, prod, c0 + n)
                e.copy(TMP0, PS[:, 0:CE]).then_inc(turned_sb, 1)
                e.wait_ge(prod, c0 + n + 1)
                wait_past(e, prod3, c0 + n)
                wait_past(e, stored[h], ph.st0 + 16 * len(ph.outs) * j)
                e.activation(TMP1, PS[:, 1024:1024 + CE], ACT.Relu)
                e.activation(OUT0[h], PS[:, 2048:2048 + CE], ACT.Relu).then_inc(prod_act, 1)
                e.wait_ge(prod_out, c0 + n + 1)
                e.wait_ge(prod_act, c0 + n + 1)
                e.sem_inc(out_ready, 1)
            over_chunks(e, chunk)

        def p5_last(e, ph, v, h, n, link):
            e.wait_ge(prod_act, 2 * CHUNKS + n + 1)
            v.tensor_tensor(OUT1[h], TMP2, IN1[h], ALU.add).then_inc(prod_out, 1)
            e.wait_ge(prod_out, 2 * CHUNKS + n + 1)
            e.sem_inc(in_used, 1)
            normalise(e, ph, v, n, link, OUT1[h], OUT0[h], TMP0)
            e.sem_inc(out_ready, 1)

        OTH = OUT2[0]

        def p5_tensor(e, ph):
            mm, c0 = nc.tensor.matmul, 2 * CHUNKS

            def chunk(j, h, n):
                e.wait_ge(mm_in, ph.mi0 + n + 1)
                wait_past(e, turned_sb, c0 + n)
                turn_chunk([TMP3], 0).then_inc(turned, 1)
                e.wait_ge(turned_sb, c0 + n + 1)
                wait_past(e, prod_act, c0 + n)
                for g in range(PAIRS):
                    ins = mm(PS[:, 1024 + g * P:1024 + (g + 1) * P], OTH[:, g * P:(g + 1) * P], W["g1"],
                             start=True, stop=True)
                ins.then_inc(prod, 1)
            over_chunks(e, chunk)

        def p5_scalar(e, ph):
            c0 = 2 * CHUNKS

            def chunk(j, h, n):
                e.wait_ge(turned, c0 + n + 1)
                wait_past(e, prod, c0 + n)
                e.copy(OTH, PS[:, 0:CE]).then_inc(turned_sb, 1)
                e.wait_ge(prod, c0 + n + 1)
                wait_past(e, prod_out, c0 + n)
                e.activation(TMP2, PS[:, 1024:1024 + CE], ACT.Relu, scale=0.5).then_inc(prod_act, 1)
                norm_scalar(e, ph, n)
            over_chunks(e, chunk)

        def sage_first(e, ph, v, h, n, link):
            v.tensor_tensor(c3(TMP3), c3(chunk_of(acc, n)), per_node(rdeg, n), ALU.mult).then_inc(mm_in, 1)
            e.wait_ge(mm_in, ph.mi0 + n + 1)
            e.sem_inc(acc_used, 1)

        def sage_tensor(wx, wa, c0):
            mm = nc.tensor.matmul

            def run(e, ph):
                def chunk(j, h, n):
                    e.wait_ge(mm_in, ph.mi0 + n + 1)
                    wait_past(e, turned_sb, c0 + n)
                    turn_chunk([IN0[h], TMP3], 0).then_inc(turned, 1)
                    e.wait_ge(turned_sb, c0 + n + 1)
                    wait_past(e, prod_out, c0 + n)
                    for g in range(PAIRS):
                        o_ = PS[:, 2048 + g * P:2048 + (g + 1) * P]
                        mm(o_, TMP0[:, g * P:(g + 1) * P], W[wx], start=True, stop=False)
                        ins = mm(o_, TMP1[:, g * P:(g + 1) * P], W[wa], start=False, stop=True)
                    ins.then_inc(prod, 1)
                over_chunks(e, chunk)
            return run

        def sage_scalar(c0, last):
            def run(e, ph):
                def chunk(j, h, n):
                    e.wait_ge(turned, c0 + n + 1)
                    wait_past(e, prod, c0 + n)
                    e.copy(TMP0, PS[:, 0:CE])
                    e.copy(TMP1, PS[:, 1024:1024 + CE]).then_inc(turned_sb, 1)
                    if not last:
                        e.wait_ge(prod_out, c0 + n + 1)
                        wait_past(e, stored[h], ph.st0 + 16 * len(ph.outs) * j)
                        e.activation(OUT0[h], TMP2, ACT.Relu).then_inc(out_ready, 1)
                over_chunks(e, chunk)
            return run

        def p6_last(e, ph, v, h, n, link):
            e.wait_ge(prod, 3 * CHUNKS + n + 1)
            wait_past(e, out_ready, ph.c0 + n)
            v.tensor_tensor(c3(TMP2), c3(PS[:, 2048:2048 + CE]), feat(b_s1), ALU.add).then_inc(prod_out, 1)
            e.wait_ge(prod_out, 3 * CHUNKS + n + 1)
            e.sem_inc(in_used, 1)

        def p7_last(e, ph, v, h, n, link):
            link(v.tensor_tensor(c3(TMP2), c3(IN1[h]), feat(b_s2), ALU.add))
            e.wait_ge(prod, 4 * CHUNKS + n + 1)
            v.tensor_tensor(OUT0[h], PS[:, 2048:2048 + CE], TMP2, ALU.add).then_inc(prod_out, 1)
            e.wait_ge(prod_out, 4 * CHUNKS + n + 1)
            e.sem_inc(in_used, 1)
            e.sem_inc(out_ready, 1)

        def norm_only_scalar(e, ph):
            over_chunks(e, lambda j, h, n: norm_scalar(e, ph, n))

        phases = [
            plan(Phase(0, [x_in], [t_g0, r_0], True, False, False)),
            plan(Phase(1, [r_0], [t_g1, r_1], False, False)),
            plan(Phase(2, [r_1], [r_2, t_a, t_c], True, True)),
            plan(Phase(3, [r_2], [t_h2, r_3], True, False)),
            plan(Phase(4, [t_h2, r_3], [t_h1, r_4], False, True)),
            plan(Phase(5, [t_h1, r_4], [t_h3, r_5], True, True)),
            plan(Phase(6, [t_h3], [t_h4], False, True)),
            plan(Phase(7, [t_h4, r_5], [out], False, True)),
        ]
        vector_parts = [(nothing, p0_last), (nothing, p1_last), (p2_first, p2_last), (nothing, p3_last),
                        (gin_first(ep0), p4_last), (gin_first(ep1), p5_last), (sage_first, p6_last),
                        (sage_first, p7_last)]
        scalar_parts = [norm_only_scalar, nothing, p2_scalar, norm_only_scalar, p4_scalar, p5_scalar,
                        sage_scalar(3 * CHUNKS, False), sage_scalar(4 * CHUNKS, True)]
        tensor_parts = [nothing, nothing, p2_tensor, nothing, p4_tensor, p5_tensor,
                        sage_tensor("s1x", "s1a", 3 * CHUNKS), sage_tensor("s2x", "s2a", 4 * CHUNKS)]

        S, DD = (idx_s, key_s, 0), (idx_d, key_d, 1)
        passes = {
            0: [Pass(t_g0, *S, 0), Pass(t_g0, *DD, 1)],
            1: [Pass(t_g1, *S, 2), Pass(t_g1, *DD, 3)],
            2: [Pass(t_c, *S, 4, table2=t_a)],
            3: [Pass(t_h2, *DD, 5)],
            4: [Pass(t_h1, *DD, 6)],
            5: [Pass(t_h3, *S, 7)],
            6: [Pass(t_h4, *S, 8)],
            7: [],
        }

        @block.sync
        def _(e):
            prep_sync(e)
            prep_sync_end(e)
            end_phase(e, "sync")
            for k, ph in enumerate(phases):
                dense_sync(e, ph)
                end_phase(e, "sync")
                end_phase(e, "sync")

        @block.gpsimd
        def _(e):
            prep_gpsimd(e)
            end_phase(e, "pool")
            for k, ph in enumerate(phases):
                dense_gpsimd(e, ph)
                end_phase(e, "pool")
                for q in passes[k]:
                    pass_gpsimd(e, q)
                end_phase(e, "pool")

        @block.scalar
        def _(e):
            prep_scalar(e)
            end_phase(e, "act")
            for k, ph in enumerate(phases):
                scalar_parts[k](e, ph)
                end_phase(e, "act")
                for q in passes[k]:
                    (edge_scalar if q.table2 is not None else pass_scalar)(e, q)
                end_phase(e, "act")

        @block.tensor
        def _(e):
            prep_tensor(e)
            end_phase(e, "pe")
            for k, ph in enumerate(phases):
                tensor_parts[k](e, ph)
                end_phase(e, "pe")
                for q in passes[k]:
                    (edge_tensor if q.table2 is not None else pass_tensor)(e, q)
                end_phase(e, "pe")

        @block.vector
        def _(e):
            regs = [e.alloc_register(f"block_at_{u}") for u in range(U)]
            prep_vector(e)
            end_phase(e, "dve")
            for k, ph in enumerate(phases):
                dense_vector(e, ph, *vector_parts[k])
                end_phase(e, "dve")
                for q in passes[k]:
                    (edge_vector if q.table2 is not None else pass_vector)(e, q, regs)
                end_phase(e, "dve")


def kernel(**inputs):
    import numpy as np
    import concourse.bacc as bacc
    from concourse.bass_utils import run_bass_kernel_spmd

    a = {k: np.asarray(v) for k, v in inputs.items()}
    f = np.float32

    def pair(w):
        o = np.zeros((P, P), f)
        o[0:D, 0:D] = w
        o[D:, D:] = w
        return o

    def rows(v):
        return np.tile(v[None, :], (P, 1))

    x = np.zeros((NPAD, D), f)
    x[:NODES] = a["x"]

    def edge_list(v):
        o = np.full(EPAD, NPAD - 1, np.int32)
        o[:EDGES] = v
        return o.reshape(P, ETILES)

    attr = np.zeros((EPAD, BASIS), f)
    attr[:EDGES] = a["edge_attr_8"]
    k, m = np.meshgrid(np.arange(P), np.arange(P), indexing="ij")
    consts32 = np.zeros((P, CONST_COLS), f)
    consts32[:, 0:P] = k == m
    consts32[:BLOCKS, P:P + BLOCKS] = (k <= m)[:BLOCKS, :BLOCKS]
    consts32[:BLOCKS, P + BLOCKS:] = (k < m)[:BLOCKS, :BLOCKS]
    consts16 = np.concatenate([np.tile(np.arange(512), (P, 1)), k < m, np.ones((P, P))], 1).astype(np.float16)
    w1, s1, s2 = a["L1_gnn_pi_W1"], a["L3_gnn_W1"], a["L3_gnn_W2"]
    blocks = {"pp": a["L1_gnn_pp_W"], "w1a": w1[:D], "w1b": w1[D:], "g0": a["L2_gnn_W0"].T,
              "gm": a["L2_gnn_Wm"].T, "g1": a["L2_gnn_W1"].T, "s1x": s1[:D], "s1a": s1[D:],
              "s2x": s2[:D], "s2a": s2[D:]}
    vectors = np.concatenate(
        [rows(a["L1_gnn_pi_b1"]), rows(a["L1_gnn_ii_b"]), rows(a["L3_gnn_b1"]), rows(a["L3_gnn_b2"]),
         np.tile(a["L1_gnn_pp_b"], 2)[:, None], np.tile(a["L2_gnn_eps0"].reshape(1, 1), (P, 1)),
         np.tile(a["L2_gnn_eps1"].reshape(1, 1), (P, 1)), np.zeros((P, 1), f)], 1)
    arrays = {
        "x": x, "src": edge_list(a["src"]), "dst": edge_list(a["dst"]),
        "attr": attr.reshape(P, ETILES * BASIS), "consts32": consts32, "consts16": consts16,
        "weights": np.concatenate([pair(blocks[n]) for n in W_NAMES], 1),
        "w2t": a["L1_gnn_pi_W2"].reshape(D, D, BASIS).transpose(1, 2, 0).reshape(D, BASIS * D),
        "iiw": a["L1_gnn_ii_W"], "vectors": vectors,
    }
    nc = bacc.Bacc("TRN2", target_bir_lowering=False, num_devices=1)
    arrays = {f"in_{n}": np.ascontiguousarray(v) for n, v in arrays.items()}
    args = [nc.dram_tensor(n, v.shape, mybir.dt.from_np(v.dtype), kind="ExternalInput").ap()
            for n, v in arrays.items()]
    args.append(nc.dram_tensor("out", (NPAD, D), mybir.dt.float32, kind="ExternalOutput").ap())
    build_program(nc, *args)
    r = run_bass_kernel_spmd(nc, [arrays], core_ids=[0])
    return r.results[0]["out"][:NODES]
```

```python
import concourse.bass as bass
from concourse import mybir
from contextlib import ExitStack

P = 128
NODES = 50000
EDGES = 50000
D = 64
COLS = 392
NPAD = P * COLS
BCOLS = 4
BLOCKS = COLS // BCOLS
BW = BCOLS * P
ETILES = 392
EPAD = P * ETILES
TILES = ETILES + BLOCKS
SLOTS = P * TILES
BASIS = 8
FS = 3 + BASIS
FD = 2
U = 14
HU = U // 2
CC = 14
CHUNKS = COLS // CC
CE = CC * D
PAIRS = CC // 2
G4 = 4
GROUPS = ETILES // G4
EPS = 1e-5

CONST_COLS = 128 + 2 * 98
W_NAMES = ["pp", "w1a", "w1b", "g0", "gm", "g1", "s1x", "s1a", "s2x", "s2a"]


def build_program(nc, x_in, src_in, dst_in, attr_in, consts32, consts16, weights, w2t, iiw,
                  vectors, out):
    f32, i32 = mybir.dt.float32, mybir.dt.int32
    f16, bf16 = mybir.dt.float16, mybir.dt.bfloat16
    ALU, ACT, AX = mybir.AluOpType, mybir.ActivationFunctionType, mybir.AxisListType
    ds = bass.ds

    def dram(name, shape):
        return nc.dram_tensor(name, shape, f32, kind="Internal").ap()

    tab_s, tab_d = dram("tab_s", [SLOTS, FS]), dram("tab_d", [SLOTS, FD])
    t_g0, t_g1, t_a, t_c, t_h2, t_h1, t_h3, t_h4 = (
        dram(n, [NPAD, D]) for n in ("t_g0", "t_g1", "t_a", "t_c", "t_h2", "t_h1", "t_h3", "t_h4"))
    r_0, r_1, r_2, r_3, r_4, r_5 = (dram(n, [NPAD, D]) for n in ("r_0", "r_1", "r_2", "r_3", "r_4", "r_5"))

    def per_partition(t):
        return t.rearrange("(p c) d -> p (c d)", p=P)

    with ExitStack() as ctx:
        def sb(name, shape, dt=f32):
            return ctx.enter_context(nc.sbuf_tensor(name, shape, dt))

        def sem(name):
            return ctx.enter_context(nc.semaphore(name))

        acc = sb("acc", [P, COLS * D])
        work = sb("work", [P, 14 * CE])
        iota16 = sb("iota16", [P, 512], f16)
        mats16 = sb("mats16", [P, 2 * P], f16)
        c32 = sb("c32", [P, CONST_COLS])
        w_sb = sb("w_sb", [P, len(W_NAMES) * P])
        small64 = sb("small64", [D, D + 512])
        vmix = sb("vmix", [D, BASIS * D])
        vecs = sb("vecs", [P, 4 * D + 4])
        key_s, key_d = sb("key_s", [P, TILES]), sb("key_d", [P, TILES])
        idx_s, idx_d = sb("idx_s", [P, TILES], i32), sb("idx_d", [P, TILES], i32)
        own_s = sb("own_s", [P, TILES], i32)
        basis = sb("basis", [P, TILES, BASIS])
        block_at = sb("block_at", [1, 2, TILES // HU * 8], i32)
        dinv, rdeg = sb("dinv", [P, COLS]), sb("rdeg", [P, COLS])
        zero = sb("zero", [P, 1])
        st = sb("st", [P, 16, CC])

        PS = ctx.enter_context(nc.psum_tensor("PS", [P, 4096], f32))
        ident = c32[:, 0:P]
        pre_inc, pre_exc = c32[0:BLOCKS, P:P + 98], c32[0:BLOCKS, P + 98:P + 196]
        lower16, ones16 = mats16[:, 0:P], mats16[:, P:2 * P]
        W = {n: w_sb[:, i * P:(i + 1) * P] for i, n in enumerate(W_NAMES)}
        b_pi1, b_ii, b_s1, b_s2 = (vecs[:, i * D:(i + 1) * D] for i in range(4))
        b_pp, ep0, ep1 = (vecs[:, 4 * D + i:4 * D + i + 1] for i in range(3))

        phase_end = sem("phase_end")
        const_in, edges_in, filled = sem("const_in"), sem("edges_in"), sem("filled")
        dve_step = sem("dve_step")
        deg_oh, deg_mm = sem("deg_oh"), sem("deg_mm")
        pe_prep, dve_prep, act_prep = sem("pe_prep"), sem("dve_prep"), sem("act_prep")
        rk_oh = [sem(f"rk_oh{s}") for s in range(2)]
        rk_mm = [sem(f"rk_mm{s}") for s in range(2)]
        rk_row = [sem(f"rk_row{s}") for s in range(2)]
        rk_pay = [sem(f"rk_pay{s}") for s in range(2)]
        rk_cum = [sem(f"rk_cum{s}") for s in range(2)]
        rk_dve = sem("rk_dve")
        sent = [[sem(f"sent{s}{u}") for u in range(G4)] for s in range(2)]
        issuing = sem("issuing")
        tab_in = sem("tab_in")
        staged = sem("staged")
        got = [sem(f"got{h}") for h in range(2)]
        got_tile = [sem(f"got_tile{u}") for u in range(U)]
        got_tile2 = [sem(f"got_tile2_{u}") for u in range(U)]
        part_hi, part_r1, part_mid, part_r2, parts_ready = (
            sem(n) for n in ("part_hi", "part_r1", "part_mid", "part_r2", "parts_ready"))
        msg_hi, msg_r1, msg_mid, msg_r2 = (sem(n) for n in ("msg_hi", "msg_r1", "msg_mid", "msg_r2"))
        onehot_ready, sum_ready, added = sem("onehot_ready"), sem("sum_ready"), sem("added")
        h_ready, ht_mm, ht_ready, z_mm, z_used, pre_ready, msg_ready = (
            sem(n) for n in ("h_ready", "ht_mm", "ht_ready", "z_mm", "z_used", "pre_ready", "msg_ready"))
        loaded = [sem(f"loaded{h}") for h in range(2)]
        stored = [sem(f"stored{h}") for h in range(2)]
        n_dve = sem("n_dve")
        in_used, out_ready, acc_used, cleared = (sem(n) for n in ("in_used", "out_ready", "acc_used", "cleared"))
        centered, squared, var_ready, root_ready = (
            sem(n) for n in ("centered", "squared", "var_ready", "root_ready"))
        mm_in = sem("mm_in")
        turned, turned_sb, prod, prod_act = (sem(n) for n in ("turned", "turned_sb", "prod", "prod_act"))
        prod2, prod3, prod_out = sem("prod2"), sem("prod3"), sem("prod_out")

        block = ctx.enter_context(nc.Block())
        phase_no = {}

        def end_phase(e, name):
            phase_no[name] = phase_no.get(name, 0) + 1
            e.drain().then_inc(phase_end, 1)
            e.wait_ge(phase_end, 5 * phase_no[name])

        def wait_past(e, s, v):
            if isinstance(v, int) and v <= 0:
                return
            e.wait_ge(s, v)

        o = 0

        def scratch(n):
            nonlocal o
            o += n
            return acc[:, o - n:o]

        E2 = 2 * ETILES
        ed_i = scratch(E2).bitcast(i32)
        ti = scratch(E2).bitcast(i32)
        nf, q_p, r_m, q_b, rem_b, t1 = (scratch(E2) for _ in range(6))
        attr = scratch(ETILES * BASIS)
        pay_s, pay_d = scratch(ETILES * FS), scratch(ETILES * FD)
        deg = scratch(2 * COLS)
        degb = scratch(2 * BLOCKS)
        fill = acc[:, o:o + SLOTS * FS // P]
        tabs_sb = acc[:, o:o + TILES * FS]
        tabd_sb = acc[:, o + TILES * FS:o + TILES * (FS + FD)]
        wo = 0

        def wscratch(n, dt=f32):
            nonlocal wo
            words = n // 2 if dt in (f16, bf16) else n
            wo += words
            a = work[:, wo - words:wo]
            return a if dt == f32 else a.bitcast(dt)

        oh_p = [[wscratch(P, bf16) for _ in range(2)] for _ in range(2)]
        oh_m = [[wscratch(COLS, bf16) for _ in range(2)] for _ in range(2)]
        oh_b = [wscratch(G4 * BLOCKS, f16) for _ in range(2)]
        cum = [wscratch(BLOCKS, f16) for _ in range(2)]
        base16 = wscratch(2 * BLOCKS, f16)
        row128 = wscratch(P, f16)
        pick = [wscratch(G4 * BLOCKS) for _ in range(2)]
        csum = [wscratch(BLOCKS) for _ in range(2)]
        posf = [wscratch(G4) for _ in range(2)]
        pos_i, pos_lo, pos_hi, row_i = ([wscratch(G4, i32) for _ in range(2)] for _ in range(4))
        pring = [wscratch(G4 * FS), wscratch(G4 * FD)]
        tl = wscratch(2)
        tl_i = wscratch(2, i32)
        tl_w = wscratch(2 * P)
        end_t = wscratch(2)
        cmp16 = wscratch(2 * TILES, f16)
        ones32 = wscratch(1)
        pays, pay_n, tabs = [pay_s, pay_d], [FS, FD], [tab_s, tab_d]

        def prep_sync(e):
            for dst_, src_ in ((iota16[:, :], consts16[:, 0:512]), (mats16[:, :], consts16[:, 512:768]),
                               (c32[:, :], consts32), (w_sb[:, :], weights), (small64[:, 0:D], iiw),
                               (small64[:, D:], w2t), (vecs[:, :], vectors)):
                e.dma_start(dst_, src_).then_inc(const_in, 16)
            e.dma_start(ed_i[:, 0:ETILES], src_in).then_inc(edges_in, 16)
            e.dma_start(ed_i[:, ETILES:], dst_in).then_inc(edges_in, 16)
            e.dma_start(attr, attr_in).then_inc(edges_in, 16)
            e.wait_ge(dve_prep, 1)
            e.dma_start(tab_s.rearrange("(p a) f -> p (a f)", p=P), fill).then_inc(filled, 16)
            e.dma_start(tab_d.rearrange("(p a) f -> p (a f)", p=P), fill[:, 0:SLOTS * FD // P]).then_inc(filled, 16)

        def prep_vector(e):
            steps = [0]

            def step(ins):
                steps[0] += 1
                ins.then_inc(dve_step, 1)
                e.wait_ge(dve_step, steps[0])

            v = nc.vector
            v.memset(zero[:, :], 0.0)
            v.memset(block_at[:, :, :], 0)
            v.memset(fill, -1.0).then_inc(dve_prep, 1)
            v.memset(ones32, 1.0)
            v.memset(row128[0:1, :], 128.0)
            for s in range(2):
                v.memset(cum[s], 0.0)
            e.wait_ge(const_in, 16 * 7)
            step(v.tensor_scalar(vecs[:, 4 * D + 1:4 * D + 3], vecs[:, 4 * D + 1:4 * D + 3], 1.0, None, ALU.add))
            e.wait_ge(edges_in, 48)
            step(v.tensor_copy(nf, ed_i))

            def divmod_(a, n, q, r):
                step(v.tensor_scalar(t1, a, 1.0 / n, None, ALU.mult))
                step(v.tensor_copy(ti, t1))
                step(v.tensor_copy(q, ti))
                step(v.scalar_tensor_tensor(r, q, -float(n), a, ALU.mult, ALU.add))
                for op, bound, sign in ((ALU.is_lt, 0.0, -1.0), (ALU.is_ge, float(n), 1.0)):
                    step(v.tensor_scalar(t1, r, bound, sign, op, ALU.mult))
                    step(v.tensor_tensor(q, q, t1, ALU.add))
                    step(v.scalar_tensor_tensor(r, t1, -float(n), r, ALU.mult, ALU.add))

            divmod_(nf, COLS, q_p, r_m)
            divmod_(r_m, BCOLS, q_b, rem_b)
            step(v.scalar_tensor_tensor(t1, rem_b, float(P), q_p, ALU.mult, ALU.add))
            ps3 = pay_s.rearrange("p (t f) -> p t f", f=FS)
            pd3 = pay_d.rearrange("p (t f) -> p t f", f=FD)
            v.tensor_copy(ps3[:, :, 0], nf[:, ETILES:])
            v.tensor_copy(ps3[:, :, 1], t1[:, 0:ETILES])
            v.tensor_copy(ps3[:, :, 2], nf[:, 0:ETILES])
            v.tensor_copy(ps3[:, :, 3:], attr.rearrange("p (t f) -> p t f", f=BASIS))
            v.tensor_copy(pd3[:, :, 0], nf[:, 0:ETILES])
            step(v.tensor_copy(pd3[:, :, 1], t1[:, ETILES:]))

            def degree_tile(j, h):
                t = 2 * j + h
                for s in range(2):
                    wait_past(e, deg_mm, 2 * (t - 2) + s + 1)
                    v.tensor_scalar(oh_p[h][s], iota16[:, 0:P], q_p[:, ds(t + s * ETILES, 1)], None, ALU.is_equal)
                    v.tensor_scalar(oh_m[h][s], iota16[:, 0:COLS], r_m[:, ds(t + s * ETILES, 1)], None,
                                    ALU.is_equal).then_inc(deg_oh, 1)

            degree_tile(0, 0)
            degree_tile(0, 1)
            with e.Fori(1, ETILES // 2) as j:
                degree_tile(j, 0)
                degree_tile(j, 1)
            e.wait_ge(deg_mm, 2 * ETILES)
            for s in range(2):
                step(v.tensor_copy(deg[:, s * COLS:(s + 1) * COLS], PS[:, s * 512:s * 512 + COLS]))
            v.tensor_reduce(degb, deg.rearrange("p (b c) -> p b c", c=BCOLS), AX.X, ALU.add).then_inc(dve_prep, 1)
            e.wait_ge(pe_prep, 1)
            step(v.tensor_scalar(tl_i[0:BLOCKS, :], PS[0:BLOCKS, 1024:1026], float(P - 1), None, ALU.add))
            step(v.tensor_scalar(tl_i[0:BLOCKS, :], tl_i[0:BLOCKS, :], 7, None, ALU.logical_shift_right))
            step(v.tensor_copy(tl[0:BLOCKS, :], tl_i[0:BLOCKS, :]))
            v.tensor_copy(tl_w[0:BLOCKS, :].rearrange("b (s p) -> b s p", s=2),
                          tl[0:BLOCKS, :].unsqueeze(2).to_broadcast([BLOCKS, 2, P])).then_inc(dve_prep, 1)
            e.wait_ge(pe_prep, 2)
            step(v.tensor_copy(end_t[0:BLOCKS, :], PS[0:BLOCKS, 1536:1538]))
            v.tensor_copy(base16[0:1, :], PS[0:1, 2048:2048 + 2 * BLOCKS])
            for s in range(2):
                ins = v.tensor_scalar(cmp16[0:BLOCKS, s * TILES:(s + 1) * TILES], iota16[0:BLOCKS, 0:TILES],
                                      end_t[0:BLOCKS, s:s + 1], None, ALU.is_ge)
            ins.then_inc(dve_prep, 1)
            e.wait_ge(pe_prep, 3)
            for s in range(2):
                ins = v.tensor_scalar(block_at[0:1, s, :].rearrange("p (k u) -> p k u", u=8)[:, :, 0:HU],
                                      PS[0:1, 2560 + 512 * s:2560 + 512 * s + TILES].rearrange("p (k u) -> p k u", u=HU),
                                      float(BLOCKS - 1), float(BCOLS * D), ALU.min, ALU.mult)
            step(ins)
            step(v.tensor_tensor(t1[:, 0:COLS], deg[:, 0:COLS], deg[:, COLS:], ALU.add))
            v.tensor_scalar(t1[:, COLS:], t1[:, 0:COLS], 1.0, None, ALU.max).then_inc(dve_prep, 1)
            e.wait_ge(act_prep, 1)
            step(v.reciprocal(dinv[:, :], nf[:, 0:COLS]))
            step(v.tensor_scalar(t1[:, 0:COLS], t1[:, 0:COLS], 1.0, None, ALU.is_ge))
            step(v.tensor_tensor(dinv[:, :], dinv[:, :], t1[:, 0:COLS], ALU.mult))
            step(v.tensor_scalar(rdeg[:, :], deg[:, 0:COLS], 1.0, None, ALU.max))
            step(v.reciprocal(rdeg[:, :], rdeg[:, :]))
            e.wait_ge(pe_prep, 4)
            step(v.tensor_copy(vmix[:, :], PS[0:D, 3584:4096]))

            n = [0]

            def link(ins, before):
                n[0] += 1
                ins.then_inc(rk_dve, 1)
                e.wait_ge(rk_dve, before + n[0])

            def group(g, before):
                n[0] = 0
                for s in range(2):
                    oh3 = oh_b[s].rearrange("p (u b) -> p u b", u=G4)
                    v.tensor_tensor(oh3, iota16[:, 0:BLOCKS].unsqueeze(1).to_broadcast([P, G4, BLOCKS]),
                                    q_b[:, ds(g * G4 + s * ETILES, G4)].unsqueeze(2).to_broadcast([P, G4, BLOCKS]),
                                    ALU.is_equal).then_inc(rk_oh[s], 1)
                for s in range(2):
                    oh3 = oh_b[s].rearrange("p (u b) -> p u b", u=G4)
                    wait_past(e, rk_oh[s], g + 1)
                    link(v.tensor_reduce(csum[s], oh3.rearrange("p u b -> p b u"), AX.X, ALU.add), before)
                    e.wait_ge(rk_mm[s], g + 1)
                    link(v.tensor_tensor(pick[s], PS[:, 512 * s:512 * s + G4 * BLOCKS], oh_b[s], ALU.mult), before)
                    v.tensor_tensor(cum[s], cum[s], csum[s], ALU.add).then_inc(rk_cum[s], 1)
                    link(v.tensor_reduce(posf[s], pick[s].rearrange("p (u b) -> p u b", u=G4), AX.X, ALU.add), before)
                    link(v.tensor_copy(pos_i[s], posf[s]), before)
                    link(v.tensor_scalar(pos_lo[s], pos_i[s], P - 1, None, ALU.bitwise_and), before)
                    link(v.tensor_scalar(pos_hi[s], pos_i[s], 7, None, ALU.logical_shift_right), before)
                    for u in range(G4):
                        wait_past(e, sent[s][u], 16 * g)
                    v.scalar_tensor_tensor(row_i[s], pos_lo[s], float(TILES), pos_hi[s], ALU.mult,
                                           ALU.add).then_inc(rk_row[s], 1)
                return n[0]

            k = group(0, 0)
            with e.Fori(1, GROUPS) as g:
                group(g, g * k)
            e.wait_ge(tab_in, 32)
            s3 = tabs_sb.rearrange("p (t f) -> p t f", f=FS)
            d3 = tabd_sb.rearrange("p (t f) -> p t f", f=FD)
            v.tensor_scalar(idx_s[:, :], s3[:, :, 0], 0.0, None, ALU.max)
            v.tensor_copy(key_s[:, :], s3[:, :, 1])
            v.tensor_scalar(own_s[:, :], s3[:, :, 2], 0.0, None, ALU.max)
            v.tensor_copy(basis[:, :, :], s3[:, :, 3:])
            v.tensor_scalar(idx_d[:, :], d3[:, :, 0], 0.0, None, ALU.max)
            step(v.tensor_copy(key_d[:, :], d3[:, :, 1]))
            step(v.memset(acc[:, :], 0.0))

        def prep_scalar(e):
            e.wait_ge(dve_prep, 5)
            e.activation(nf[:, 0:COLS], t1[:, COLS:], ACT.Sqrt).then_inc(act_prep, 1)

            def group(g):
                for s in range(2):
                    for u in range(G4):
                        wait_past(e, sent[s][u], 16 * g)
                    n = G4 * pay_n[s]
                    e.copy(pring[s], pays[s][:, ds(g * n, n)]).then_inc(rk_pay[s], 1)

            group(0)
            with e.Fori(1, GROUPS) as g:
                group(g)

        def prep_tensor(e):
            mm = nc.tensor.matmul

            def degree_tile(t, h, start, stop):
                for s in range(2):
                    e.wait_ge(deg_oh, 2 * t + s + 1)
                    mm(PS[:, s * 512:s * 512 + COLS], oh_p[h][s], oh_m[h][s], start=start, stop=stop,
                       skip_group_check=True).then_inc(deg_mm, 1)

            degree_tile(0, 0, True, False)
            degree_tile(1, 1, False, False)
            with e.Fori(1, ETILES // 2 - 1) as j:
                degree_tile(2 * j, 0, False, False)
                degree_tile(2 * j + 1, 1, False, False)
            degree_tile(ETILES - 2, 0, False, False)
            degree_tile(ETILES - 1, 1, False, True)
            e.wait_ge(dve_prep, 2)
            for s in range(2):
                ins = mm(PS[0:BLOCKS, 1024 + s:1025 + s], degb[:, s * BLOCKS:(s + 1) * BLOCKS], ones32,
                         start=True, stop=True)
            ins.then_inc(pe_prep, 1)
            e.wait_ge(dve_prep, 3)
            for s in range(2):
                mm(PS[0:BLOCKS, 1536 + s:1537 + s], pre_inc, tl[0:BLOCKS, s:s + 1], start=True, stop=True)
                ins = mm(PS[:, 2048 + s * BLOCKS:2048 + (s + 1) * BLOCKS], tl_w[0:BLOCKS, s * P:(s + 1) * P],
                         pre_exc, start=True, stop=True)
            ins.then_inc(pe_prep, 1)
            e.wait_ge(dve_prep, 4)
            for s in range(2):
                ins = mm(PS[:, 2560 + 512 * s:2560 + 512 * s + TILES], ones16[0:BLOCKS, :],
                         cmp16[0:BLOCKS, s * TILES:(s + 1) * TILES], start=True, stop=True)
            ins.then_inc(pe_prep, 1)
            for b in range(BASIS):
                ins = mm(PS[0:D, 3584 + b * D:3584 + (b + 1) * D], small64[:, D + b * D:D + (b + 1) * D],
                         small64[:, 0:D], start=True, stop=True)
            ins.then_inc(pe_prep, 1)

            def group(g):
                for s in range(2):
                    ps = PS[:, 512 * s:512 * s + G4 * BLOCKS]
                    ps3 = ps.rearrange("p (u b) -> p u b", u=G4)
                    e.wait_ge(rk_oh[s], g + 1)
                    wait_past(e, rk_cum[s], g)
                    mm(ps, lower16, oh_b[s], start=True, stop=False, skip_group_check=True)
                    mm(ps3, ones16, cum[s].unsqueeze(1).to_broadcast([P, G4, BLOCKS]), start=False, stop=False,
                       skip_group_check=True)
                    for u in range(G4 - 1):
                        mm(ps3[:, u + 1:, :], ones16,
                           oh_b[s][:, u * BLOCKS:(u + 1) * BLOCKS].unsqueeze(1).to_broadcast([P, G4 - 1 - u, BLOCKS]),
                           start=False, stop=False, skip_group_check=True)
                    mm(ps3, row128[0:1, :],
                       base16[0:1, s * BLOCKS:(s + 1) * BLOCKS].unsqueeze(1).to_broadcast([1, G4, BLOCKS]),
                       start=False, stop=True, skip_group_check=True).then_inc(rk_mm[s], 1)

            group(0)
            with e.Fori(1, GROUPS) as g:
                group(g)

        def prep_gpsimd(e):
            e.wait_ge(filled, 32)

            def group(g):
                for s in range(2):
                    e.wait_ge(rk_row[s], g + 1)
                    e.wait_ge(rk_pay[s], g + 1)
                    e.sem_inc(issuing, 1)
                    for u in range(G4):
                        e.indirect_dma_start(
                            out=tabs[s], out_offset=bass.IndirectOffsetOnAxis(ap=row_i[s][:, u:u + 1], axis=0),
                            in_=pring[s][:, u * pay_n[s]:(u + 1) * pay_n[s]], in_offset=None,
                        ).then_inc(sent[s][u], 16)

            group(0)
            with e.Fori(1, GROUPS) as g:
                group(g)

        def prep_sync_end(e):
            for s in range(2):
                for u in range(G4):
                    e.wait_ge(sent[s][u], 16 * GROUPS)
            e.dma_start(tabs_sb, tab_s.rearrange("(p a) f -> p (a f)", p=P)).then_inc(tab_in, 16)
            e.dma_start(tabd_sb, tab_d.rearrange("(p a) f -> p (a f)", p=P)).then_inc(tab_in, 16)

        wp = 0

        def ring(n, dt=f32):
            nonlocal wp
            words = n // 2 if dt in (f16, bf16) else n
            wp += words
            a = work[:, wp - words:wp]
            return a if dt == f32 else a.bitcast(dt)

        HALVES = TILES // HU
        LOOPS = TILES // U
        LAG = 7
        stage = [ring(HU + 1, i32) for _ in range(2)]
        stage2 = [ring(HU + 1, i32) for _ in range(2)]
        rows = [ring(HU * D) for _ in range(2)]
        rows2 = [ring(HU * D) for _ in range(2)]
        parts = [ring(HU * 3 * D, bf16) for _ in range(2)]
        onehot = [ring(BW, bf16) for _ in range(2)]
        iota_w = iota16[:, 0:BW]
        h_r = [ring(D) for _ in range(2)]
        ht_r = [ring(P) for _ in range(2)]
        zb_r = [ring((BASIS + 1) * D) for _ in range(2)]
        pre_r = [ring(D) for _ in range(2)]
        msg_r = [ring(D) for _ in range(HU)]
        assert wp <= 14 * CE

        class Pass:
            def __init__(self, table, idx, key, side, k, plain, table2=None):
                self.table, self.idx, self.key, self.side, self.table2 = table, idx, key, side, table2
                self.t0, self.h0 = k * TILES, k * HALVES
                self.g0 = plain * LOOPS * 16 * HU
                self.s0 = plain * HALVES

        def sums(par):
            return PS[:, 512 * par:512 * par + BCOLS * D]

        def tile_sum(e, q, t, par, part3):
            e.wait_ge(onehot_ready, q.t0 + t + 1)
            wait_past(e, added, q.t0 + t - 1)
            for j in range(BCOLS):
                for k in range(3):
                    ins = nc.tensor.matmul(sums(par)[:, j * D:(j + 1) * D], onehot[par][:, j * P:(j + 1) * P],
                                           part3[:, k * D:(k + 1) * D], start=(k == 0), stop=(k == 2))
            ins.then_inc(sum_ready, 1)

        def make_onehot(e, q, t, par):
            wait_past(e, sum_ready, q.t0 + t - 1)
            nc.vector.tensor_scalar(onehot[par], iota_w, q.key[:, ds(t, 1)], None,
                                    ALU.is_equal).then_inc(onehot_ready, 1)

        def add_tile(e, q, t, par, where):
            e.wait_ge(sum_ready, q.t0 + t + 1)
            wait_past(e, added, q.t0 + t)
            a = acc[:, ds(where, BCOLS * D)]
            nc.vector.tensor_tensor(a, a, sums(par), ALU.add).then_inc(added, 1)

        def load_blocks(e, q, half, regs):
            e.load(regs, block_at[0:1, q.side, ds(half * 8, 8)])
            return [e.snap(r, min_val=0, max_val=(BLOCKS - 1) * BCOLS * D) for r in regs[0:HU]]

        def pass_gpsimd(e, q):
            def body(i):
                for h in range(2):
                    e.wait_ge(staged, q.h0 + 2 * i + h + 1)
                    if q.table2 is None:
                        wait_past(e, parts_ready, q.s0 + 2 * i + h - 1)
                    e.sem_inc(issuing, 1)
                    for u in range(HU):
                        if q.table2 is not None:
                            wait_past(e, h_ready, (i - 1) * U + h * HU + u + 1)
                            e.sem_inc(issuing, 1)
                            e.indirect_dma_start(out=rows2[h][:, u * D:(u + 1) * D], out_offset=None, in_=q.table2,
                                                 in_offset=bass.IndirectOffsetOnAxis(
                                                     ap=stage2[h][:, u:u + 1], axis=0)).then_inc(got_tile2[h * HU + u], 16)
                        e.indirect_dma_start(out=rows[h][:, u * D:(u + 1) * D], out_offset=None, in_=q.table,
                                             in_offset=bass.IndirectOffsetOnAxis(
                                                 ap=stage[h][:, u:u + 1], axis=0)).then_inc(
                            got[h] if q.table2 is None else got_tile[h * HU + u], 16)
            body(0)
            with e.Fori(1, LOOPS) as i:
                body(i)

        def pass_scalar(e, q):
            def stage_half(half, h):
                e.copy(stage[h][:, 0:HU], q.idx[:, ds(half * HU, HU)]).then_inc(staged, 1)

            def split(i, h, stages):
                half = 2 * i + h
                hi, mid, lo = (parts[h].rearrange("p (u k d) -> p u k d", k=3, d=D)[:, :, k, :] for k in range(3))
                r = rows[h].rearrange("p (u d) -> p u d", d=D)
                e.wait_ge(got[h], q.g0 + 16 * HU * (i + 1))
                wait_past(e, sum_ready, q.t0 + (half - 1) * HU)
                e.copy(hi, r).then_inc(part_hi, 1)
                if stages:
                    stage_half(half + 2, h)
                e.wait_ge(part_r1, q.s0 + half + 1)
                e.copy(mid, r).then_inc(part_mid, 1)
                e.wait_ge(part_r2, q.s0 + half + 1)
                e.copy(lo, r).then_inc(parts_ready, 1)

            stage_half(0, 0)
            stage_half(1, 1)
            split(0, 0, True)
            split(0, 1, True)
            with e.Fori(1, LOOPS - 1) as i:
                split(i, 0, True)
                split(i, 1, True)
            split(LOOPS - 1, 0, False)
            split(LOOPS - 1, 1, False)

        def pass_tensor(e, q):
            def half_sums(half, h):
                e.wait_ge(parts_ready, q.s0 + half + 1)
                for u in range(HU):
                    tile_sum(e, q, half * HU + u, (h + u) % 2, parts[h][:, u * 3 * D:(u + 1) * 3 * D])
            half_sums(0, 0)
            half_sums(1, 1)
            with e.Fori(1, LOOPS) as i:
                half_sums(2 * i, 0)
                half_sums(2 * i + 1, 1)

        def pass_vector(e, q, regs):
            def rest(half, h, k):
                got_part, signal = ((part_hi, part_r1), (part_mid, part_r2))[k]
                r = rows[h].rearrange("p (u d) -> p u d", d=D)
                part = parts[h].rearrange("p (u k d) -> p u k d", k=3, d=D)[:, :, k, :]
                e.wait_ge(got_part, q.s0 + half + 1)
                nc.vector.tensor_tensor(r, r, part, ALU.subtract).then_inc(signal, 1)

            def half_step(half, h, splits, last=False):
                at = load_blocks(e, q, half - 1, regs)
                for u in range(HU):
                    t, par = (half - 1) * HU + u, (h + 1 + u) % 2
                    if not (last and u == HU - 1):
                        make_onehot(e, q, t + 1, 1 - par)
                    add_tile(e, q, t, par, at[u])
                    if splits and u in (0, 2):
                        rest(half, h, u // 2)

            rest(0, 0, 0)
            rest(0, 0, 1)
            make_onehot(e, q, 0, 0)
            half_step(1, 1, True)
            with e.Fori(1, LOOPS) as i:
                half_step(2 * i, 0, True)
                half_step(2 * i + 1, 1, True)
            half_step(HALVES, 0, False, last=True)

        def edge_tensor(e, q):
            mm = nc.tensor.matmul

            def turn(t, par):
                e.wait_ge(h_ready, t + 1)
                wait_past(e, ht_ready, t - 1)
                mm(PS[0:D, 1024 + 512 * par:1024 + 512 * par + P], h_r[par], ident,
                   start=True, stop=True).then_inc(ht_mm, 1)

            def mix(t, par):
                e.wait_ge(ht_ready, t + 1)
                wait_past(e, z_used, t - 1)
                mm(PS[:, 2048 + 512 * par:2560 + 512 * par], ht_r[par][0:D, :], vmix[:, :],
                   start=True, stop=True).then_inc(z_mm, 1)

            def scatter(t, par, slot):
                e.wait_ge(msg_ready, t + 1)
                tile_sum(e, q, t, par, msg_part[slot])

            def body(i):
                for u in range(U):
                    t = i * U + u
                    early = t if isinstance(t, int) else LAG
                    turn(t, u % 2)
                    if early >= 1:
                        mix(t - 1, (u - 1) % 2)
                    if early >= 5:
                        scatter(t - 5, (u - 5) % 2, (u - 5) % HU)
            body(0)
            with e.Fori(1, LOOPS) as i:
                body(i)
            mix(TILES - 1, (TILES - 1) % 2)
            for t in range(TILES - 5, TILES):
                scatter(t, t % 2, t % HU)

        msg_part = [parts[0][:, k * 3 * D:(k + 1) * 3 * D] for k in range(HU)]

        def edge_scalar(e, q):
            def stage_half(half, h):
                wait_past(e, h_ready, (half - 1) * HU)
                e.copy(stage2[h][:, 0:HU], own_s[:, ds(half * HU, HU)])
                e.copy(stage[h][:, 0:HU], q.idx[:, ds(half * HU, HU)]).then_inc(staged, 1)

            def turn_out(t, par):
                e.wait_ge(ht_mm, t + 1)
                wait_past(e, z_mm, t - 1)
                e.copy(ht_r[par][0:D, :], PS[0:D, 1024 + 512 * par:1024 + 512 * par + P]).then_inc(ht_ready, 1)

            def message(t, par, slot):
                e.wait_ge(pre_ready, t + 1)
                wait_past(e, sum_ready, q.t0 + t - HU + 1)
                e.activation(msg_r[slot], pre_r[par], ACT.Tanh)
                e.activation(msg_part[slot][:, 0:D], pre_r[par], ACT.Tanh).then_inc(msg_hi, 1)

            def next_part(t, slot, k, ready, signal):
                e.wait_ge(ready, t + 1)
                e.copy(msg_part[slot][:, k * D:(k + 1) * D], msg_r[slot]).then_inc(signal, 1)

            def late(t, u):
                first, last = (t, t) if isinstance(t, int) else (LAG, 0)
                if 2 <= first and last - 2 < TILES:
                    message(t - 2, u % 2, (u - 2) % HU)
                if 3 <= first and last - 3 < TILES:
                    next_part(t - 3, (u - 3) % HU, 1, msg_r1, msg_mid)
                if 4 <= first and last - 4 < TILES:
                    next_part(t - 4, (u - 4) % HU, 2, msg_r2, msg_ready)

            def body(i, last):
                for u in range(U):
                    turn_out(i * U + u, u % 2)
                    late(i * U + u, u)
                    if u == 0 and not (isinstance(i, int) and i == 0):
                        stage_half(2 * i + 1, 1)
                    if u == HU and not last:
                        stage_half(2 * i + 2, 0)
            stage_half(0, 0)
            stage_half(1, 1)
            body(0, False)
            with e.Fori(1, LOOPS - 1) as i:
                body(i, False)
            body(LOOPS - 1, True)
            for t in range(TILES, TILES + 4):
                late(t, t)

        def edge_vector(e, q, regs):
            v = nc.vector
            for s in range(2):
                v.tensor_copy(zb_r[s][:, BASIS * D:], b_ii)

            def ends(t, u, i):
                e.wait_ge(got_tile[u], 16 * (i + 1))
                e.wait_ge(got_tile2[u], 16 * (i + 1))
                wait_past(e, ht_mm, t - 1)
                r = slice((u % HU) * D, (u % HU + 1) * D)
                v.tensor_tensor(h_r[u % 2], rows[u // HU][:, r], rows2[u // HU][:, r], ALU.add).then_inc(h_ready, 1)

            def weigh(t, par):
                e.wait_ge(z_mm, t + 1)
                v.tensor_tensor(zb_r[par][:, 0:BASIS * D].rearrange("p (b c) -> p b c", b=BASIS),
                                PS[:, 2048 + 512 * par:2560 + 512 * par].rearrange("p (b c) -> p b c", b=BASIS),
                                basis[:, ds(t, 1), :].rearrange("p o b -> p (o b)").unsqueeze(2).to_broadcast([P, BASIS, D]),
                                ALU.mult).then_inc(z_used, 1)
                e.wait_ge(z_used, t + 1)
                wait_past(e, msg_hi, t - 1)
                v.tensor_reduce(pre_r[par], zb_r[par].rearrange("p (b c) -> p c b", c=D), AX.X,
                                ALU.add).then_inc(pre_ready, 1)

            def rest(t, slot, k, ready, signal):
                e.wait_ge(ready, t + 1)
                v.tensor_tensor(msg_r[slot], msg_r[slot], msg_part[slot][:, k * D:(k + 1) * D],
                                ALU.subtract).then_inc(signal, 1)

            def late(t, u, where):
                first, last = (t, t) if isinstance(t, int) else (LAG, 0)
                if 2 <= first and last - 2 < TILES:
                    weigh(t - 2, u % 2)
                if 3 <= first and last - 3 < TILES:
                    rest(t - 3, (u - 3) % HU, 0, msg_hi, msg_r1)
                if 4 <= first and last - 4 < TILES:
                    rest(t - 4, (u - 4) % HU, 1, msg_mid, msg_r2)
                if 5 <= first and last - 5 < TILES:
                    make_onehot(e, q, t - 5, (u - 5) % 2)
                if LAG <= first:
                    add_tile(e, q, t - LAG, (u - LAG) % 2, where)

            def half_step(i, h):
                half = 2 * i + h
                at = None if isinstance(half, int) and half == 0 else load_blocks(e, q, half - 1, regs)
                for u in range(h * HU, (h + 1) * HU):
                    ends(i * U + u, u, i)
                    late(i * U + u, u, at and at[u % HU])

            half_step(0, 0)
            half_step(0, 1)
            with e.Fori(1, LOOPS) as i:
                half_step(i, 0)
                half_step(i, 1)
            at = load_blocks(e, q, HALVES - 1, regs)
            for u in range(LAG):
                late(TILES + u, TILES + u, at[u])

        def chunk_of(a, n):
            return a[:, ds(n * CE, CE)]

        def buf(k):
            return work[:, k * CE:(k + 1) * CE]

        def c3(a):
            return a.rearrange("p (c d) -> p c d", d=D)

        def per_node(a, n):
            return a[:, ds(n * CC, CC)].unsqueeze(2).to_broadcast([P, CC, D])

        def feat(a):
            return a.unsqueeze(1).to_broadcast([P, CC, D])

        IN0, IN1 = [buf(0), buf(1)], [buf(2), buf(3)]
        OUT0, OUT1, OUT2 = [buf(4), buf(5)], [buf(6), buf(7)], [buf(8), buf(9)]
        TMP0, TMP1, TMP2, TMP3 = buf(10), buf(11), buf(12), buf(13)
        HALF = CHUNKS // 2

        class Phase:
            def __init__(self, k, ins, outs, norm, prods, uses_acc=True):
                self.k, self.ins, self.outs, self.norm, self.prods, self.uses_acc = k, ins, outs, norm, prods, uses_acc
                self.c0 = k * CHUNKS

        def over_chunks(e, chunk):
            chunk(0, 0, 0)
            chunk(0, 1, 1)
            with e.Fori(1, HALF) as j:
                chunk(j, 0, 2 * j)
                chunk(j, 1, 2 * j + 1)

        totals = dict(ld=0, st=0, ln=0, acc=0, mi=0)

        def plan(ph):
            ph.ld0, ph.st0, ph.ln0, ph.acc0, ph.mi0 = (totals[x] for x in ("ld", "st", "ln", "acc", "mi"))
            totals["ld"] += 16 * len(ph.ins) * HALF
            totals["st"] += 16 * len(ph.outs) * HALF
            totals["ln"] += CHUNKS if ph.norm else 0
            totals["acc"] += CHUNKS if ph.uses_acc else 0
            totals["mi"] += CHUNKS if ph.prods else 0
            return ph

        def dense_sync(e, ph):
            bufs_in, bufs_out = [IN0, IN1], [OUT0, OUT1, OUT2]

            def load(n, h):
                wait_past(e, in_used, ph.c0 + n - 1 if not (isinstance(n, int) and n < 2) else 0)
                for a, t in zip(bufs_in, ph.ins):
                    e.dma_start(a[h], chunk_of(per_partition(t), n)).then_inc(loaded[h], 16)

            def store(n, h):
                e.wait_ge(out_ready, ph.c0 + n + 1)
                for a, t in zip(bufs_out, ph.outs):
                    e.dma_start(chunk_of(per_partition(t), n), a[h]).then_inc(stored[h], 16)

            load(0, 0)
            load(1, 1)
            store(0, 0)
            with e.Fori(1, HALF) as j:
                load(2 * j, 0)
                store(2 * j - 1, 1)
                load(2 * j + 1, 1)
                store(2 * j, 0)
            store(CHUNKS - 1, 1)
            for h in range(2):
                e.wait_ge(stored[h], ph.st0 + 16 * len(ph.outs) * HALF)

        def dense_gpsimd(e, ph):
            if not ph.uses_acc:
                return

            def chunk(j, h, n):
                e.wait_ge(acc_used, ph.acc0 + n + 1)
                e.tensor_copy(chunk_of(acc, n), zero[:, 0:1].to_broadcast([P, CE])).then_inc(cleared, 1)
            over_chunks(e, chunk)

        def dense_vector(e, ph, first_part, last_part):
            v = nc.vector
            count = [0]

            def chunk(j, h, n, before):
                count[0] = 0

                def link(ins):
                    count[0] += 1
                    ins.then_inc(n_dve, 1)
                    e.wait_ge(n_dve, before + count[0])

                e.wait_ge(loaded[h], ph.ld0 + 16 * len(ph.ins) * (j + 1))
                wait_past(e, stored[h], ph.st0 + 16 * len(ph.outs) * j)
                first_part(e, ph, v, h, n, link)
                last_part(e, ph, v, h, n, link)
                return count[0]

            base = dve_total[0]
            k = chunk(0, 0, 0, base)
            assert chunk(0, 1, 1, base + k) == k
            with e.Fori(1, HALF) as j:
                chunk(j, 0, 2 * j, base + 2 * j * k)
                chunk(j, 1, 2 * j + 1, base + 2 * j * k + k)
            dve_total[0] += k * CHUNKS

        dve_total = [0]
        mean, var, rstd = st[:, 0, :], st[:, 1, :], st[:, 2, :]
        root = st[:, 3, :]

        def bc(a):
            return a.unsqueeze(2).to_broadcast([P, CC, D])

        def normalise(e, ph, v, n, link, src, dst, cen):
            link(v.tensor_reduce(mean, c3(src), AX.X, ALU.add))
            link(v.tensor_scalar(mean, mean, 1.0 / D, None, ALU.mult))
            v.tensor_tensor(c3(cen), c3(src), bc(mean), ALU.subtract).then_inc(centered, 1)
            e.wait_ge(squared, ph.ln0 + n + 1)
            link(v.tensor_reduce(var, c3(TMP1), AX.X, ALU.add))
            v.tensor_scalar(var, var, 1.0 / D, EPS, ALU.mult, ALU.add).then_inc(var_ready, 1)
            e.wait_ge(root_ready, ph.ln0 + n + 1)
            link(v.reciprocal(rstd, root))
            link(v.scalar_tensor_tensor(c3(dst), c3(cen), 0.0, bc(rstd), ALU.max, ALU.mult))

        def norm_scalar(e, ph, n):
            e.wait_ge(centered, ph.ln0 + n + 1)
            e.activation(TMP1, TMP0, ACT.Square).then_inc(squared, 1)
            e.wait_ge(var_ready, ph.ln0 + n + 1)
            e.activation(root, var, ACT.Sqrt).then_inc(root_ready, 1)

        def nothing(*a):
            pass

        def p0_last(e, ph, v, h, n, link):
            x = IN0[h]
            normalise(e, ph, v, n, link, x, TMP2, TMP0)
            link(v.tensor_tensor(c3(OUT0[h]), c3(TMP2), per_node(dinv, n), ALU.mult))
            v.scalar_tensor_tensor(OUT1[h], TMP2, 1.0 / 3.0, x, ALU.mult, ALU.add).then_inc(out_ready, 1)
            e.wait_ge(out_ready, ph.c0 + n + 1)
            e.sem_inc(in_used, 1)

        def p1_last(e, ph, v, h, n, link):
            v.tensor_tensor(c3(TMP2), c3(chunk_of(acc, n)), per_node(dinv, n), ALU.mult).then_inc(acc_used, 1)
            e.wait_ge(acc_used, ph.acc0 + n + 1)
            link(v.tensor_tensor(c3(OUT0[h]), c3(TMP2), per_node(dinv, n), ALU.mult))
            v.scalar_tensor_tensor(OUT1[h], TMP2, 1.0 / 3.0, IN0[h], ALU.mult, ALU.add).then_inc(out_ready, 1)
            e.wait_ge(out_ready, ph.c0 + n + 1)
            e.sem_inc(in_used, 1)

        def p2_first(e, ph, v, h, n, link):
            v.tensor_tensor(c3(TMP2), c3(chunk_of(acc, n)), per_node(dinv, n), ALU.mult).then_inc(acc_used, 1)
            e.wait_ge(acc_used, ph.acc0 + n + 1)
            link(v.scalar_tensor_tensor(TMP2, TMP2, 1.0 / 3.0, IN0[h], ALU.mult, ALU.add))
            normalise(e, ph, v, n, link, TMP2, TMP3, TMP0)
            e.sem_inc(mm_in, 1)
            link(v.tensor_tensor(OUT0[h], TMP2, TMP3, ALU.add))
            e.sem_inc(in_used, 1)

        def p2_last(e, ph, v, h, n, link):
            e.wait_ge(prod3, n + 1)
            ac = PS[:, 2048:2048 + PAIRS * 256].rearrange("p (g s c) -> p g s c", s=2, c=P)
            v.tensor_tensor(OUT1[h].rearrange("p (g n d) -> p g n d", n=2, d=D),
                            ac[:, :, 0, :].rearrange("p g (n d) -> p g n d", d=D),
                            b_pi1.unsqueeze(1).unsqueeze(1).to_broadcast([P, PAIRS, 2, D]), ALU.add)
            link(v.tensor_copy(OUT2[h].rearrange("p (g c) -> p g c", c=P), ac[:, :, 1, :]))
            e.sem_inc(prod_out, 1)
            e.sem_inc(out_ready, 1)

        def turn_chunk(srcs, at):
            for k, s in enumerate(srcs):
                for g in range(PAIRS):
                    ins = nc.tensor.transpose(PS[:, at + 1024 * k + g * P:at + 1024 * k + (g + 1) * P],
                                              s[:, g * P:(g + 1) * P], ident)
            return ins

        def p2_tensor(e, ph):
            mm = nc.tensor.matmul

            def chunk(j, h, n):
                e.wait_ge(mm_in, ph.mi0 + n + 1)
                wait_past(e, turned_sb, n)
                turn_chunk([TMP3], 0).then_inc(turned, 1)
                e.wait_ge(turned_sb, n + 1)
                wait_past(e, prod_act, n)
                mm(PS[:, 1024:1536], W["pp"], OUTT[:, 0:512], start=True, stop=True)
                mm(PS[:, 1536:1024 + CE], W["pp"], OUTT[:, 512:CE], start=True, stop=True).then_inc(prod, 1)
                e.wait_ge(prod_act, n + 1)
                wait_past(e, prod_out, n)
                for g in range(PAIRS):
                    ins = mm(PS[:, 2048 + g * 256:2048 + (g + 1) * 256], P1T[:, g * P:(g + 1) * P],
                             w_sb[:, P:3 * P], start=True, stop=True)
                ins.then_inc(prod3, 1)
            over_chunks(e, chunk)

        OUTT, P1T = IN1[0], IN1[1]

        def p2_scalar(e, ph):
            def chunk(j, h, n):
                norm_scalar(e, ph, n)
                e.wait_ge(turned, n + 1)
                wait_past(e, prod, n)
                e.copy(OUTT, PS[:, 0:CE]).then_inc(turned_sb, 1)
                e.wait_ge(prod, n + 1)
                wait_past(e, prod3, n)
                e.activation(P1T, PS[:, 1024:1024 + CE], ACT.Tanh, bias=b_pp).then_inc(prod_act, 1)
            over_chunks(e, chunk)

        def p3_last(e, ph, v, h, n, link):
            v.tensor_tensor(OUT1[h], chunk_of(acc, n), IN0[h], ALU.add).then_inc(acc_used, 1)
            e.wait_ge(acc_used, ph.acc0 + n + 1)
            e.sem_inc(in_used, 1)
            normalise(e, ph, v, n, link, OUT1[h], OUT0[h], TMP0)
            e.sem_inc(out_ready, 1)

        def gin_first(ep):
            def part(e, ph, v, h, n, link):
                v.scalar_tensor_tensor(TMP3, IN0[h], ep, chunk_of(acc, n), ALU.mult, ALU.add).then_inc(mm_in, 1)
                e.wait_ge(mm_in, ph.mi0 + n + 1)
                e.sem_inc(acc_used, 1)
            return part

        def p4_last(e, ph, v, h, n, link):
            e.wait_ge(prod3, CHUNKS + n + 1)
            v.scalar_tensor_tensor(OUT1[h], PS[:, 3072:3072 + CE], 0.5, IN1[h], ALU.mult, ALU.add).then_inc(prod_out, 1)
            e.wait_ge(prod_out, CHUNKS + n + 1)
            e.sem_inc(in_used, 1)

        def p4_tensor(e, ph):
            mm = nc.tensor.matmul
            c0 = CHUNKS

            def chunk(j, h, n):
                e.wait_ge(mm_in, ph.mi0 + n + 1)
                wait_past(e, turned_sb, c0 + n)
                turn_chunk([TMP3], 0).then_inc(turned, 1)
                e.wait_ge(turned_sb, c0 + n + 1)
                wait_past(e, prod_act, c0 + n)
                mm(PS[:, 1024:1536], W["g0"], TMP0[:, 0:512], start=True, stop=True)
                mm(PS[:, 1536:1024 + CE], W["g0"], TMP0[:, 512:CE], start=True, stop=True)
                for g in range(PAIRS):
                    ins = mm(PS[:, 2048 + g * P:2048 + (g + 1) * P], TMP0[:, g * P:(g + 1) * P], W["g0"],
                             start=True, stop=True)
                ins.then_inc(prod, 1)
                e.wait_ge(prod_act, c0 + n + 1)
                wait_past(e, prod_out, c0 + n)
                for g in range(PAIRS):
                    ins = mm(PS[:, 3072 + g * P:3072 + (g + 1) * P], TMP1[:, g * P:(g + 1) * P], W["gm"],
                             start=True, stop=True)
                ins.then_inc(prod3, 1)
            over_chunks(e, chunk)

        def p4_scalar(e, ph):
            c0 = CHUNKS

            def chunk(j, h, n):
                e.wait_ge(turned, c0 + n + 1)
                wait_past(e, prod, c0 + n)
                e.copy(TMP0, PS[:, 0:CE]).then_inc(turned_sb, 1)
                e.wait_ge(prod, c0 + n + 1)
                wait_past(e, prod3, c0 + n)
                wait_past(e, stored[h], ph.st0 + 16 * len(ph.outs) * j)
                e.activation(TMP1, PS[:, 1024:1024 + CE], ACT.Relu)
                e.activation(OUT0[h], PS[:, 2048:2048 + CE], ACT.Relu).then_inc(prod_act, 1)
                e.wait_ge(prod_out, c0 + n + 1)
                e.wait_ge(prod_act, c0 + n + 1)
                e.sem_inc(out_ready, 1)
            over_chunks(e, chunk)

        def p5_last(e, ph, v, h, n, link):
            e.wait_ge(prod_act, 2 * CHUNKS + n + 1)
            v.tensor_tensor(OUT1[h], TMP2, IN1[h], ALU.add).then_inc(prod_out, 1)
            e.wait_ge(prod_out, 2 * CHUNKS + n + 1)
            e.sem_inc(in_used, 1)
            normalise(e, ph, v, n, link, OUT1[h], OUT0[h], TMP0)
            e.sem_inc(out_ready, 1)

        OTH = OUT2[0]

        def p5_tensor(e, ph):
            mm, c0 = nc.tensor.matmul, 2 * CHUNKS

            def chunk(j, h, n):
                e.wait_ge(mm_in, ph.mi0 + n + 1)
                wait_past(e, turned_sb, c0 + n)
                turn_chunk([TMP3], 0).then_inc(turned, 1)
                e.wait_ge(turned_sb, c0 + n + 1)
                wait_past(e, prod_act, c0 + n)
                for g in range(PAIRS):
                    ins = mm(PS[:, 1024 + g * P:1024 + (g + 1) * P], OTH[:, g * P:(g + 1) * P], W["g1"],
                             start=True, stop=True)
                ins.then_inc(prod, 1)
            over_chunks(e, chunk)

        def p5_scalar(e, ph):
            c0 = 2 * CHUNKS

            def chunk(j, h, n):
                e.wait_ge(turned, c0 + n + 1)
                wait_past(e, prod, c0 + n)
                e.copy(OTH, PS[:, 0:CE]).then_inc(turned_sb, 1)
                e.wait_ge(prod, c0 + n + 1)
                wait_past(e, prod_out, c0 + n)
                e.activation(TMP2, PS[:, 1024:1024 + CE], ACT.Relu, scale=0.5).then_inc(prod_act, 1)
                norm_scalar(e, ph, n)
            over_chunks(e, chunk)

        def sage_first(e, ph, v, h, n, link):
            v.tensor_tensor(c3(TMP3), c3(chunk_of(acc, n)), per_node(rdeg, n), ALU.mult).then_inc(mm_in, 1)
            e.wait_ge(mm_in, ph.mi0 + n + 1)
            e.sem_inc(acc_used, 1)

        def sage_tensor(wx, wa, c0):
            mm = nc.tensor.matmul

            def run(e, ph):
                def chunk(j, h, n):
                    e.wait_ge(mm_in, ph.mi0 + n + 1)
                    wait_past(e, turned_sb, c0 + n)
                    turn_chunk([IN0[h], TMP3], 0).then_inc(turned, 1)
                    e.wait_ge(turned_sb, c0 + n + 1)
                    wait_past(e, prod_out, c0 + n)
                    for g in range(PAIRS):
                        o_ = PS[:, 2048 + g * P:2048 + (g + 1) * P]
                        mm(o_, TMP0[:, g * P:(g + 1) * P], W[wx], start=True, stop=False)
                        ins = mm(o_, TMP1[:, g * P:(g + 1) * P], W[wa], start=False, stop=True)
                    ins.then_inc(prod, 1)
                over_chunks(e, chunk)
            return run

        def sage_scalar(c0, last):
            def run(e, ph):
                def chunk(j, h, n):
                    e.wait_ge(turned, c0 + n + 1)
                    wait_past(e, prod, c0 + n)
                    e.copy(TMP0, PS[:, 0:CE])
                    e.copy(TMP1, PS[:, 1024:1024 + CE]).then_inc(turned_sb, 1)
                    if not last:
                        e.wait_ge(prod_out, c0 + n + 1)
                        wait_past(e, stored[h], ph.st0 + 16 * len(ph.outs) * j)
                        e.activation(OUT0[h], TMP2, ACT.Relu).then_inc(out_ready, 1)
                over_chunks(e, chunk)
            return run

        def p6_last(e, ph, v, h, n, link):
            e.wait_ge(prod, 3 * CHUNKS + n + 1)
            wait_past(e, out_ready, ph.c0 + n)
            v.tensor_tensor(c3(TMP2), c3(PS[:, 2048:2048 + CE]), feat(b_s1), ALU.add).then_inc(prod_out, 1)
            e.wait_ge(prod_out, 3 * CHUNKS + n + 1)
            e.sem_inc(in_used, 1)

        def p7_last(e, ph, v, h, n, link):
            link(v.tensor_tensor(c3(TMP2), c3(IN1[h]), feat(b_s2), ALU.add))
            e.wait_ge(prod, 4 * CHUNKS + n + 1)
            v.tensor_tensor(OUT0[h], PS[:, 2048:2048 + CE], TMP2, ALU.add).then_inc(prod_out, 1)
            e.wait_ge(prod_out, 4 * CHUNKS + n + 1)
            e.sem_inc(in_used, 1)
            e.sem_inc(out_ready, 1)

        def norm_only_scalar(e, ph):
            over_chunks(e, lambda j, h, n: norm_scalar(e, ph, n))

        phases = [
            plan(Phase(0, [x_in], [t_g0, r_0], True, False, False)),
            plan(Phase(1, [r_0], [t_g1, r_1], False, False)),
            plan(Phase(2, [r_1], [r_2, t_a, t_c], True, True)),
            plan(Phase(3, [r_2], [t_h2, r_3], True, False)),
            plan(Phase(4, [t_h2, r_3], [t_h1, r_4], False, True)),
            plan(Phase(5, [t_h1, r_4], [t_h3, r_5], True, True)),
            plan(Phase(6, [t_h3], [t_h4], False, True)),
            plan(Phase(7, [t_h4, r_5], [out], False, True)),
        ]
        vector_parts = [(nothing, p0_last), (nothing, p1_last), (p2_first, p2_last), (nothing, p3_last),
                        (gin_first(ep0), p4_last), (gin_first(ep1), p5_last), (sage_first, p6_last),
                        (sage_first, p7_last)]
        scalar_parts = [norm_only_scalar, nothing, p2_scalar, norm_only_scalar, p4_scalar, p5_scalar,
                        sage_scalar(3 * CHUNKS, False), sage_scalar(4 * CHUNKS, True)]
        tensor_parts = [nothing, nothing, p2_tensor, nothing, p4_tensor, p5_tensor,
                        sage_tensor("s1x", "s1a", 3 * CHUNKS), sage_tensor("s2x", "s2a", 4 * CHUNKS)]

        S, DD = (idx_s, key_s, 0), (idx_d, key_d, 1)
        passes = {
            0: [Pass(t_g0, *S, 0, 0), Pass(t_g0, *DD, 1, 1)],
            1: [Pass(t_g1, *S, 2, 2), Pass(t_g1, *DD, 3, 3)],
            2: [Pass(t_c, *S, 4, 4, t_a)],
            3: [Pass(t_h2, *DD, 5, 4)],
            4: [Pass(t_h1, *DD, 6, 5)],
            5: [Pass(t_h3, *S, 7, 6)],
            6: [Pass(t_h4, *S, 8, 7)],
            7: [],
        }

        @block.sync
        def _(e):
            prep_sync(e)
            prep_sync_end(e)
            end_phase(e, "sync")
            for k, ph in enumerate(phases):
                dense_sync(e, ph)
                end_phase(e, "sync")
                end_phase(e, "sync")

        @block.gpsimd
        def _(e):
            prep_gpsimd(e)
            end_phase(e, "pool")
            for k, ph in enumerate(phases):
                dense_gpsimd(e, ph)
                end_phase(e, "pool")
                for q in passes[k]:
                    pass_gpsimd(e, q)
                end_phase(e, "pool")

        @block.scalar
        def _(e):
            prep_scalar(e)
            end_phase(e, "act")
            for k, ph in enumerate(phases):
                scalar_parts[k](e, ph)
                end_phase(e, "act")
                for q in passes[k]:
                    (edge_scalar if q.table2 is not None else pass_scalar)(e, q)
                end_phase(e, "act")

        @block.tensor
        def _(e):
            prep_tensor(e)
            end_phase(e, "pe")
            for k, ph in enumerate(phases):
                tensor_parts[k](e, ph)
                end_phase(e, "pe")
                for q in passes[k]:
                    (edge_tensor if q.table2 is not None else pass_tensor)(e, q)
                end_phase(e, "pe")

        @block.vector
        def _(e):
            regs = [e.alloc_register(f"block_at_{u}") for u in range(8)]
            prep_vector(e)
            end_phase(e, "dve")
            for k, ph in enumerate(phases):
                dense_vector(e, ph, *vector_parts[k])
                end_phase(e, "dve")
                for q in passes[k]:
                    (edge_vector if q.table2 is not None else pass_vector)(e, q, regs)
                end_phase(e, "dve")


def kernel(**inputs):
    import numpy as np
    import concourse.bacc as bacc
    from concourse.bass_utils import run_bass_kernel_spmd

    a = {k: np.asarray(v) for k, v in inputs.items()}
    f = np.float32

    def pair(w):
        o = np.zeros((P, P), f)
        o[0:D, 0:D] = w
        o[D:, D:] = w
        return o

    def rows(v):
        return np.tile(v[None, :], (P, 1))

    x = np.zeros((NPAD, D), f)
    x[:NODES] = a["x"]

    def edge_list(v):
        o = np.full(EPAD, NPAD - 1, np.int32)
        o[:EDGES] = v
        return o.reshape(P, ETILES)

    attr = np.zeros((EPAD, BASIS), f)
    attr[:EDGES] = a["edge_attr_8"]
    k, m = np.meshgrid(np.arange(P), np.arange(P), indexing="ij")
    consts32 = np.zeros((P, CONST_COLS), f)
    consts32[:, 0:P] = k == m
    consts32[:BLOCKS, P:P + BLOCKS] = (k <= m)[:BLOCKS, :BLOCKS]
    consts32[:BLOCKS, P + BLOCKS:] = (k < m)[:BLOCKS, :BLOCKS]
    consts16 = np.concatenate([np.tile(np.arange(512), (P, 1)), k < m, np.ones((P, P))], 1).astype(np.float16)
    w1, s1, s2 = a["L1_gnn_pi_W1"], a["L3_gnn_W1"], a["L3_gnn_W2"]
    blocks = {"pp": a["L1_gnn_pp_W"], "w1a": w1[:D], "w1b": w1[D:], "g0": a["L2_gnn_W0"].T,
              "gm": a["L2_gnn_Wm"].T, "g1": a["L2_gnn_W1"].T, "s1x": s1[:D], "s1a": s1[D:],
              "s2x": s2[:D], "s2a": s2[D:]}
    vectors = np.concatenate(
        [rows(a["L1_gnn_pi_b1"]), rows(a["L1_gnn_ii_b"]), rows(a["L3_gnn_b1"]), rows(a["L3_gnn_b2"]),
         np.tile(a["L1_gnn_pp_b"], 2)[:, None], np.tile(a["L2_gnn_eps0"].reshape(1, 1), (P, 1)),
         np.tile(a["L2_gnn_eps1"].reshape(1, 1), (P, 1)), np.zeros((P, 1), f)], 1)
    arrays = {
        "x": x, "src": edge_list(a["src"]), "dst": edge_list(a["dst"]),
        "attr": attr.reshape(P, ETILES * BASIS), "consts32": consts32, "consts16": consts16,
        "weights": np.concatenate([pair(blocks[n]) for n in W_NAMES], 1),
        "w2t": a["L1_gnn_pi_W2"].reshape(D, D, BASIS).transpose(1, 2, 0).reshape(D, BASIS * D),
        "iiw": a["L1_gnn_ii_W"], "vectors": vectors,
    }
    nc = bacc.Bacc("TRN2", target_bir_lowering=False, num_devices=1)
    arrays = {f"in_{n}": np.ascontiguousarray(v) for n, v in arrays.items()}
    args = [nc.dram_tensor(n, v.shape, mybir.dt.from_np(v.dtype), kind="ExternalInput").ap()
            for n, v in arrays.items()]
    args.append(nc.dram_tensor("out", (NPAD, D), mybir.dt.float32, kind="ExternalOutput").ap())
    build_program(nc, *args)
    r = run_bass_kernel_spmd(nc, [arrays], core_ids=[0])
    return r.results[0]["out"][:NODES]
```

```python
import concourse.bass as bass
from concourse import mybir
from contextlib import ExitStack

P = 128
NODES = 50000
EDGES = 50000
D = 64
COLS = 392
NPAD = P * COLS
BCOLS = 4
BLOCKS = COLS // BCOLS
BW = BCOLS * P
ETILES = 392
EPAD = P * ETILES
TILES = ETILES + BLOCKS
SLOTS = P * TILES
BASIS = 8
FS = 3 + BASIS
FD = 2
U = 14
HU = U // 2
CC = 8
CHUNKS = COLS // CC
CE = CC * D
PAIRS = CC // 2
G4 = 4
GROUPS = ETILES // G4
EPS = 1e-5

CONST_COLS = 128 + 2 * 98
W_NAMES = ["pp", "w1a", "w1b", "g0", "g1", "gm", "s1a", "s1x", "s2a", "s2x"]


def build_program(nc, x_in, src_in, dst_in, attr_in, consts32, consts16, weights, w2t, iiw,
                  vectors, out):
    f32, i32 = mybir.dt.float32, mybir.dt.int32
    f16, bf16 = mybir.dt.float16, mybir.dt.bfloat16
    ALU, ACT, AX = mybir.AluOpType, mybir.ActivationFunctionType, mybir.AxisListType
    ds = bass.ds

    def dram(name, shape):
        return nc.dram_tensor(name, shape, f32, kind="Internal").ap()

    tab_s, tab_d = dram("tab_s", [SLOTS, FS]), dram("tab_d", [SLOTS, FD])
    t_g0, t_g1, t_a, t_c, t_y0, t_y1, t_s1, t_s2 = (
        dram(n, [NPAD, D]) for n in ("t_g0", "t_g1", "t_a", "t_c", "t_y0", "t_y1", "t_s1", "t_s2"))
    r_0, r_1, r_2, r_3, r_4, r_5, r_6, r_s1 = (
        dram(n, [NPAD, D]) for n in ("r_0", "r_1", "r_2", "r_3", "r_4", "r_5", "r_6", "r_s1"))

    def per_partition(t):
        return t.rearrange("(p c) d -> p (c d)", p=P)

    with ExitStack() as ctx:
        def sb(name, shape, dt=f32):
            return ctx.enter_context(nc.sbuf_tensor(name, shape, dt))

        def sem(name):
            return ctx.enter_context(nc.semaphore(name))

        acc = sb("acc", [P, COLS * D])
        work = sb("work", [P, 19 * CE])
        iota16 = sb("iota16", [P, 512], f16)
        mats16 = sb("mats16", [P, 2 * P], f16)
        ident16 = sb("ident16", [P, P], bf16)
        c32 = sb("c32", [P, CONST_COLS])
        w_sb = sb("w_sb", [P, len(W_NAMES) * P])
        small64 = sb("small64", [D, D + BASIS * P])
        vmix = sb("vmix", [P, 3, BASIS * D], bf16)
        vecs = sb("vecs", [P, 4 * D + 4])
        key_s, key_d = sb("key_s", [P, TILES]), sb("key_d", [P, TILES])
        idx_s, idx_d = sb("idx_s", [P, TILES], i32), sb("idx_d", [P, TILES], i32)
        own_s = sb("own_s", [P, TILES], i32)
        basis = sb("basis", [P, TILES, BASIS])
        block_at = sb("block_at", [1, 2, TILES // HU * 8], i32)
        dinv, rdeg = sb("dinv", [P, COLS]), sb("rdeg", [P, COLS])
        consts = sb("consts", [P, 2])
        zero, eps_sb = consts[:, 0:1], consts[:, 1:2]
        st = sb("st", [P, 4, CC])

        PS = ctx.enter_context(nc.psum_tensor("PS", [P, 4096], f32))
        ident = c32[:, 0:P]
        pre_inc, pre_exc = c32[0:BLOCKS, P:P + 98], c32[0:BLOCKS, P + 98:P + 196]
        lower16, ones16 = mats16[:, 0:P], mats16[:, P:2 * P]
        W = {n: w_sb[:, i * P:(i + 1) * P] for i, n in enumerate(W_NAMES)}
        b_pi1, b_ii, b_s1, b_s2 = (vecs[:, i * D:(i + 1) * D] for i in range(4))
        b_pp, ep0, ep1 = (vecs[:, 4 * D + i:4 * D + i + 1] for i in range(3))

        phase_end = sem("phase_end")
        const_in, edges_in, filled = sem("const_in"), sem("edges_in"), sem("filled")
        dve_step = sem("dve_step")
        ends_known = sem("ends_known")
        deg_diff, deg_sq, deg_row, deg_oh, deg_mm = (
            sem(n) for n in ("deg_diff", "deg_sq", "deg_row", "deg_oh", "deg_mm"))
        pe_prep, dve_prep, act_prep = sem("pe_prep"), sem("dve_prep"), sem("act_prep")
        rk_oh, rk_mm, rk_row, rk_pay, rk_cum, rk_dve = (
            sem(n) for n in ("rk_oh", "rk_mm", "rk_row", "rk_pay", "rk_cum", "rk_dve"))
        sent = [sem(f"sent{c}") for c in range(2)]
        issuing = sem("issuing")
        tab_in = sem("tab_in")
        staged = sem("staged")
        got = [sem(f"got{h}") for h in range(2)]
        got_ends = [sem(f"got_ends{h}") for h in range(2)]
        part_hi, part_r1, part_mid, part_r2, parts_ready = (
            sem(n) for n in ("part_hi", "part_r1", "part_mid", "part_r2", "parts_ready"))
        h_sum, h_hi, h_r1, h_mid, h_r2, h_parts = (
            sem(n) for n in ("h_sum", "h_hi", "h_r1", "h_mid", "h_r2", "h_parts"))
        m_high, m_hi, m_r1, m_mid, m_r2, m_parts = (
            sem(n) for n in ("m_high", "m_hi", "m_r1", "m_mid", "m_r2", "m_parts"))
        onehot_ready, sum_ready, added = sem("onehot_ready"), sem("sum_ready"), sem("added")
        ht_mm, ht_ready, z_mm, z_used, za_used, pre_ready = (
            sem(n) for n in ("ht_mm", "ht_ready", "z_mm", "z_used", "za_used", "pre_ready"))
        in1_loaded, in2_loaded, stored1, stored2 = (
            [sem(f"{n}_{h}") for h in range(2)] for n in ("in1_loaded", "in2_loaded", "stored1", "stored2"))
        v1_step, v1_done, v2_done, e_done = (sem(n) for n in ("v1_step", "v1_done", "v2_done", "e_done"))
        acc_used, cleared = sem("acc_used"), sem("cleared")
        centered, squared, var_ready, root_ready = (
            sem(n) for n in ("centered", "squared", "var_ready", "root_ready"))
        x_ready, turned, turned_sb, multiplied = (sem(n) for n in ("x_ready", "turned", "turned_sb", "multiplied"))
        pp_done, p1_ready = sem("pp_done"), sem("p1_ready")

        block = ctx.enter_context(nc.Block())
        phase_no = {}

        def end_phase(e, name):
            phase_no[name] = phase_no.get(name, 0) + 1
            e.drain().then_inc(phase_end, 1)
            e.wait_ge(phase_end, 5 * phase_no[name])

        def wait_past(e, s, v):
            if isinstance(v, int) and v <= 0:
                return
            e.wait_ge(s, v)

        o = 0

        def scratch(n):
            nonlocal o
            o += n
            return acc[:, o - n:o]

        E2 = 2 * ETILES
        ed_i = scratch(E2).bitcast(i32)
        ti = scratch(E2).bitcast(i32)
        nf, q_p, r_m, q_b, rem_b, t1 = (scratch(E2) for _ in range(6))
        attr = scratch(ETILES * BASIS)
        pay_s, pay_d = scratch(ETILES * FS), scratch(ETILES * FD)
        deg = scratch(2 * COLS)
        degb = scratch(2 * BLOCKS)
        fill = acc[:, o:o + SLOTS * FS // P]
        tabs_sb = acc[:, o:o + TILES * FS]
        tabd_sb = acc[:, o + TILES * FS:o + TILES * (FS + FD)]
        spare = {"early": [2 * CE, 6 * CE], "late": [10 * CE, 16 * CE]}

        def wscratch(n, dt=f32, part="late"):
            words = n // 2 if dt in (f16, bf16) else n
            at, end = spare[part]
            assert at + words <= end
            spare[part][0] += words
            a = work[:, at:at + words]
            return a if dt == f32 else a.bitcast(dt)

        oh_p = [wscratch(4 * P, bf16, "early") for _ in range(2)]
        oh_m = [[wscratch(COLS, bf16, "early") for _ in range(2)] for _ in range(2)]
        GB = G4 * BLOCKS
        oh_b = [wscratch(2 * GB, f16) for _ in range(2)]
        cum, base16, row128 = wscratch(2 * BLOCKS, f16), wscratch(2 * BLOCKS, f16), wscratch(P, f16)
        pick, csum, posf = wscratch(2 * GB), wscratch(2 * BLOCKS), wscratch(2 * G4)
        diff = [pick[:, w * 2 * P:(w + 1) * 2 * P].bitcast(bf16) for w in range(2)]
        sq = [oh_b[w][:, 0:4 * P].bitcast(bf16) for w in range(2)]
        pos_i, pos_lo, pos_hi = (wscratch(2 * G4, i32) for _ in range(3))
        row_i = [wscratch(2 * G4, i32) for _ in range(2)]
        pring = [[wscratch(G4 * f) for _ in range(2)] for f in (FS, FD)]
        tl = wscratch(2)
        tl_i = wscratch(2, i32)
        tl_w = wscratch(2 * P, part="early")
        end_t = wscratch(2)
        cmp16 = wscratch(2 * TILES, f16, "early")
        ones32 = wscratch(1)
        pays, pay_n, tabs = [pay_s, pay_d], [FS, FD], [tab_s, tab_d]

        DU = 8

        def prep_sync(e):
            for dst_, src_ in ((iota16[:, :], consts16[:, 0:512]), (mats16[:, :], consts16[:, 512:768]),
                               (c32[:, :], consts32), (w_sb[:, :], weights), (small64[:, 0:D], iiw),
                               (small64[:, D:], w2t), (vecs[:, :], vectors)):
                e.dma_start(dst_, src_).then_inc(const_in, 16)
            e.dma_start(ed_i[:, 0:ETILES], src_in).then_inc(edges_in, 16)
            e.dma_start(ed_i[:, ETILES:], dst_in).then_inc(edges_in, 16)
            e.dma_start(attr, attr_in).then_inc(edges_in, 16)
            e.wait_ge(dve_prep, 1)
            e.dma_start(tab_s.rearrange("(p a) f -> p (a f)", p=P), fill).then_inc(filled, 16)
            e.dma_start(tab_d.rearrange("(p a) f -> p (a f)", p=P), fill[:, 0:SLOTS * FD // P]).then_inc(filled, 16)

        def prep_vector(e):
            steps = [0]

            def step(ins):
                steps[0] += 1
                ins.then_inc(dve_step, 1)
                e.wait_ge(dve_step, steps[0])

            v = nc.vector
            v.memset(zero, 0.0)
            v.memset(eps_sb, D * D * EPS)
            v.memset(block_at[:, :, :], 0)
            v.memset(fill, -1.0).then_inc(dve_prep, 1)
            v.memset(ones32, 1.0)
            v.memset(row128[0:1, :], 128.0)
            v.memset(cum, 0.0)
            e.wait_ge(const_in, 16 * 7)
            v.tensor_copy(ident16[:, :], ident)
            step(v.tensor_scalar(vecs[:, 4 * D + 1:4 * D + 3], vecs[:, 4 * D + 1:4 * D + 3], 1.0, None, ALU.add))
            e.wait_ge(edges_in, 48)
            step(v.tensor_copy(nf, ed_i))

            def divmod_(a, n, q, r):
                step(v.tensor_scalar(t1, a, 1.0 / n, None, ALU.mult))
                step(v.tensor_copy(ti, t1))
                step(v.tensor_copy(q, ti))
                step(v.scalar_tensor_tensor(r, q, -float(n), a, ALU.mult, ALU.add))
                for op, bound, sign in ((ALU.is_lt, 0.0, -1.0), (ALU.is_ge, float(n), 1.0)):
                    step(v.tensor_scalar(t1, r, bound, sign, op, ALU.mult))
                    step(v.tensor_tensor(q, q, t1, ALU.add))
                    step(v.scalar_tensor_tensor(r, t1, -float(n), r, ALU.mult, ALU.add))

            divmod_(nf, COLS, q_p, r_m)
            divmod_(r_m, BCOLS, q_b, rem_b)
            step(v.scalar_tensor_tensor(t1, rem_b, float(P), q_p, ALU.mult, ALU.add))
            ps3 = pay_s.rearrange("p (t f) -> p t f", f=FS)
            pd3 = pay_d.rearrange("p (t f) -> p t f", f=FD)
            v.tensor_copy(ps3[:, :, 0], nf[:, ETILES:])
            v.tensor_copy(ps3[:, :, 1], t1[:, 0:ETILES])
            v.tensor_copy(ps3[:, :, 2], nf[:, 0:ETILES])
            v.tensor_copy(ps3[:, :, 3:], attr.rearrange("p (t f) -> p t f", f=BASIS))
            v.tensor_copy(pd3[:, :, 0], nf[:, 0:ETILES])
            step(v.tensor_copy(pd3[:, :, 1], t1[:, ETILES:]))

            e.sem_inc(ends_known, 1)
            def degree_tile(t, h):
                for s in range(2):
                    wait_past(e, deg_mm, 2 * (t - 2) + s + 1)
                    v.tensor_scalar(oh_m[h][s], iota16[:, 0:COLS], r_m[:, ds(t + s * ETILES, 1)], None,
                                    ALU.is_equal).then_inc(deg_oh, 1)

            for t in range(DU):
                degree_tile(t, t % 2)
            with e.Fori(1, ETILES // DU) as j:
                for u in range(DU):
                    degree_tile(DU * j + u, u % 2)
            e.wait_ge(deg_mm, 2 * ETILES)
            for s in range(2):
                step(v.tensor_copy(deg[:, s * COLS:(s + 1) * COLS], PS[:, s * 512:s * 512 + COLS]))
            v.tensor_reduce(degb, deg.rearrange("p (b c) -> p b c", c=BCOLS), AX.X, ALU.add).then_inc(dve_prep, 1)
            e.wait_ge(pe_prep, 1)
            step(v.tensor_scalar(tl_i[0:BLOCKS, :], PS[0:BLOCKS, 1024:1026], float(P - 1), None, ALU.add))
            step(v.tensor_scalar(tl_i[0:BLOCKS, :], tl_i[0:BLOCKS, :], 7, None, ALU.logical_shift_right))
            step(v.tensor_copy(tl[0:BLOCKS, :], tl_i[0:BLOCKS, :]))
            v.tensor_copy(tl_w[0:BLOCKS, :].rearrange("b (s p) -> b s p", s=2),
                          tl[0:BLOCKS, :].unsqueeze(2).to_broadcast([BLOCKS, 2, P])).then_inc(dve_prep, 1)
            e.wait_ge(pe_prep, 2)
            step(v.tensor_copy(end_t[0:BLOCKS, :], PS[0:BLOCKS, 1536:1538]))
            v.tensor_copy(base16[0:1, :], PS[0:1, 2048:2048 + 2 * BLOCKS])
            for s in range(2):
                ins = v.tensor_scalar(cmp16[0:BLOCKS, s * TILES:(s + 1) * TILES], iota16[0:BLOCKS, 0:TILES],
                                      end_t[0:BLOCKS, s:s + 1], None, ALU.is_ge)
            ins.then_inc(dve_prep, 1)
            e.wait_ge(pe_prep, 3)
            for s in range(2):
                ins = v.tensor_scalar(block_at[0:1, s, :].rearrange("p (k u) -> p k u", u=8)[:, :, 0:HU],
                                      PS[0:1, 2560 + 512 * s:2560 + 512 * s + TILES].rearrange("p (k u) -> p k u", u=HU),
                                      float(BLOCKS - 1), float(BCOLS * D), ALU.min, ALU.mult)
            step(ins)
            step(v.tensor_tensor(t1[:, 0:COLS], deg[:, 0:COLS], deg[:, COLS:], ALU.add))
            v.tensor_scalar(t1[:, COLS:], t1[:, 0:COLS], 1.0, None, ALU.max).then_inc(dve_prep, 1)
            e.wait_ge(act_prep, 1)
            step(v.reciprocal(dinv[:, :], nf[:, 0:COLS]))
            step(v.tensor_scalar(t1[:, 0:COLS], t1[:, 0:COLS], 1.0, None, ALU.is_ge))
            step(v.tensor_tensor(dinv[:, :], dinv[:, :], t1[:, 0:COLS], ALU.mult))
            step(v.tensor_scalar(rdeg[:, :], deg[:, 0:COLS], 1.0, None, ALU.max))
            step(v.reciprocal(rdeg[:, :], rdeg[:, :]))
            e.wait_ge(pe_prep, 4)
            vm = t1[:, 0:BASIS * D]
            step(v.tensor_copy(vm, PS[:, 3584:4096]))
            step(v.tensor_copy(vmix[:, 0, :], vm))
            step(v.tensor_tensor(vm, vm, vmix[:, 0, :], ALU.subtract))
            step(v.tensor_copy(vmix[:, 1, :], vm))
            step(v.tensor_tensor(vm, vm, vmix[:, 1, :], ALU.subtract))
            v.tensor_copy(vmix[0:D, 2, :], vm[0:D, :])
            step(v.tensor_copy(vmix[D:, 2, :], vmix[D:, 0, :]))

            n = [0]

            def link(ins, before):
                n[0] += 1
                ins.then_inc(rk_dve, 1)
                e.wait_ge(rk_dve, before + n[0])

            q_b3 = q_b.rearrange("p (s t) -> p s t", s=2)

            def block_onehot(g, c):
                v.tensor_tensor(oh_b[c].rearrange("p (s u b) -> p s u b", s=2, u=G4),
                                iota16[:, 0:BLOCKS].unsqueeze(1).unsqueeze(1).to_broadcast([P, 2, G4, BLOCKS]),
                                q_b3[:, :, ds(g * G4, G4)].unsqueeze(3).to_broadcast([P, 2, G4, BLOCKS]),
                                ALU.is_equal).then_inc(rk_oh, 1)

            def group(m, c, before):
                g = 2 * m + c
                n[0] = 0
                if not (isinstance(g, int) and g + 1 == GROUPS):
                    block_onehot(g + 1, 1 - c)
                e.wait_ge(rk_oh, g + 1)
                link(v.tensor_reduce(csum.rearrange("p (s b) -> p s b", s=2),
                                     oh_b[c].rearrange("p (s u b) -> p s b u", s=2, u=G4), AX.X, ALU.add), before)
                e.wait_ge(rk_mm, g + 1)
                v.tensor_tensor(cum, cum, csum, ALU.add).then_inc(rk_cum, 1)
                link(v.tensor_tensor(pick.rearrange("p (s k) -> p s k", s=2),
                                     PS[:, 1024 * c:1024 * (c + 1)].rearrange("p (s k) -> p s k", s=2)[:, :, 0:GB],
                                     oh_b[c].rearrange("p (s k) -> p s k", s=2), ALU.mult), before)
                link(v.tensor_reduce(posf, pick.rearrange("p (k b) -> p k b", b=BLOCKS), AX.X, ALU.add), before)
                link(v.tensor_copy(pos_i, posf), before)
                v.tensor_scalar(pos_lo, pos_i, P - 1, None, ALU.bitwise_and)
                link(v.tensor_scalar(pos_hi, pos_i, 7, None, ALU.logical_shift_right), before)
                wait_past(e, sent[c], 16 * 2 * G4 * m)
                v.scalar_tensor_tensor(row_i[c], pos_lo, float(TILES), pos_hi, ALU.mult,
                                       ALU.add).then_inc(rk_row, 1)
                return n[0]

            block_onehot(0, 0)
            per_group = []

            def two_groups(m):
                for c in range(2):
                    k = per_group[0] if per_group else 0
                    per_group.append(group(m, c, (2 * m + c) * k))

            dense_vector(e, phases[0], *vector_parts[0], beside=two_groups)
            assert len(set(per_group)) == 1
            e.wait_ge(tab_in, 32)
            s3 = tabs_sb.rearrange("p (t f) -> p t f", f=FS)
            d3 = tabd_sb.rearrange("p (t f) -> p t f", f=FD)
            v.tensor_scalar(idx_s[:, :], s3[:, :, 0], 0.0, None, ALU.max)
            v.tensor_copy(key_s[:, :], s3[:, :, 1])
            v.tensor_scalar(own_s[:, :], s3[:, :, 2], 0.0, None, ALU.max)
            v.tensor_copy(basis[:, :, :], s3[:, :, 3:])
            v.tensor_scalar(idx_d[:, :], d3[:, :, 0], 0.0, None, ALU.max)
            step(v.tensor_copy(key_d[:, :], d3[:, :, 1]))
            step(v.memset(acc[:, :], 0.0))

        def prep_scalar(e):
            e.wait_ge(ends_known, 1)

            def square(k, w):
                e.wait_ge(deg_diff, k + 1)
                wait_past(e, deg_row, k - 1)
                e.activation(sq[w], diff[w], ACT.Square).then_inc(deg_sq, 1)

            def onehot_rows(k, w):
                e.wait_ge(deg_sq, k + 1)
                wait_past(e, deg_mm, 4 * (k - 1))
                e.activation(oh_p[w], sq[w], ACT.Relu, scale=-1.0, bias=ones32).then_inc(deg_row, 1)

            def pair(k, u):
                square(k, u % 2)
                if not (isinstance(k, int) and k == 0):
                    onehot_rows(k - 1, 1 - u % 2)

            for u in range(DU // 2):
                pair(u, u)
            with e.Fori(1, ETILES // DU) as j:
                for u in range(DU // 2):
                    pair(DU // 2 * j + u, u)
            onehot_rows(ETILES // 2 - 1, 1)
            e.wait_ge(dve_prep, 5)
            e.activation(nf[:, 0:COLS], t1[:, COLS:], ACT.Sqrt).then_inc(act_prep, 1)

            def two_groups(m):
                for c in range(2):
                    wait_past(e, sent[c], 16 * 2 * G4 * m)
                    for s in range(2):
                        n = G4 * pay_n[s]
                        e.copy(pring[s][c], pays[s][:, ds((2 * m + c) * n, n)]).then_inc(rk_pay, 1)

            dense_scalar(e, phases[0], None, beside=two_groups)

        def prep_tensor(e):
            mm = nc.tensor.matmul

            def degree_tile(t0, u, start=False, stop=False):
                k, w = t0 * (DU // 2) + u // 2, u // 2 % 2
                e.wait_ge(deg_row, k + 1)
                t = t0 * DU + u
                for s in range(2):
                    e.wait_ge(deg_oh, 2 * t + s + 1)
                    at = (2 * s + u % 2) * P
                    mm(PS[:, s * 512:s * 512 + COLS], oh_p[w][:, at:at + P], oh_m[u % 2][s],
                       start=start, stop=stop, skip_group_check=True).then_inc(deg_mm, 1)

            for u in range(DU):
                degree_tile(0, u, start=(u == 0))
            with e.Fori(1, ETILES // DU - 1) as j:
                for u in range(DU):
                    degree_tile(j, u)
            for u in range(DU):
                degree_tile(ETILES // DU - 1, u, stop=(u == DU - 1))
            e.wait_ge(dve_prep, 2)
            for s in range(2):
                ins = mm(PS[0:BLOCKS, 1024 + s:1025 + s], degb[:, s * BLOCKS:(s + 1) * BLOCKS], ones32,
                         start=True, stop=True)
            ins.then_inc(pe_prep, 1)
            e.wait_ge(dve_prep, 3)
            for s in range(2):
                mm(PS[0:BLOCKS, 1536 + s:1537 + s], pre_inc, tl[0:BLOCKS, s:s + 1], start=True, stop=True)
                ins = mm(PS[:, 2048 + s * BLOCKS:2048 + (s + 1) * BLOCKS], tl_w[0:BLOCKS, s * P:(s + 1) * P],
                         pre_exc, start=True, stop=True)
            ins.then_inc(pe_prep, 1)
            e.wait_ge(dve_prep, 4)
            for s in range(2):
                ins = mm(PS[:, 2560 + 512 * s:2560 + 512 * s + TILES], ones16[0:BLOCKS, :],
                         cmp16[0:BLOCKS, s * TILES:(s + 1) * TILES], start=True, stop=True)
            ins.then_inc(pe_prep, 1)
            for b in range(BASIS):
                ins = mm(PS[:, 3584 + b * D:3584 + (b + 1) * D], small64[:, D + b * P:D + (b + 1) * P],
                         small64[:, 0:D], start=True, stop=True)
            ins.then_inc(pe_prep, 1)

            def group(g, c):
                e.wait_ge(rk_oh, g + 1)
                wait_past(e, rk_cum, g)
                for s in range(2):
                    ps = PS[:, 1024 * c + 512 * s:1024 * c + 512 * s + GB]
                    ps3 = ps.rearrange("p (u b) -> p u b", u=G4)
                    oh = oh_b[c][:, s * GB:(s + 1) * GB]

                    def every(a):
                        return a[:, s * BLOCKS:(s + 1) * BLOCKS].unsqueeze(1).to_broadcast([a.shape[0], G4, BLOCKS])

                    mm(ps, lower16, oh, start=True, stop=False, skip_group_check=True)
                    mm(ps3, ones16, every(cum), start=False, stop=False, skip_group_check=True)
                    for u in range(G4 - 1):
                        mm(ps3[:, u + 1:, :], ones16,
                           oh[:, u * BLOCKS:(u + 1) * BLOCKS].unsqueeze(1).to_broadcast([P, G4 - 1 - u, BLOCKS]),
                           start=False, stop=False, skip_group_check=True)
                    ins = mm(ps3, row128[0:1, :], every(base16[0:1, :]), start=False, stop=True, skip_group_check=True)
                ins.then_inc(rk_mm, 1)

            group(0, 0)
            group(1, 1)
            with e.Fori(1, GROUPS // 2) as m:
                group(2 * m, 0)
                group(2 * m + 1, 1)

        def prep_gpsimd(e):
            e.wait_ge(const_in, 16 * 7)
            e.wait_ge(ends_known, 1)

            def distances(k, w):
                wait_past(e, deg_sq, k - 1)
                e.tensor_tensor(diff[w].rearrange("p (s u k) -> p s u k", s=2, u=2),
                                iota16[:, 0:P].unsqueeze(1).unsqueeze(1).to_broadcast([P, 2, 2, P]),
                                q_p.rearrange("p (s t) -> p s t", s=2)[:, :, ds(2 * k, 2)].unsqueeze(3).to_broadcast(
                                    [P, 2, 2, P]), ALU.subtract).then_inc(deg_diff, 1)

            for u in range(DU // 2):
                distances(u, u % 2)
            with e.Fori(1, ETILES // DU) as j:
                for u in range(DU // 2):
                    distances(DU // 2 * j + u, u % 2)
            e.wait_ge(filled, 32)

            def two_groups(m):
                for c in range(2):
                    e.wait_ge(rk_row, 2 * m + c + 1)
                    e.wait_ge(rk_pay, 2 * (2 * m + c + 1))
                    e.sem_inc(issuing, 1)
                    for s in range(2):
                        for u in range(G4):
                            e.indirect_dma_start(
                                out=tabs[s], out_offset=bass.IndirectOffsetOnAxis(ap=row_i[c][:, s * G4 + u:s * G4 + u + 1], axis=0),
                                in_=pring[s][c][:, u * pay_n[s]:(u + 1) * pay_n[s]], in_offset=None,
                            ).then_inc(sent[c], 16)

            two_groups(0)
            with e.Fori(1, GROUPS // 2) as m:
                two_groups(m)

        def prep_sync_end(e):
            for c in range(2):
                e.wait_ge(sent[c], 16 * G4 * GROUPS)
            e.dma_start(tabs_sb, tab_s.rearrange("(p a) f -> p (a f)", p=P)).then_inc(tab_in, 16)
            e.dma_start(tabd_sb, tab_d.rearrange("(p a) f -> p (a f)", p=P)).then_inc(tab_in, 16)

        wp = 0

        def ring(n, dt=f32):
            nonlocal wp
            words = n // 2 if dt in (f16, bf16) else n
            wp += words
            a = work[:, wp - words:wp]
            return a if dt == f32 else a.bitcast(dt)

        HALVES = TILES // HU
        LOOPS = TILES // U
        stage = [ring(HU + 1, i32) for _ in range(2)]
        stage2 = [ring(HU + 1, i32) for _ in range(2)]
        rows = [ring(HU * D) for _ in range(2)]
        rows2 = [ring(HU * D) for _ in range(2)]
        parts = [ring(HU * 3 * D, bf16) for _ in range(2)]
        onehot = [ring(BW, bf16) for _ in range(2)]
        iota_w = iota16[:, 0:BW]
        hparts = [ring(HU * 3 * D, bf16) for _ in range(2)]
        mparts = parts
        ht_r = [ring(2 * P, bf16) for _ in range(2)]
        zb_r = [ring((BASIS + 1) * D) for _ in range(2)]
        pre_r = [ring(HU * D) for _ in range(2)]
        HT = [PS[:, 1024 + 512 * k:1024 + 512 * k + P].bitcast(bf16) for k in range(2)]
        VB = 5
        Z = [PS[:, 2048 + 1024 * k:2048 + 1024 * k + VB * D] for k in range(2)]
        ZA = [PS[:, 2560 + 1024 * k:2560 + 1024 * k + (BASIS - VB) * D] for k in range(2)]
        assert wp <= 19 * CE

        class Pass:
            def __init__(self, table, idx, key, side, k, plain, table2=None):
                self.table, self.idx, self.key, self.side, self.table2 = table, idx, key, side, table2
                self.t0, self.h0 = k * TILES, k * HALVES
                self.g0 = plain * LOOPS * 16 * HU
                self.s0 = plain * HALVES

        def sums(par):
            return PS[:, 512 * par:512 * par + BCOLS * D]

        def tile_sum(e, q, t, par, part3):
            e.wait_ge(onehot_ready, q.t0 + t + 1)
            wait_past(e, added, q.t0 + t - 1)
            for j in range(BCOLS):
                for k in range(3):
                    ins = nc.tensor.matmul(sums(par)[:, j * D:(j + 1) * D], onehot[par][:, j * P:(j + 1) * P],
                                           part3[:, k * D:(k + 1) * D], start=(k == 0), stop=(k == 2))
            ins.then_inc(sum_ready, 1)

        def make_onehot(e, q, t, par):
            wait_past(e, sum_ready, q.t0 + t - 1)
            nc.vector.tensor_scalar(onehot[par], iota_w, q.key[:, ds(t, 1)], None,
                                    ALU.is_equal).then_inc(onehot_ready, 1)

        def add_tile(e, q, t, par, where):
            e.wait_ge(sum_ready, q.t0 + t + 1)
            wait_past(e, added, q.t0 + t)
            a = acc[:, ds(where, BCOLS * D)]
            nc.vector.tensor_tensor(a, a, sums(par), ALU.add).then_inc(added, 1)

        def load_blocks(e, q, half, regs):
            e.load(regs, block_at[0:1, q.side, ds(half * 8, 8)])
            return [e.snap(r, min_val=0, max_val=(BLOCKS - 1) * BCOLS * D) for r in regs[0:HU]]

        def pass_gpsimd(e, q):
            def body(i):
                for h in range(2):
                    e.wait_ge(staged, q.h0 + 2 * i + h + 1)
                    if q.table2 is None:
                        wait_past(e, parts_ready, q.s0 + 2 * i + h - 1)
                    else:
                        wait_past(e, h_parts, 2 * i + h - 1)
                    e.sem_inc(issuing, 1)
                    for u in range(HU):
                        if q.table2 is not None:
                            e.indirect_dma_start(out=rows2[h][:, u * D:(u + 1) * D], out_offset=None, in_=q.table2,
                                                 in_offset=bass.IndirectOffsetOnAxis(
                                                     ap=stage2[h][:, u:u + 1], axis=0)).then_inc(got_ends[h], 16)
                        e.indirect_dma_start(out=rows[h][:, u * D:(u + 1) * D], out_offset=None, in_=q.table,
                                             in_offset=bass.IndirectOffsetOnAxis(
                                                 ap=stage[h][:, u:u + 1], axis=0)).then_inc(
                            got[h] if q.table2 is None else got_ends[h], 16)
            body(0)
            with e.Fori(1, LOOPS) as i:
                body(i)

        def pass_scalar(e, q):
            def stage_half(half, h):
                e.copy(stage[h][:, 0:HU], q.idx[:, ds(half * HU, HU)]).then_inc(staged, 1)

            def split(i, h, stages):
                half = 2 * i + h
                hi, mid, lo = (parts[h].rearrange("p (u k d) -> p u k d", k=3, d=D)[:, :, k, :] for k in range(3))
                r = rows[h].rearrange("p (u d) -> p u d", d=D)
                e.wait_ge(got[h], q.g0 + 16 * HU * (i + 1))
                wait_past(e, sum_ready, q.t0 + (half - 1) * HU)
                e.copy(hi, r).then_inc(part_hi, 1)
                if stages:
                    stage_half(half + 2, h)
                e.wait_ge(part_r1, q.s0 + half + 1)
                e.copy(mid, r).then_inc(part_mid, 1)
                e.wait_ge(part_r2, q.s0 + half + 1)
                e.copy(lo, r).then_inc(parts_ready, 1)

            stage_half(0, 0)
            stage_half(1, 1)
            split(0, 0, True)
            split(0, 1, True)
            with e.Fori(1, LOOPS - 1) as i:
                split(i, 0, True)
                split(i, 1, True)
            split(LOOPS - 1, 0, False)
            split(LOOPS - 1, 1, False)

        def pass_tensor(e, q):
            def half_sums(half, h):
                e.wait_ge(parts_ready, q.s0 + half + 1)
                for u in range(HU):
                    tile_sum(e, q, half * HU + u, (h + u) % 2, parts[h][:, u * 3 * D:(u + 1) * 3 * D])
            half_sums(0, 0)
            half_sums(1, 1)
            with e.Fori(1, LOOPS) as i:
                half_sums(2 * i, 0)
                half_sums(2 * i + 1, 1)

        def pass_vector(e, q, regs):
            def rest(half, h, k):
                got_part, signal = ((part_hi, part_r1), (part_mid, part_r2))[k]
                r = rows[h].rearrange("p (u d) -> p u d", d=D)
                part = parts[h].rearrange("p (u k d) -> p u k d", k=3, d=D)[:, :, k, :]
                e.wait_ge(got_part, q.s0 + half + 1)
                nc.vector.tensor_tensor(r, r, part, ALU.subtract).then_inc(signal, 1)

            def half_step(half, h, splits, last=False):
                at = load_blocks(e, q, half - 1, regs)
                for u in range(HU):
                    t, par = (half - 1) * HU + u, (h + 1 + u) % 2
                    if not (last and u == HU - 1):
                        make_onehot(e, q, t + 1, 1 - par)
                    add_tile(e, q, t, par, at[u])
                    if splits and u in (0, 2):
                        rest(half, h, u // 2)

            rest(0, 0, 0)
            rest(0, 0, 1)
            make_onehot(e, q, 0, 0)
            half_step(1, 1, True)
            with e.Fori(1, LOOPS) as i:
                half_step(2 * i, 0, True)
                half_step(2 * i + 1, 1, True)
            half_step(HALVES, 0, False, last=True)

        STEPS = HALVES + 3
        ENDS_AT = (1, 0, 2)

        def there(half):
            return not isinstance(half, int) or 0 <= half < HALVES

        def over_steps(e, step):
            for k in range(4):
                step(k, k % 2)
            with e.Fori(2, HALVES // 2 - 1) as i:
                step(2 * i, 0)
                step(2 * i + 1, 1)
            for k in range(HALVES - 2, STEPS):
                step(k, k % 2)

        def next_tile(k, h, u):
            t = (k - 1) * HU + u + 1
            if isinstance(t, int) and not 0 <= t < TILES:
                return None
            return (t, 1 - h, u + 1) if u + 1 < HU else (t, h, 0)

        def in_parts(a):
            return a.rearrange("p (u k d) -> p u k d", k=3, d=D)

        def in_tiles(a):
            return a.rearrange("p (u d) -> p u d", d=D)

        def edge_tensor(e, q):
            mm = nc.tensor.matmul

            def turn(t, par, slot, u):
                if isinstance(t, int) or u == 0:
                    e.wait_ge(h_parts, t // HU + 1 if isinstance(t, int) else q.half_now)
                wait_past(e, ht_ready, t - 1)
                for k in range(2):
                    at = u * 3 * D + k * D
                    ins = nc.tensor.transpose(HT[par][:, k * P:(k + 1) * P], hparts[slot][:, at:at + P], ident16[:, :])
                ins.then_inc(ht_mm, 1)

            def mix(t, par):
                e.wait_ge(ht_ready, t + 1)
                wait_past(e, z_used, t - 1)
                wait_past(e, za_used, t - 1)
                for out_, c in ((ZA[par], slice(VB * D, BASIS * D)), (Z[par], slice(0, VB * D))):
                    for k in range(3):
                        ins = mm(out_, ht_r[par][:, (k // 2) * P:(k // 2 + 1) * P], vmix[:, k, c],
                                 start=(k == 0), stop=(k == 2))
                ins.then_inc(z_mm, 1)

            def step(k, h):
                if there(k - 3):
                    e.wait_ge(m_parts, k - 2)
                for u in range(HU):
                    par = (h + 1 + u) % 2
                    nxt = next_tile(k, h, u)
                    if nxt and there(k if u + 1 == HU else k - 1):
                        q.half_now = k + 1
                        turn(nxt[0], 1 - par, nxt[1], nxt[2])
                    if there(k - 1):
                        mix((k - 1) * HU + u, par)
                    if there(k - 3):
                        tile_sum(e, q, (k - 3) * HU + u, par, mparts[1 - h][:, u * 3 * D:(u + 1) * 3 * D])
            over_steps(e, step)

        def edge_scalar(e, q):
            def stage_half(half, h):
                e.copy(stage2[h][:, 0:HU], own_s[:, ds(half * HU, HU)])
                e.copy(stage[h][:, 0:HU], q.idx[:, ds(half * HU, HU)]).then_inc(staged, 1)

            def turn_out(t, par):
                e.wait_ge(ht_mm, t + 1)
                wait_past(e, z_mm, t - 1)
                e.copy(ht_r[par], HT[par]).then_inc(ht_ready, 1)

            def weigh_rest(t, par):
                e.wait_ge(z_mm, t + 1)
                wait_past(e, pre_ready, t - 1)
                for b in range(VB, BASIS):
                    ins = e.activation(zb_r[par][:, b * D:(b + 1) * D], ZA[par][:, (b - VB) * D:(b - VB + 1) * D],
                                       ACT.Copy, scale=basis[:, ds(t, 1), b])
                ins.then_inc(za_used, 1)

            def ends_part(half, slot, k):
                ready, signal = ((h_sum, h_hi), (h_r1, h_mid), (h_r2, h_parts))[k]
                e.wait_ge(ready, half + 1)
                if k == 0:
                    wait_past(e, ht_mm, (half - 1) * HU)
                e.copy(in_parts(hparts[slot])[:, :, ENDS_AT[k], :], in_tiles(rows[slot])).then_inc(signal, 1)
                if k == 0 and there(half + 2) and not (isinstance(half, int) and half + 2 >= HALVES):
                    stage_half(half + 2, slot)

            def message_part(half, slot, k):
                ready, signal = ((None, m_hi), (m_r1, m_mid), (m_r2, m_parts))[k]
                part, pre = in_parts(mparts[slot])[:, :, k, :], in_tiles(pre_r[slot])
                if k == 0:
                    e.wait_ge(pre_ready, (half + 1) * HU)
                    wait_past(e, sum_ready, q.t0 + (half - 1) * HU)
                    e.activation(part, pre, ACT.Tanh).then_inc(m_high, 1)
                    e.wait_ge(m_high, half + 1)
                    e.activation(pre, pre, ACT.Tanh).then_inc(m_hi, 1)
                else:
                    e.wait_ge(ready, half + 1)
                    e.copy(part, pre).then_inc(signal, 1)

            def step(k, h):
                for u in range(HU):
                    nxt = next_tile(k, h, u)
                    if nxt and there(k if u + 1 == HU else k - 1):
                        turn_out(nxt[0], (h + u) % 2)
                    if there(k - 1):
                        weigh_rest((k - 1) * HU + u, (h + 1 + u) % 2)
                    if u in (0, 2, 4) and there(k - 2):
                        message_part(k - 2, h, u // 2)
                    if u in (1, 3, 5) and there(k):
                        ends_part(k, h, u // 2)
            stage_half(0, 0)
            stage_half(1, 1)
            over_steps(e, step)

        def edge_vector(e, q, regs):
            v = nc.vector
            for s in range(2):
                v.tensor_copy(zb_r[s][:, BASIS * D:], b_ii)

            def weigh(t, par, slot, u, half):
                e.wait_ge(z_mm, t + 1)
                v.tensor_tensor(zb_r[par][:, 0:VB * D].rearrange("p (b c) -> p b c", b=VB),
                                Z[par].rearrange("p (b c) -> p b c", b=VB),
                                basis[:, ds(t, 1), 0:VB].rearrange("p o b -> p (o b)").unsqueeze(2).to_broadcast([P, VB, D]),
                                ALU.mult).then_inc(z_used, 1)
                e.wait_ge(z_used, t + 1)
                e.wait_ge(za_used, t + 1)
                if u == 0:
                    wait_past(e, m_parts, half - 1)
                v.tensor_reduce(pre_r[slot][:, u * D:(u + 1) * D], zb_r[par].rearrange("p (b c) -> p c b", c=D),
                                AX.X, ALU.add).then_inc(pre_ready, 1)

            def ends(half, slot, i):
                e.wait_ge(got_ends[slot], 16 * 2 * HU * (i + 1))
                v.tensor_tensor(rows[slot], rows[slot], rows2[slot], ALU.add).then_inc(h_sum, 1)

            def rest(half, a, three, k, ready, signal):
                e.wait_ge(ready, half + 1)
                v.tensor_tensor(in_tiles(a), in_tiles(a), in_parts(three)[:, :, k, :], ALU.subtract).then_inc(signal, 1)

            def step(k, h):
                i = k // 2 if isinstance(k, int) else q.i
                at = load_blocks(e, q, k - 3, regs) if there(k - 3) else None
                for u in range(HU):
                    par, t = (h + 1 + u) % 2, (k - 3) * HU + u
                    if there(k - 1):
                        weigh((k - 1) * HU + u, par, 1 - h, u, k - 1)
                    if there(k - 3):
                        if u + 1 < HU or there(k - 2) and not (isinstance(k, int) and k - 2 >= HALVES):
                            make_onehot(e, q, t + 1, 1 - par)
                        add_tile(e, q, t, par, at[u])
                    elif k == 2 and u == HU - 1:
                        make_onehot(e, q, 0, 0)
                    if there(k) and not (isinstance(k, int) and k >= HALVES):
                        if u == 0:
                            ends(k, h, i)
                        if u == 2:
                            rest(k, rows[h], hparts[h], ENDS_AT[0], h_hi, h_r1)
                        if u == 4:
                            rest(k, rows[h], hparts[h], ENDS_AT[1], h_mid, h_r2)
                    if there(k - 2):
                        if u == 1:
                            rest(k - 2, pre_r[h], mparts[h], 0, m_hi, m_r1)
                        if u == 3:
                            rest(k - 2, pre_r[h], mparts[h], 1, m_mid, m_r2)

            for k in range(4):
                step(k, k % 2)
            with e.Fori(2, HALVES // 2 - 1) as i:
                q.i = i
                step(2 * i, 0)
                step(2 * i + 1, 1)
            for k in range(HALVES - 2, STEPS):
                step(k, k % 2)

        def chunk_of(a, n):
            return a[:, ds(n * CE, CE)]

        def buf(k):
            return work[:, k * CE:(k + 1) * CE]

        def two(k):
            return [buf(k), buf(k + 1)]

        def c3(a):
            return a.rearrange("p (c d) -> p c d", d=D)

        def per_node(a, n):
            return a[:, ds(n * CC, CC)].unsqueeze(2).to_broadcast([P, CC, D])

        def feat(a):
            return a.unsqueeze(1).to_broadcast([P, CC, D])

        A0, A1, B0 = two(0), two(2), two(4)
        O1, O2, O3 = two(6), two(8), two(10)
        XIN, XT = two(12), two(14)
        CEN, SQ, TMP = buf(16), buf(17), buf(18)
        P1T = two(2)
        TURNED = PS[:, 0:CE]
        MULT = [[PS[:, 1024 * (h + 1) + 512 * k:1024 * (h + 1) + 512 * k + CE] for k in range(2)] for h in range(2)]
        PP = PS[:, 512:512 + CE]
        mean, var, rstd, root = (st[:, k, :] for k in range(4))

        class Phase:
            def __init__(self, k, in1, in2, out1, out2, norm, uses_acc):
                self.k, self.in1, self.in2, self.out1, self.out2 = k, in1, in2, out1, out2
                self.norm, self.uses_acc = norm, uses_acc
                self.prods = bool(out2)

        counted = {"chunks": 0, "norm": 0, "acc": 0, "prods": 0}
        moved = {name: [0, 0] for name in ("in1", "in2", "out1", "out2")}

        def plan(ph):
            ph.c0, ph.ln0, ph.acc0, ph.m0 = counted.values()
            for name, times in zip(counted, (1, ph.norm, ph.uses_acc, ph.prods)):
                counted[name] += CHUNKS * times
            ph.l1, ph.l2, ph.s1, ph.s2 = (list(at) for at in moved.values())
            for at, arrays in zip(moved.values(), (ph.in1, ph.in2, ph.out1, ph.out2)):
                for h in range(2):
                    at[h] += 16 * len(arrays) * ((CHUNKS + 1 - h) // 2)
            return ph

        def exists(n):
            return not isinstance(n, int) or 0 <= n < CHUNKS

        def over_chunks(e, step):
            for n in range(-3, 2):
                step(n, n % 2, n // 2)
            with e.Fori(0, (CHUNKS - 5) // 4) as i:
                for u in range(4):
                    step(4 * i + 2 + u, u % 2, 2 * i + 1 + u // 2)
            for n in range(CHUNKS // 2 * 2 - 2, CHUNKS):
                step(n, n % 2, n // 2)

        def dense_sync(e, ph):
            def load1(n, h, j):
                wait_past(e, v1_done, ph.c0 + n - 1 if not (isinstance(n, int) and n < 2) else 0)
                for a, t in zip((A0, A1), ph.in1):
                    e.dma_start(a[h], chunk_of(per_partition(t), n)).then_inc(in1_loaded[h], 16)

            def load2(n, h, j):
                wait_past(e, v2_done, ph.m0 + n - 1 if not (isinstance(n, int) and n < 2) else 0)
                for a, t in zip((B0,), ph.in2):
                    e.dma_start(a[h], chunk_of(per_partition(t), n)).then_inc(in2_loaded[h], 16)

            def store1(n, h):
                e.wait_ge(v1_done, ph.c0 + n + 1)
                for a, t in zip((O1, O2), ph.out1):
                    e.dma_start(chunk_of(per_partition(t), n), a[h]).then_inc(stored1[h], 16)

            def store2(n, h):
                e.wait_ge(v2_done, ph.m0 + n + 1)
                e.wait_ge(e_done, ph.m0 + n + 1)
                for a, t in zip((O2, O3), ph.out2):
                    e.dma_start(chunk_of(per_partition(t), n), a[h]).then_inc(stored2[h], 16)

            def step(n, h, j):
                if exists(n + 3):
                    load1(n + 3, 1 - h, j)
                if exists(n + 2) and ph.out1:
                    store1(n + 2, h)
                if exists(n + 1) and ph.in2:
                    load2(n + 1, 1 - h, j)
                if exists(n) and ph.out2:
                    store2(n, h)
            over_chunks(e, step)
            for h in range(2):
                n = (CHUNKS + 1 - h) // 2
                if ph.out1:
                    e.wait_ge(stored1[h], ph.s1[h] + 16 * len(ph.out1) * n)
                if ph.out2:
                    e.wait_ge(stored2[h], ph.s2[h] + 16 * len(ph.out2) * n)

        def dense_gpsimd(e, ph):
            if not ph.uses_acc or ph.k == LAST:
                return

            def step(n, h, j):
                if exists(n):
                    e.wait_ge(acc_used, ph.acc0 + n + 1)
                    e.tensor_copy(chunk_of(acc, n), zero.to_broadcast([P, CE])).then_inc(cleared, 1)
            over_chunks(e, step)

        def dense_vector(e, ph, v1, v2, beside=None):
            v = nc.vector
            per_chunk = []

            def run_v1(n, h, meanwhile):
                count = [0]
                before = link_base[0] + (per_chunk[0] * n if per_chunk else 0)

                def link(ins):
                    count[0] += 1
                    ins.then_inc(v1_step, 1)
                    e.wait_ge(v1_step, before + count[0])
                v1(e, ph, v, n, h, link, meanwhile)
                per_chunk.append(count[0])
                assert len(set(per_chunk)) == 1

            fill_wait = ph.norm

            def step(n, h, j):
                def outputs():
                    if exists(n) and ph.prods:
                        if ph.in2:
                            e.wait_ge(in2_loaded[h], ph.l2[h] + 16 * len(ph.in2) * (j + 1))
                        wait_past(e, stored2[h], ph.s2[h] + 16 * len(ph.out2) * j)
                        e.wait_ge(multiplied, ph.m0 + n + 1)
                        v2(e, ph, v, n, h)
                if exists(n + 2):
                    if beside:
                        beside(n + 2)
                    j1 = j + 1
                    e.wait_ge(in1_loaded[h], ph.l1[h] + 16 * len(ph.in1) * (j1 + 1))
                    if ph.out1:
                        wait_past(e, stored1[h], ph.s1[h] + 16 * len(ph.out1) * j1)
                    if ph.prods:
                        wait_past(e, turned, ph.m0 + n + 1)
                    run_v1(n + 2, h, outputs if fill_wait else lambda: None)
                    if not fill_wait:
                        outputs()
                else:
                    outputs()
            over_chunks(e, step)
            link_base[0] += per_chunk[0] * CHUNKS

        link_base = [0]

        def bc(a):
            return a.unsqueeze(2).to_broadcast([P, CC, D])

        def normalise(e, ph, v, n, link, src, dst, meanwhile):
            link(v.tensor_reduce(mean, c3(src), AX.X, ALU.add))
            v.scalar_tensor_tensor(c3(CEN), c3(src), float(D), bc(mean), ALU.mult, ALU.subtract).then_inc(centered, 1)
            meanwhile()
            e.wait_ge(squared, ph.ln0 + n + 1)
            v.tensor_reduce(var, c3(SQ), AX.X, ALU.add).then_inc(var_ready, 1)
            e.wait_ge(root_ready, ph.ln0 + n + 1)
            link(v.reciprocal(rstd, root))
            return v.scalar_tensor_tensor(c3(dst), c3(CEN), 0.0, bc(rstd), ALU.max, ALU.mult)

        def finish(e, ph, n):
            if ph.prods:
                e.wait_ge(x_ready, ph.m0 + n + 1)
            e.sem_inc(v1_done, 1)

        def p0_v1(e, ph, v, n, h, link, meanwhile):
            x = A0[h]
            link(normalise(e, ph, v, n, link, x, TMP, meanwhile))
            link(v.tensor_tensor(c3(O1[h]), c3(TMP), per_node(dinv, n), ALU.mult))
            link(v.scalar_tensor_tensor(O2[h], TMP, 1.0 / 3.0, x, ALU.mult, ALU.add))
            finish(e, ph, n)

        def p1_v1(e, ph, v, n, h, link, meanwhile):
            v.tensor_tensor(c3(TMP), c3(chunk_of(acc, n)), per_node(dinv, n), ALU.mult).then_inc(acc_used, 1)
            e.wait_ge(acc_used, ph.acc0 + n + 1)
            link(v.tensor_tensor(c3(O1[h]), c3(TMP), per_node(dinv, n), ALU.mult))
            link(v.scalar_tensor_tensor(O2[h], TMP, 1.0 / 3.0, A0[h], ALU.mult, ALU.add))
            finish(e, ph, n)

        def p2_v1(e, ph, v, n, h, link, meanwhile):
            v.tensor_tensor(c3(TMP), c3(chunk_of(acc, n)), per_node(dinv, n), ALU.mult).then_inc(acc_used, 1)
            e.wait_ge(acc_used, ph.acc0 + n + 1)
            link(v.scalar_tensor_tensor(TMP, TMP, 1.0 / 3.0, A0[h], ALU.mult, ALU.add))
            normalise(e, ph, v, n, link, TMP, XIN[h], meanwhile).then_inc(x_ready, 1)
            e.wait_ge(x_ready, ph.m0 + n + 1)
            link(v.tensor_tensor(O1[h], TMP, XIN[h], ALU.add))
            finish(e, ph, n)

        def p2_v2(e, ph, v, n, h):
            v.tensor_tensor(c3(O2[h]), c3(MULT[h][0]), feat(b_pi1), ALU.add).then_inc(v2_done, 1)

        def p3_v1(e, ph, v, n, h, link, meanwhile):
            v.tensor_tensor(O1[h], chunk_of(acc, n), A0[h], ALU.add).then_inc(acc_used, 1)
            e.wait_ge(acc_used, ph.acc0 + n + 1)
            normalise(e, ph, v, n, link, O1[h], XIN[h], meanwhile).then_inc(x_ready, 1)
            finish(e, ph, n)

        def p3_v2(e, ph, v, n, h):
            v.tensor_copy(O2[h], MULT[h][0]).then_inc(v2_done, 1)

        def p4_v1(e, ph, v, n, h, link, meanwhile):
            v.scalar_tensor_tensor(TMP, A0[h], ep0, chunk_of(acc, n), ALU.mult, ALU.add).then_inc(acc_used, 1)
            e.wait_ge(acc_used, ph.acc0 + n + 1)
            v.tensor_scalar(XIN[h], TMP, 0.0, None, ALU.max).then_inc(x_ready, 1)
            finish(e, ph, n)

        def p4_v2(e, ph, v, n, h):
            v.scalar_tensor_tensor(O3[h], MULT[h][1], 0.5, B0[h], ALU.mult, ALU.add).then_inc(v2_done, 1)

        def p5_v1(e, ph, v, n, h, link, meanwhile):
            v.scalar_tensor_tensor(TMP, A0[h], ep1, chunk_of(acc, n), ALU.mult, ALU.add).then_inc(acc_used, 1)
            e.wait_ge(acc_used, ph.acc0 + n + 1)
            link(v.tensor_scalar(TMP, TMP, 0.0, 0.5, ALU.max, ALU.mult))
            link(v.tensor_tensor(O1[h], TMP, A1[h], ALU.add))
            normalise(e, ph, v, n, link, O1[h], XIN[h], meanwhile).then_inc(x_ready, 1)
            finish(e, ph, n)

        def p5_v2(e, ph, v, n, h):
            v.tensor_tensor(c3(O3[h]), c3(MULT[h][1]), feat(b_s1), ALU.add).then_inc(v2_done, 1)

        def p6_v1(e, ph, v, n, h, link, meanwhile):
            v.tensor_tensor(c3(TMP), c3(chunk_of(acc, n)), per_node(rdeg, n), ALU.mult).then_inc(acc_used, 1)
            e.wait_ge(acc_used, ph.acc0 + n + 1)
            link(v.tensor_tensor(TMP, TMP, A0[h], ALU.add))
            v.tensor_scalar(XIN[h], TMP, 0.0, None, ALU.max).then_inc(x_ready, 1)
            finish(e, ph, n)

        def p6_v2(e, ph, v, n, h):
            v.tensor_tensor(O3[h], MULT[h][1], B0[h], ALU.add).then_inc(v2_done, 1)

        def p7_v1(e, ph, v, n, h, link, meanwhile):
            v.tensor_tensor(c3(TMP), c3(chunk_of(acc, n)), per_node(rdeg, n), ALU.mult).then_inc(acc_used, 1)
            e.wait_ge(acc_used, ph.acc0 + n + 1)
            link(v.tensor_tensor(TMP, TMP, A0[h], ALU.add))
            link(v.tensor_tensor(c3(O1[h]), c3(TMP), feat(b_s2), ALU.add))
            finish(e, ph, n)

        def dense_tensor(e, ph, weights_of):
            mm = nc.tensor.matmul

            def turn(n, h):
                e.wait_ge(x_ready, ph.m0 + n + 1)
                wait_past(e, turned_sb, ph.m0 + n)
                for g in range(PAIRS):
                    ins = nc.tensor.transpose(TURNED[:, g * P:(g + 1) * P], XIN[h][:, g * P:(g + 1) * P], ident)
                ins.then_inc(turned, 1)

            def multiply(n, h, src, w):
                wait_past(e, v2_done, ph.m0 + n - 1)
                wait_past(e, e_done, ph.m0 + n - 1)
                for g in range(PAIRS):
                    for k, name in enumerate(w):
                        ins = mm(MULT[h][k][:, g * P:(g + 1) * P], src[:, g * P:(g + 1) * P], W[name],
                                 start=True, stop=True)
                ins.then_inc(multiplied, 1)

            def step(n, h, j):
                if ph.k == 2:
                    if exists(n):
                        e.wait_ge(turned_sb, ph.m0 + n + 1)
                        wait_past(e, p1_ready, n)
                        mm(PP, W["pp"], XT[h], start=True, stop=True).then_inc(pp_done, 1)
                    if exists(n + 1):
                        turn(n + 1, 1 - h)
                    if exists(n):
                        e.wait_ge(p1_ready, n + 1)
                        multiply(n, h, P1T[h], weights_of)
                    return
                if exists(n + 1):
                    turn(n + 1, 1 - h)
                if exists(n):
                    e.wait_ge(turned_sb, ph.m0 + n + 1)
                    multiply(n, h, XT[h], weights_of)
            over_chunks(e, step)

        def dense_scalar(e, ph, evacuate, beside=None):
            def norm_part(n):
                e.wait_ge(centered, ph.ln0 + n + 1)
                e.activation(SQ, CEN, ACT.Square).then_inc(squared, 1)
                e.wait_ge(var_ready, ph.ln0 + n + 1)
                e.activation(root, var, ACT.Sqrt, scale=1.0 / D, bias=eps_sb).then_inc(root_ready, 1)

            def copy_turned(n, h):
                e.wait_ge(turned, ph.m0 + n + 1)
                wait_past(e, pp_done if ph.k == 2 else multiplied, (0 if ph.k == 2 else ph.m0) + n - 1)
                e.copy(XT[h], TURNED).then_inc(turned_sb, 1)

            def step(n, h, j):
                if ph.k == 2 and exists(n):
                    e.wait_ge(pp_done, n + 1)
                    wait_past(e, multiplied, ph.m0 + n - 1)
                    e.activation(P1T[h], PP, ACT.Tanh, bias=b_pp).then_inc(p1_ready, 1)
                if exists(n + 1) and ph.prods:
                    copy_turned(n + 1, 1 - h)
                if exists(n + 2) and ph.norm:
                    if beside:
                        beside(n + 2)
                    norm_part(n + 2)
                if exists(n) and ph.prods:
                    e.wait_ge(multiplied, ph.m0 + n + 1)
                    wait_past(e, stored2[h], ph.s2[h] + 16 * len(ph.out2) * j)
                    evacuate(e, n, h)
            if ph.prods or ph.norm:
                over_chunks(e, step)

        def evac(which, out_bufs):
            def run(e, n, h):
                e.copy(out_bufs[h], MULT[h][which]).then_inc(e_done, 1)
            return run

        def evac_none(e, n, h):
            e.sem_inc(e_done, 1)

        phases = [
            plan(Phase(0, [x_in], [], [t_g0, r_0], [], True, False)),
            plan(Phase(1, [r_0], [], [t_g1, r_1], [], False, True)),
            plan(Phase(2, [r_1], [], [r_2], [t_a, t_c], True, True)),
            plan(Phase(3, [r_2], [], [r_3], [t_y0], True, True)),
            plan(Phase(4, [t_y0], [r_3], [], [t_y1, r_4], False, True)),
            plan(Phase(5, [t_y1, r_4], [], [r_5], [t_s1, r_s1], True, True)),
            plan(Phase(6, [r_s1], [r_5], [], [t_s2, r_6], False, True)),
            plan(Phase(7, [r_6], [], [out], [], False, True)),
        ]
        LAST = len(phases) - 1
        vector_parts = [(p0_v1, None), (p1_v1, None), (p2_v1, p2_v2), (p3_v1, p3_v2), (p4_v1, p4_v2),
                        (p5_v1, p5_v2), (p6_v1, p6_v2), (p7_v1, None)]
        evacs = [None, None, evac(1, O3), evac_none, evac(0, O2), evac(0, O2), evac(0, O2), None]
        products = [None, None, ("w1a", "w1b"), ("g0",), ("g1", "gm"), ("s1a", "s1x"), ("s2a", "s2x"), None]

        S, DD = (idx_s, key_s, 0), (idx_d, key_d, 1)
        passes = {
            0: [Pass(t_g0, *S, 0, 0), Pass(t_g0, *DD, 1, 1)],
            1: [Pass(t_g1, *S, 2, 2), Pass(t_g1, *DD, 3, 3)],
            2: [Pass(t_c, *S, 4, 4, t_a)],
            3: [Pass(t_y0, *DD, 5, 4)],
            4: [Pass(t_y1, *DD, 6, 5)],
            5: [Pass(t_s1, *S, 7, 6)],
            6: [Pass(t_s2, *S, 8, 7)],
            7: [],
        }

        @block.sync
        def _(e):
            prep_sync(e)
            dense_sync(e, phases[0])
            prep_sync_end(e)
            end_phase(e, "sync")
            for k, ph in enumerate(phases):
                if k:
                    dense_sync(e, ph)
                    end_phase(e, "sync")
                end_phase(e, "sync")

        @block.gpsimd
        def _(e):
            prep_gpsimd(e)
            end_phase(e, "pool")
            for k, ph in enumerate(phases):
                if k:
                    dense_gpsimd(e, ph)
                    end_phase(e, "pool")
                for q in passes[k]:
                    pass_gpsimd(e, q)
                end_phase(e, "pool")

        @block.scalar
        def _(e):
            prep_scalar(e)
            end_phase(e, "act")
            for k, ph in enumerate(phases):
                if k:
                    dense_scalar(e, ph, evacs[k])
                    end_phase(e, "act")
                for q in passes[k]:
                    (edge_scalar if q.table2 is not None else pass_scalar)(e, q)
                end_phase(e, "act")

        @block.tensor
        def _(e):
            prep_tensor(e)
            end_phase(e, "pe")
            for k, ph in enumerate(phases):
                if k:
                    if ph.prods:
                        dense_tensor(e, ph, products[k])
                    end_phase(e, "pe")
                for q in passes[k]:
                    (edge_tensor if q.table2 is not None else pass_tensor)(e, q)
                end_phase(e, "pe")

        @block.vector
        def _(e):
            regs = [e.alloc_register(f"block_at_{u}") for u in range(8)]
            prep_vector(e)
            end_phase(e, "dve")
            for k, ph in enumerate(phases):
                if k:
                    dense_vector(e, ph, *vector_parts[k])
                    end_phase(e, "dve")
                for q in passes[k]:
                    (edge_vector if q.table2 is not None else pass_vector)(e, q, regs)
                end_phase(e, "dve")


def kernel(**inputs):
    import numpy as np
    import concourse.bacc as bacc
    from concourse.bass_utils import run_bass_kernel_spmd

    a = {k: np.asarray(v) for k, v in inputs.items()}
    f = np.float32

    def pair(w):
        o = np.zeros((P, P), f)
        o[0:D, 0:D] = w
        o[D:, D:] = w
        return o

    def rows(v):
        return np.tile(v[None, :], (P, 1))

    x = np.zeros((NPAD, D), f)
    x[:NODES] = a["x"]

    def edge_list(v):
        o = np.full(EPAD, NPAD - 1, np.int32)
        o[:EDGES] = v
        return o.reshape(P, ETILES)

    attr = np.zeros((EPAD, BASIS), f)
    attr[:EDGES] = a["edge_attr_8"]
    k, m = np.meshgrid(np.arange(P), np.arange(P), indexing="ij")
    consts32 = np.zeros((P, CONST_COLS), f)
    consts32[:, 0:P] = k == m
    consts32[:BLOCKS, P:P + BLOCKS] = (k <= m)[:BLOCKS, :BLOCKS]
    consts32[:BLOCKS, P + BLOCKS:] = (k < m)[:BLOCKS, :BLOCKS]
    consts16 = np.concatenate([np.tile(np.arange(512), (P, 1)), k < m, np.ones((P, P))], 1).astype(np.float16)
    w1, s1, s2 = a["L1_gnn_pi_W1"], a["L3_gnn_W1"], a["L3_gnn_W2"]
    blocks = {"pp": a["L1_gnn_pp_W"], "w1a": w1[:D], "w1b": w1[D:], "g0": a["L2_gnn_W0"].T,
              "gm": a["L2_gnn_Wm"].T, "g1": a["L2_gnn_W1"].T, "s1x": s1[:D], "s1a": s1[D:],
              "s2x": s2[:D], "s2a": s2[D:]}
    vectors = np.concatenate(
        [rows(a["L1_gnn_pi_b1"]), rows(a["L1_gnn_ii_b"]), rows(a["L3_gnn_b1"]), rows(a["L3_gnn_b2"]),
         np.tile(a["L1_gnn_pp_b"], 2)[:, None], np.tile(a["L2_gnn_eps0"].reshape(1, 1), (P, 1)),
         np.tile(a["L2_gnn_eps1"].reshape(1, 1), (P, 1)), np.zeros((P, 1), f)], 1)
    arrays = {
        "x": x, "src": edge_list(a["src"]), "dst": edge_list(a["dst"]),
        "attr": attr.reshape(P, ETILES * BASIS), "consts32": consts32, "consts16": consts16,
        "weights": np.concatenate([pair(blocks[n]) for n in W_NAMES], 1),
        "w2t": np.tile(a["L1_gnn_pi_W2"].reshape(D, D, BASIS).transpose(1, 2, 0)[:, :, None, :],
                       (1, 1, 2, 1)).reshape(D, BASIS * P),
        "iiw": a["L1_gnn_ii_W"], "vectors": vectors,
    }
    nc = bacc.Bacc("TRN2", target_bir_lowering=False, num_devices=1)
    arrays = {f"in_{n}": np.ascontiguousarray(v) for n, v in arrays.items()}
    args = [nc.dram_tensor(n, v.shape, mybir.dt.from_np(v.dtype), kind="ExternalInput").ap()
            for n, v in arrays.items()]
    args.append(nc.dram_tensor("out", (NPAD, D), mybir.dt.float32, kind="ExternalOutput").ap())
    build_program(nc, *args)
    r = run_bass_kernel_spmd(nc, [arrays], core_ids=[0])
    return r.results[0]["out"][:NODES]
```
